# Optimizing a Trainium2 kernel written in Bass

```python
import numpy as np
import jax
import jax.numpy as jnp

def _softmax(x, axis=-1):
    return jax.nn.softmax(x, axis=axis)

def _gelu(x):
    return jax.nn.gelu(x, approximate=True)

def _silu(x):
    return jax.nn.silu(x)

def _sigmoid(x):
    return jax.nn.sigmoid(x)

def _layernorm(x, axis=-1, eps=1e-05):
    m = jnp.mean(x, axis=axis, keepdims=True)
    v = jnp.var(x, axis=axis, keepdims=True)
    return (x - m) / jnp.sqrt(v + eps)

def _scatter_add(tgt, idx, src, axis=0):
    return tgt.at[idx].add(src)

def _segment_sum(src, seg, n):
    return jax.ops.segment_sum(src, seg, n)
kernel_name = 'mk_audio_tower_d1_tok_audfeat512_r4_8d91f5'

def setup_inputs(seed: int=0):
    np.random.seed(seed)
    _w = jnp.asarray

    def _rec_inputs():
        import jax
        import jax.numpy as jnp
        _rk = jax.random.key(seed)
        x = -0.000356955 + 1 * jax.random.normal(jax.random.fold_in(_rk, 1), (64, 196, 96), jnp.float32)
        return x
    x = _rec_inputs()

    def _L0_tok_setup():
        import jax, jax.numpy as jnp
        import numpy as np
        import itertools
        B, RES, RES_, STRIDE = (64, 14, 7, 2)
        N, N_ = (RES * RES, RES_ * RES_)
        IN_DIM, OUT_DIM = (96, 128)
        H, KD, AR = (12, 32, 2)
        D = AR * KD
        DH = D * H
        NH_KD = KD * H
        KV_H = DH + NH_KD
        EPS = 1e-05

        def _bias_idxs():
            points = list(itertools.product(range(RES), range(RES)))
            points_ = list(itertools.product(range(RES_), range(RES_)))
            offsets, idxs = ({}, [])
            for p1 in points_:
                for p2 in points:
                    off = (abs(p1[0] * STRIDE - p2[0]), abs(p1[1] * STRIDE - p2[1]))
                    if off not in offsets:
                        offsets[off] = len(offsets)
                    idxs.append(offsets[off])
            return (np.array(idxs, dtype=np.int32).reshape(N_, N), len(offsets))

        def linear_bn(x, w, gamma, beta, mean, var):
            s = gamma / jnp.sqrt(var + EPS)
            return jnp.matmul(x, w.T) * s + (beta - mean * s)
        key = jax.random.key(seed)
        ks = jax.random.split(key, 12)
        idxs_np, n_off = _bias_idxs()

        def bn_params(k, dim):
            k1, k2, k3, k4 = jax.random.split(k, 4)
            return (jax.random.normal(k1, (dim,)) * 0.1 + 1.0, jax.random.normal(k2, (dim,)) * 0.1, jax.random.normal(k3, (dim,)) * 0.1, jax.random.uniform(k4, (dim,), minval=0.5, maxval=1.5))
        kv_g, kv_b, kv_m, kv_v = bn_params(ks[1], KV_H)
        q_g, q_b, q_m, q_v = bn_params(ks[3], NH_KD)
        pr_g, pr_b, pr_m, pr_v = bn_params(ks[5], OUT_DIM)
        return {'x': jax.random.normal(ks[0], (B, N, IN_DIM), dtype=jnp.float32), 'kv_w': jax.random.normal(ks[6], (KV_H, IN_DIM), dtype=jnp.float32) * IN_DIM ** (-0.5), 'kv_g': kv_g, 'kv_b': kv_b, 'kv_m': kv_m, 'kv_v': kv_v, 'q_w': jax.random.normal(ks[7], (NH_KD, IN_DIM), dtype=jnp.float32) * IN_DIM ** (-0.5), 'q_g': q_g, 'q_b': q_b, 'q_m': q_m, 'q_v': q_v, 'proj_w': jax.random.normal(ks[8], (OUT_DIM, DH), dtype=jnp.float32) * DH ** (-0.5), 'proj_g': pr_g, 'proj_b': pr_b, 'proj_m': pr_m, 'proj_v': pr_v, 'attention_biases': jax.random.normal(ks[9], (H, n_off), dtype=jnp.float32) * 0.02, 'bias_idxs': jnp.asarray(idxs_np)}
    _L0_tok_all = _L0_tok_setup()
    _L0_tok_in = {k: v for k, v in _L0_tok_all.items() if k in ('kv_w', 'kv_g', 'kv_b', 'kv_m', 'kv_v', 'q_w', 'q_g', 'q_b', 'q_m', 'q_v', 'proj_w', 'proj_g', 'proj_b', 'proj_m', 'proj_v', 'attention_biases', 'bias_idxs')}
    del _L0_tok_all

    def _L0_attn_setup():
        import jax, jax.numpy as jnp
        import numpy as np
        SIZE = 128
        NUM_HEADS = 8
        HEAD_SIZE = SIZE // NUM_HEADS
        EPS = 1e-05

        def _retention(x, W_Q, W_K, W_V):
            B, T, D = x.shape
            H, dh = (NUM_HEADS, HEAD_SIZE)
            q = (x @ W_Q).reshape(B, T, H, dh).transpose(0, 2, 1, 3)
            k = (x @ W_K).reshape(B, T, H, dh).transpose(0, 2, 1, 3)
            v = (x @ W_V).reshape(B, T, H, dh).transpose(0, 2, 1, 3)
            gammas = 1.0 - jnp.exp2(-5.0 - jnp.arange(H, dtype=jnp.float32))
            idx = jnp.arange(T)
            diff = (idx[:, None] - idx[None, :]).astype(jnp.float32)
            causal = diff >= 0
            decay = jnp.where(causal[None], jnp.exp(diff[None] * jnp.log(gammas)[:, None, None]), 0.0)
            scores = jnp.einsum('bhtd,bhsd->bhts', q, k) / jnp.sqrt(jnp.float32(dh))
            out = jnp.einsum('bhts,bhsd->bhtd', scores * decay[None], v)
            return out.transpose(0, 2, 1, 3).reshape(B, T, D)

        def _group_norm(y, weight, bias):
            B, T, D = y.shape
            g = y.reshape(B * T, NUM_HEADS, HEAD_SIZE)
            mean = jnp.mean(g, axis=-1, keepdims=True)
            var = jnp.var(g, axis=-1, keepdims=True)
            g = (g - mean) / jnp.sqrt(var + EPS)
            g = g.reshape(B * T, D) * weight + bias
            return g.reshape(B, T, D)
        key = jax.random.key(seed)
        ks = jax.random.split(key, 8)
        B, T, D = (2, 512, SIZE)
        mk = lambda k: jax.random.normal(k, (D, D), dtype=jnp.float32) / D
        return {'x': jax.random.normal(ks[0], (B, T, D), dtype=jnp.float32), 'W_Q': mk(ks[1]), 'W_K': mk(ks[2]), 'W_V': mk(ks[3]), 'W_G': mk(ks[4]), 'W_O': mk(ks[5]), 'gn_weight': jnp.ones((D,), dtype=jnp.float32), 'gn_bias': jnp.zeros((D,), dtype=jnp.float32)}
    _L0_attn_all = _L0_attn_setup()
    _L0_attn_in = {k: v for k, v in _L0_attn_all.items() if k in ('W_Q', 'W_K', 'W_V', 'W_G', 'W_O', 'gn_weight', 'gn_bias')}
    del _L0_attn_all

    def _L0_ffn_setup():
        import jax, jax.numpy as jnp
        import numpy as np
        D, H, E, B, S = (128, 512, 16, 8, 2048)
        MAX_GROUP_SIZE = 1024
        MIN_CAPACITY = 8
        CAPACITY_FACTOR = 1.0

        def _group_dims(num_tokens, num_experts):
            num_groups = -(-num_tokens // MAX_GROUP_SIZE)
            while num_tokens % num_groups != 0 or num_groups % num_experts != 0:
                num_groups += 1
            return (num_tokens // num_groups, num_groups)
        key = jax.random.key(seed)
        ks = jax.random.split(key, 6)
        s = 0.02
        return {'x': jax.random.normal(ks[0], (B, S, D), jnp.float32), 'gate_w': jax.random.normal(ks[1], (D, E), jnp.float32) * s, 'w1': jax.random.normal(ks[2], (E, D, H), jnp.float32) * s, 'b1': jnp.zeros((E, H), jnp.float32), 'w2': jax.random.normal(ks[3], (E, H, D), jnp.float32) * s, 'b2': jnp.zeros((E, D), jnp.float32), 'sw1': jax.random.normal(ks[4], (D, H), jnp.float32) * s, 'sb1': jnp.zeros((H,), jnp.float32), 'sw2': jax.random.normal(ks[5], (H, D), jnp.float32) * s, 'sb2': jnp.zeros((D,), jnp.float32)}
    _L0_ffn_all = _L0_ffn_setup()
    _L0_ffn_in = {k: v for k, v in _L0_ffn_all.items() if k in ('gate_w', 'w1', 'b1', 'w2', 'b2', 'sw1', 'sb1', 'sw2', 'sb2')}
    del _L0_ffn_all
    return {'x': x, 'L0_tok_kv_w': _L0_tok_in['kv_w'], 'L0_tok_kv_g': _L0_tok_in['kv_g'], 'L0_tok_kv_b': _L0_tok_in['kv_b'], 'L0_tok_kv_m': _L0_tok_in['kv_m'], 'L0_tok_kv_v': _L0_tok_in['kv_v'], 'L0_tok_q_w': _L0_tok_in['q_w'], 'L0_tok_q_g': _L0_tok_in['q_g'], 'L0_tok_q_b': _L0_tok_in['q_b'], 'L0_tok_q_m': _L0_tok_in['q_m'], 'L0_tok_q_v': _L0_tok_in['q_v'], 'L0_tok_proj_w': _L0_tok_in['proj_w'], 'L0_tok_proj_g': _L0_tok_in['proj_g'], 'L0_tok_proj_b': _L0_tok_in['proj_b'], 'L0_tok_proj_m': _L0_tok_in['proj_m'], 'L0_tok_proj_v': _L0_tok_in['proj_v'], 'L0_tok_attention_biases': _L0_tok_in['attention_biases'], 'L0_tok_bias_idxs': _L0_tok_in['bias_idxs'], 'L0_attn_W_Q': _L0_attn_in['W_Q'], 'L0_attn_W_K': _L0_attn_in['W_K'], 'L0_attn_W_V': _L0_attn_in['W_V'], 'L0_attn_W_G': _L0_attn_in['W_G'], 'L0_attn_W_O': _L0_attn_in['W_O'], 'L0_attn_gn_weight': _L0_attn_in['gn_weight'], 'L0_attn_gn_bias': _L0_attn_in['gn_bias'], 'L0_ffn_gate_w': _L0_ffn_in['gate_w'], 'L0_ffn_w1': _L0_ffn_in['w1'], 'L0_ffn_b1': _L0_ffn_in['b1'], 'L0_ffn_w2': _L0_ffn_in['w2'], 'L0_ffn_b2': _L0_ffn_in['b2'], 'L0_ffn_sw1': _L0_ffn_in['sw1'], 'L0_ffn_sb1': _L0_ffn_in['sb1'], 'L0_ffn_sw2': _L0_ffn_in['sw2'], 'L0_ffn_sb2': _L0_ffn_in['sb2']}

def reference(x, L0_tok_kv_w, L0_tok_kv_g, L0_tok_kv_b, L0_tok_kv_m, L0_tok_kv_v, L0_tok_q_w, L0_tok_q_g, L0_tok_q_b, L0_tok_q_m, L0_tok_q_v, L0_tok_proj_w, L0_tok_proj_g, L0_tok_proj_b, L0_tok_proj_m, L0_tok_proj_v, L0_tok_attention_biases, L0_tok_bias_idxs, L0_attn_W_Q, L0_attn_W_K, L0_attn_W_V, L0_attn_W_G, L0_attn_W_O, L0_attn_gn_weight, L0_attn_gn_bias, L0_ffn_gate_w, L0_ffn_w1, L0_ffn_b1, L0_ffn_w2, L0_ffn_b2, L0_ffn_sw1, L0_ffn_sb1, L0_ffn_sw2, L0_ffn_sb2):
    import jax
    import jax.numpy as jnp

    def _L0_tok_ref(x, kv_w, kv_g, kv_b, kv_m, kv_v, q_w, q_g, q_b, q_m, q_v, proj_w, proj_g, proj_b, proj_m, proj_v, attention_biases, bias_idxs):
        import jax, jax.numpy as jnp
        import numpy as np
        import itertools
        B, RES, RES_, STRIDE = (64, 14, 7, 2)
        N, N_ = (RES * RES, RES_ * RES_)
        IN_DIM, OUT_DIM = (96, 128)
        H, KD, AR = (12, 32, 2)
        D = AR * KD
        DH = D * H
        NH_KD = KD * H
        KV_H = DH + NH_KD
        EPS = 1e-05

        def _bias_idxs():
            points = list(itertools.product(range(RES), range(RES)))
            points_ = list(itertools.product(range(RES_), range(RES_)))
            offsets, idxs = ({}, [])
            for p1 in points_:
                for p2 in points:
                    off = (abs(p1[0] * STRIDE - p2[0]), abs(p1[1] * STRIDE - p2[1]))
                    if off not in offsets:
                        offsets[off] = len(offsets)
                    idxs.append(offsets[off])
            return (np.array(idxs, dtype=np.int32).reshape(N_, N), len(offsets))

        def linear_bn(x, w, gamma, beta, mean, var):
            s = gamma / jnp.sqrt(var + EPS)
            return jnp.matmul(x, w.T) * s + (beta - mean * s)
        Bsz = x.shape[0]
        scale = KD ** (-0.5)
        kv = linear_bn(x, kv_w, kv_g, kv_b, kv_m, kv_v).reshape(Bsz, N, H, KD + D)
        k, v = (kv[..., :KD], kv[..., KD:])
        xs = x.reshape(Bsz, RES, RES, IN_DIM)[:, ::STRIDE, ::STRIDE].reshape(Bsz, N_, IN_DIM)
        q = linear_bn(xs, q_w, q_g, q_b, q_m, q_v).reshape(Bsz, N_, H, KD)
        bias = attention_biases[:, bias_idxs]
        attn = jnp.einsum('bqhd,bkhd->bhqk', q, k) * scale + bias
        attn = jax.nn.softmax(attn, axis=-1)
        out = jnp.einsum('bhqk,bkhd->bqhd', attn, v).reshape(Bsz, N_, DH)
        out = jax.nn.hard_swish(out)
        return linear_bn(out, proj_w, proj_g, proj_b, proj_m, proj_v)

    def _L0_attn_ref(x, W_Q, W_K, W_V, W_G, W_O, gn_weight, gn_bias):
        import jax, jax.numpy as jnp
        import numpy as np
        SIZE = 128
        NUM_HEADS = 8
        HEAD_SIZE = SIZE // NUM_HEADS
        EPS = 1e-05

        def _retention(x, W_Q, W_K, W_V):
            B, T, D = x.shape
            H, dh = (NUM_HEADS, HEAD_SIZE)
            q = (x @ W_Q).reshape(B, T, H, dh).transpose(0, 2, 1, 3)
            k = (x @ W_K).reshape(B, T, H, dh).transpose(0, 2, 1, 3)
            v = (x @ W_V).reshape(B, T, H, dh).transpose(0, 2, 1, 3)
            gammas = 1.0 - jnp.exp2(-5.0 - jnp.arange(H, dtype=jnp.float32))
            idx = jnp.arange(T)
            diff = (idx[:, None] - idx[None, :]).astype(jnp.float32)
            causal = diff >= 0
            decay = jnp.where(causal[None], jnp.exp(diff[None] * jnp.log(gammas)[:, None, None]), 0.0)
            scores = jnp.einsum('bhtd,bhsd->bhts', q, k) / jnp.sqrt(jnp.float32(dh))
            out = jnp.einsum('bhts,bhsd->bhtd', scores * decay[None], v)
            return out.transpose(0, 2, 1, 3).reshape(B, T, D)

        def _group_norm(y, weight, bias):
            B, T, D = y.shape
            g = y.reshape(B * T, NUM_HEADS, HEAD_SIZE)
            mean = jnp.mean(g, axis=-1, keepdims=True)
            var = jnp.var(g, axis=-1, keepdims=True)
            g = (g - mean) / jnp.sqrt(var + EPS)
            g = g.reshape(B * T, D) * weight + bias
            return g.reshape(B, T, D)
        ret = _retention(x, W_Q, W_K, W_V)
        normed = _group_norm(ret, gn_weight, gn_bias)
        return jax.nn.silu(x @ W_G + normed) @ W_O

    def _L0_ffn_ref(x, gate_w, w1, b1, w2, b2, sw1, sb1, sw2, sb2):
        import jax, jax.numpy as jnp
        import numpy as np
        D, H, E, B, S = (128, 512, 16, 8, 2048)
        MAX_GROUP_SIZE = 1024
        MIN_CAPACITY = 8
        CAPACITY_FACTOR = 1.0

        def _group_dims(num_tokens, num_experts):
            num_groups = -(-num_tokens // MAX_GROUP_SIZE)
            while num_tokens % num_groups != 0 or num_groups % num_experts != 0:
                num_groups += 1
            return (num_tokens // num_groups, num_groups)
        Bn, Sn, Dn = x.shape
        En = gate_w.shape[1]
        T = Bn * Sn
        group_size, num_groups = _group_dims(T, En)
        cap = max(int(round(CAPACITY_FACTOR * group_size * num_groups / En)), MIN_CAPACITY)
        xg = x.reshape(num_groups, group_size, Dn)
        logits = jnp.einsum('gsd,de->gse', xg, gate_w)
        probs = jax.nn.softmax(logits, axis=-1)
        flat_probs = probs.transpose(2, 0, 1).reshape(En, T)
        scores, tok_idx = jax.lax.top_k(flat_probs, cap)
        xf = x.reshape(T, Dn)
        toks = xf[tok_idx]
        h = jax.nn.gelu(jnp.einsum('ecd,edh->ech', toks, w1) + b1[:, None, :])
        y = jnp.einsum('ech,ehd->ecd', h, w2) + b2[:, None, :]
        y = y * scores[..., None]
        routed = jnp.zeros_like(xf).at[tok_idx.reshape(-1)].add(y.reshape(-1, Dn))
        shared = jax.nn.gelu(xf @ sw1 + sb1) @ sw2 + sb2
        out = (routed + shared).reshape(Bn, Sn, Dn)
        return out
    h = _L0_tok_ref(x, L0_tok_kv_w, L0_tok_kv_g, L0_tok_kv_b, L0_tok_kv_m, L0_tok_kv_v, L0_tok_q_w, L0_tok_q_g, L0_tok_q_b, L0_tok_q_m, L0_tok_q_v, L0_tok_proj_w, L0_tok_proj_g, L0_tok_proj_b, L0_tok_proj_m, L0_tok_proj_v, L0_tok_attention_biases, L0_tok_bias_idxs)
    h = h + _L0_attn_ref(_layernorm(h, axis=-1), L0_attn_W_Q, L0_attn_W_K, L0_attn_W_V, L0_attn_W_G, L0_attn_W_O, L0_attn_gn_weight, L0_attn_gn_bias)
    h = h + _L0_ffn_ref(_layernorm(h, axis=-1), L0_ffn_gate_w, L0_ffn_w1, L0_ffn_b1, L0_ffn_w2, L0_ffn_b2, L0_ffn_sw1, L0_ffn_sb1, L0_ffn_sw2, L0_ffn_sb2)
    return h

_drawn_inputs = setup_inputs


def setup_inputs(seed=0):
    import zlib

    import numpy as np

    out = dict(_drawn_inputs(seed))
    spreads = {'L0_attn_gn_weight': (1.0, 0.2),
     'L0_attn_gn_bias': (0.0, 0.399),
     'L0_ffn_b1': (0.0, 0.8),
     'L0_ffn_b2': (0.0, 0.1),
     'L0_ffn_sb1': (0.0, 0.1),
     'L0_ffn_sb2': (0.0, 0.1)}
    factors = {'L0_tok_attention_biases': 7.249,
     'L0_attn_W_G': 2.941,
     'L0_ffn_w1': 3.286,
     'L0_ffn_w2': 2.96}
    for name, (base, spread) in spreads.items():
        noise = np.random.default_rng([zlib.crc32(name.encode()), seed]).standard_normal(out[name].shape)
        drawn = base * np.exp(spread * noise) if base else spread * noise
        out[name] = jnp.asarray(drawn.astype(out[name].dtype))
    for name, factor in factors.items():
        out[name] = (out[name] * factor).astype(out[name].dtype)
    return out
```

```python
import math
from contextlib import ExitStack

import numpy as np

import concourse.bass as bass
from concourse import mybir

F32 = mybir.dt.float32
BF16 = mybir.dt.bfloat16
I32 = mybir.dt.int32
ALU = mybir.AluOpType
ACT = mybir.ActivationFunctionType
AX = mybir.AxisListType
ds = bass.ds

B, RES, STRIDE = 64, 14, 2
N = RES * RES
NQ = (RES // STRIDE) ** 2
C = 96
CA = C + 1
H, KD, VD = 12, 32, 64
DH = H * VD
NOFF = N
HALF = N // 2
ROWS = H * NQ
CH = 5
CR = -(-ROWS // CH)
D = 128
T2 = 2 * NQ
NP = B // 2
T = B * NQ
EPS = 1e-5

RH, RD = 8, 16
TG = 4
NG = NP // TG
GT = TG * T2

E = 16
HID = 512
HC = HID // 128
CAP = T // E
TH = CAP // 2
EC = 8
ROW = D + E
SA, SB_ = -(-CAP // 16), 16
SLOTS = SA * SB_
RING = 4
EG = 8


def chunk_rows(c):
    return min(CR, ROWS - c * CR)


def build(nc, d, out):
    with ExitStack() as ctx:
        tok_scope = ExitStack()
        scope = [ctx]

        def sb(name, shape, dt=F32):
            return scope[0].enter_context(nc.sbuf_tensor(name, shape, dt))

        def sem(name):
            return ctx.enter_context(nc.semaphore(name))

        bank = [ctx.enter_context(nc.psum_tensor(f"bank{k}", [128, 512], F32)) for k in range(8)]
        s_bank, t_bank, m_bank = bank[0:3], bank[3:5], bank[5:8]

        prob_rows = nc.dram_tensor("prob_rows", [T, ROW], F32).ap()
        list_d = nc.dram_tensor("list_scratch", [E, SLOTS], F32).ap()
        bias_d = nc.dram_tensor("bias_scratch", [3, H, NQ * N], F32).ap()

        ident = sb("ident", [128, 128])
        w_q, w_k, w_o = (sb(n, [D, D]) for n in ("w_q", "w_k", "w_o"))
        w_vg = sb("w_vg", [D, 2 * D])
        head_mask = sb("head_mask", [D, RH])
        decay = sb("decay", [T2, RH, T2])
        gn_w, gn_b = sb("gn_w", [T2, D]), sb("gn_b", [T2, D])
        gate_w = sb("gate_w", [D, E])
        sw1, sw2 = sb("sw1", [D, HID]), sb("sw2", [128, HC, D])
        sb1, sb2 = sb("sb1", [128, HC]), sb("sb2", [T2, D])
        same_expert = sb("same_expert", [128, 128])
        before = sb("before", [128, 128])
        iota_slot = sb("iota_slot", [T2, SB_])
        tok_col = sb("tok_col", [T2, 1])
        tile_num = sb("tile_num", [T2, TG, EC])
        diag = sb("diag", [EG * SA, EG, SB_])
        h_all = sb("h_all", [T2, NP, D])
        scope[0] = tok_scope
        iota_off = sb("iota_off", [HALF, 2])
        bias_cols = sb("bias_cols", [HALF, 2, H])
        q_w = sb("q_w", [KD, H, C])
        k_w = sb("k_w", [KD, H, C])
        par_qk = sb("par_qk", [KD, 4, 2 * H])
        s_qk = sb("s_qk", [KD, 2, 2 * H])
        q_aug = sb("q_aug", [KD, H, CA])
        k_aug = sb("k_aug", [KD, H, CA])
        qk_mat = sb("qk_mat", [CA, H, CA])
        par_v = sb("par_v", [128, 4, DH + D])
        s_v = sb("s_v", [128, 2, DH + D])
        v_w = sb("v_w", [C, DH])
        v_aug = sb("v_aug", [CA, H, VD + 1])
        proj = sb("proj", [128, DH // 128, D])
        idx_f = sb("idx_f", [HALF, 2, 7 * N], I32)
        onehot = [sb(f"onehot{p}", [HALF, 2, 7 * N], BF16) for p in range(2)]
        bias_rest = sb("bias_rest", [HALF, 2, H])
        bias_parts = sb("bias_parts", [HALF, 2, 3, 32], BF16)
        bias_out = sb("bias_out", [96, 2, 7 * N])
        bias_neg = sb("bias_neg", [CR, CH, N])
        bias_low = sb("bias_low", [CR, 2, CH, N])

        x_t = [sb(f"x_t{p}", [CA, 2 * N]) for p in range(2)]
        x_n = [sb(f"x_n{p}", [HALF, 4, CA]) for p in range(2)]
        g_t = sb("g_t", [CA, 2, ROWS])
        probs = sb("probs", [CR, 2, CH, N])
        neg_max = sb("neg_max", [CR, 2, CH])
        p_t = sb("p_t", [HALF, 2, ROWS])
        px_t = sb("px_t", [CA, H, T2])
        o_rec = sb("o_rec", [T2, 2, H // 2])
        o_sb = sb("o_sb", [T2, DH])
        o_u = sb("o_u", [T2, DH])
        o_a = sb("o_a", [T2, DH])
        three = sb("three", [T2, 1])
        a_t = sb("a_t", [128, DH // 128, T2])
        tok_scope.close()
        scope[0] = ctx

        hn_t = sb("hn_t", [D, T])
        hn_g = sb("hn_g", [D, GT])
        rows = sb("rows", [T2, NP, ROW])
        logit = sb("logit", [T2, NP, E])
        lmax, lsum = sb("lmax", [T2, NP]), sb("lsum", [T2, NP])
        stats = sb("stats", [T2, TG, 6])
        mean_var = sb("mean_var", [T2, TG, 2])
        rstd = sb("rstd", [T2, TG])
        ln = sb("ln", [T2, TG, D])
        ret_scope = ExitStack()
        scope[0] = ret_scope
        ln_t = sb("ln_t", [D, GT])
        k_t = sb("k_t", [D, GT])
        v_sb = sb("v_sb", [T2, TG, D])
        gate_all = sb("gate_all", [T2, NP, D])
        q_heads = [sb(f"q_heads{p}", [D, RH, T2]) for p in range(2)]
        sc_tmp = sb("sc_tmp", [T2, RH // 2, T2])
        sc = [sb(f"sc{p}", [T2, RH, T2]) for p in range(2)]
        ret = sb("ret", [T2, TG * RH, RD])
        ret_c = sb("ret_c", [T2, TG * RH, RD])
        ret_sq = sb("ret_sq", [T2, TG * RH, RD])
        ret_n = sb("ret_n", [T2, TG, D])
        gmean = sb("gmean", [T2, TG * RH])
        gstd = sb("gstd", [T2, TG * RH])
        z = sb("z", [T2, TG, D])
        z_t = sb("z_t", [D, GT])
        ret_scope.close()
        scope[0] = ctx
        prob_j = sb("prob_j", [T2, TG, E * EC])
        xp = sb("xp", [128, GT])
        thr, cand, bit, mask = (sb(n, [128, 1], I32) for n in ("thr", "cand", "bit", "mask"))
        cnt = sb("cnt", [128, 1])
        above, equal, scan_e, sel, scan_s = (sb(n, [128, GT]) for n in ("above", "equal", "scan_e", "sel", "scan_s"))
        col = sb("col", [128, 4])
        hid = [sb(f"hid{p}", [128, HC, GT]) for p in range(2)]
        out_g = [sb(f"out_g{p}", [T2, TG, D]) for p in range(2)]
        slot = sb("slot", [T2, TG, 128], I32)
        slot_a, slot_b = sb("slot_a", [T2, TG, 128], I32), sb("slot_b", [T2, TG, 128], I32)
        hot_a = sb("hot_a", [T2, TG, EC, E, SA], BF16)
        hot_at = sb("hot_at", [T2, TG, EC, E, SA], BF16)
        hot_ap = sb("hot_ap", [T2, TG, EC, E, SA], BF16)
        hot_b = sb("hot_b", [T2, TG, EC, E, SB_], BF16)
        list_t = sb("list_t", [EG * SA, 2, EG, SB_])
        list_s = sb("list_s", [EG * SA, 2, SB_])
        list_r = sb("list_r", [2 * E, TH])
        idx_all = sb("idx_all", [TH, 2 * E], I32)
        idx2 = [sb(f"idx2{p}", [TH, 2], I32) for p in range(RING)]
        tok = [[sb(f"tok{p}{s}", [TH, ROW]) for s in range(2)] for p in range(RING)]
        tok_t = [sb(f"tok_t{p}", [D, CAP]) for p in range(2)]
        w1 = [sb(f"w1{p}", [D, HID]) for p in range(2)]
        w2 = [sb(f"w2{p}", [128, HC, D]) for p in range(2)]
        b1 = [sb(f"b1{p}", [128, HC]) for p in range(2)]
        b2 = [sb(f"b2{p}", [TH, D]) for p in range(2)]
        ehid = [sb(f"ehid{p}", [128, HC, CAP]) for p in range(2)]
        y = [[sb(f"y{p}{s}", [TH, D]) for s in range(2)] for p in range(RING)]

        small_in, wts2_in = sem("small_in"), sem("wts2_in")
        names = ("step var_ready std_ready ln_ready lt_ready lt_copied q_ready k_ready k_copied vg_ready vg_copied qm_made "
                 "sa_ready sb_ready sb_copied sa_done sb_done pv_ready ret_copied c_ready sq_ready gvar_ready gstd_ready gn_ready "
                 "pool_step z_done zs_ready zt_ready zt_copied wo_ready h2_done l_var l_std hn_ready hnt_ready hnt_copied "
                 "rows_copied lg_ready lg_done lx_ready le_ready pr_ready xp_ready xp_copied sh_ready sh_gelu shy_ready shy_taken "
                 "cnt_ready tot_ready col_ready off_ready slot_ready slot_taken hot_ready list_ready list_done lr_ready lr_done "
                 "table_out list_out list_in idx_copied tt_ready tt_copied eh_ready eh_gelu ey_ready ey_taken y_done "
                 "scattered").split()
        (step, var_ready, std_ready, ln_ready, lt_ready, lt_copied, q_ready, k_ready, k_copied, vg_ready, vg_copied, qm_made,
         sa_ready, sb_ready, sb_copied, sa_done, sb_done, pv_ready, ret_copied, c_ready, sq_ready, gvar_ready, gstd_ready, gn_ready,
         pool_step, z_done, zs_ready, zt_ready, zt_copied, wo_ready, h2_done, l_var, l_std, hn_ready, hnt_ready, hnt_copied,
         rows_copied, lg_ready, lg_done, lx_ready, le_ready, pr_ready, xp_ready, xp_copied, sh_ready, sh_gelu, shy_ready, shy_taken,
         cnt_ready, tot_ready, col_ready, off_ready, slot_ready, slot_taken, hot_ready, list_ready, list_done, lr_ready, lr_done,
         table_out, list_out, list_in, idx_copied, tt_ready, tt_copied, eh_ready, eh_gelu, ey_ready, ey_taken, y_done,
         scattered) = (sem(n) for n in names)
        out_sent = [sem(f"out_sent{p}") for p in range(2)]
        tok_in = [sem(f"tok_in{p}") for p in range(RING)]
        ew_in = [sem(f"ew_in{p}") for p in range(2)]
        out_rows = out.rearrange("(i p) c -> p i c", p=T2)

        const_in = sem("const_in")
        wts_in = sem("wts_in")
        idx_in = [sem(f"idx_in{p}") for p in range(2)]
        bias_back = sem("bias_back")
        bias_stored = [sem(f"bias_stored{p}") for p in range(2)]
        ones_set = sem("ones_set")
        x_in = [sem(f"x_in{p}") for p in range(2)]
        set_dve = sem("set_dve")
        set_act = sem("set_act")
        bank_read, parts_done = sem("bank_read"), sem("parts_done")
        mat_ready = sem("mat_ready")
        mat_copied = sem("mat_copied")
        hot_made = sem("hot_made")
        bias_mm = sem("bias_mm")
        bias_copied = sem("bias_copied")
        g_ready, g_copied = sem("g_ready"), sem("g_copied")
        s_ready, s_taken = sem("s_ready"), sem("s_taken")
        ttr_done, exp_done = sem("ttr_done"), sem("exp_done")
        t_ready, pt_copied = sem("t_ready"), sem("pt_copied")
        px_ready, px_copied = sem("px_ready"), sem("px_copied")
        o_ready, o_read, o_rec_done = sem("o_ready"), sem("o_read"), sem("o_rec_done")
        u_ready, a_ready = sem("u_ready"), sem("a_ready")
        at_ready, at_copied = sem("at_ready"), sem("at_copied")
        h_ready, h_copied = sem("h_ready"), sem("h_copied")
        dve_waited, pool_waited = sem("dve_waited"), sem("pool_waited")

        idx_flat = d["idx"].rearrange("q k -> (q k)")
        W7 = 7 * N

        def row_of_h(g):
            return h_all[:, g, :]

        with nc.Block() as block:
            @block.sync
            def _(sp):
                sp.dma_start(iota_off[:], d["iota_off"]).then_inc(const_in, 16)
                sp.dma_start(bias_cols[:], d["bias_cols"]).then_inc(const_in, 16)
                for k in range(2):
                    sp.dma_start(idx_f[:, k, :], idx_flat[k * W7:(k + 1) * W7].partition_broadcast(HALF)).then_inc(idx_in[k], 16)
                sp.dma_start(par_qk[:], d["par_qk"]).then_inc(wts_in, 16)
                sp.dma_start(q_w[:], d["q_w"]).then_inc(wts_in, 16)
                sp.dma_start(k_w[:], d["k_w"]).then_inc(wts_in, 16)
                sp.dma_start(v_w[:], d["v_w"]).then_inc(wts_in, 16)
                sp.dma_start(proj[:], d["proj"]).then_inc(wts_in, 16)
                sp.dma_start(par_v[:], d["par_v"].partition_broadcast(128)).then_inc(wts_in, 16)
                sp.dma_start(ident[:], d["ident"]).then_inc(wts_in, 16)

                def load_x(i, p):
                    sp.dma_start(x_t[p][0:C, :], d["x_t"][:, ds(i * 2 * N, 2 * N)]).then_inc(x_in[p], 16)
                    sp.dma_start(x_n[p][:, :, 0:C],
                                 d["x"][ds(i * 2, 2)].rearrange("b (s p) c -> p (b s) c", s=2)).then_inc(x_in[p], 16)

                load_x(0, 0)
                load_x(1, 1)
                for k in range(2, 9):
                    if k < 7:
                        sp.wait_ge(hot_made, k - 1)
                        sp.dma_start(idx_f[:, k % 2, :], idx_flat[k * W7:(k + 1) * W7].partition_broadcast(HALF)).then_inc(idx_in[k % 2], 16)
                    sp.wait_ge(bias_copied, k - 1)
                    for part in range(3):
                        sp.dma_start(bias_d[part, :, (k - 2) * W7:(k - 1) * W7],
                                     bias_out[32 * part:32 * part + H, k % 2, :]).then_inc(bias_stored[k % 2], 16)
                sp.wait_ge(bias_stored[0], 4 * 48)
                sp.wait_ge(bias_stored[1], 3 * 48)
                for part, o in ((0, bias_neg[:]), (1, bias_low[:, 0]), (2, bias_low[:, 1])):
                    flat = bias_d[part].rearrange("h (q k) -> (h q) k", k=N)
                    sp.dma_start(o[:, 0:CH - 1, :], flat[0:(CH - 1) * CR].rearrange("(c p) k -> p c k", p=CR)).then_inc(bias_back, 16)
                    sp.dma_start(o[0:chunk_rows(CH - 1), CH - 1, :], flat[(CH - 1) * CR:ROWS]).then_inc(bias_back, 16)
                for o, n in ((w_q, "w_q"), (w_k, "w_k"), (w_vg, "w_vg"), (w_o, "w_o"), (head_mask, "head_mask"), (decay, "decay"),
                             (gate_w, "gate_w"), (sw1, "sw1"), (sw2, "sw2"), (sb1, "sb1"), (same_expert, "same_expert"),
                             (before, "before"), (iota_slot, "iota_slot"), (tok_col, "tok_col"), (tile_num, "tile_num"), (diag, "diag")):
                    sp.dma_start(o[:], d[n]).then_inc(wts2_in, 16)
                for o, n in ((gn_w, "gn_w"), (gn_b, "gn_b"), (sb2, "sb2")):
                    sp.dma_start(o[:], d[n].partition_broadcast(T2)).then_inc(wts2_in, 16)
                with sp.Fori(1, NP // 2) as j:
                    for p in range(2):
                        sp.wait_ge(o_ready, 2 * (2 * j + p) - 2)
                        load_x(2 * j + p, p)
                sp.wait_ge(h_copied, NP)
                sp.wait_ge(rows_copied, NG)
                sp.wait_ge(pr_ready, 1)
                sp.dma_start(prob_rows.rearrange("(i p) c -> p i c", p=T2), rows[:, :, :]).then_inc(table_out, 16)

                def load_expert(e, p):
                    sp.dma_start(w1[p][:], d["w1"][ds(e, 1)].rearrange("e d h -> (e d) h")).then_inc(ew_in[p], 16)
                    sp.dma_start(w2[p][:], d["w2"][ds(e, 1)].rearrange("e k c n -> (e k) c n")).then_inc(ew_in[p], 16)
                    sp.dma_start(b1[p][:], d["b1"][ds(e, 1)].rearrange("e k c -> (e k) c")).then_inc(ew_in[p], 16)
                    sp.dma_start(b2[p][:], d["b2"][ds(e, 1)].rearrange("e n -> (e n)").partition_broadcast(TH)).then_inc(ew_in[p], 16)

                load_expert(0, 0)
                load_expert(1, 1)
                with sp.Fori(0, NG // 2) as j:
                    for p in range(2):
                        sp.wait_ge(shy_taken, 2 * j + p + 1)
                        sp.dma_start(out_rows[:, ds((2 * j + p) * TG, TG), :], out_g[p][:]).then_inc(out_sent[p], 16)
                sp.wait_ge(list_done, 1)
                sp.dma_start(list_d.rearrange("(g e) (a b) -> (e a) g b", g=2, a=SA), list_s[:]).then_inc(list_out, 16)
                sp.wait_ge(list_out, 16)
                for s in range(2):
                    sp.dma_start(list_r[s * E:(s + 1) * E, :], list_d[:, s * TH:(s + 1) * TH]).then_inc(list_in, 16)
                with sp.Fori(1, E // 2) as j:
                    for p in range(2):
                        sp.wait_ge(y_done, 2 * (2 * j + p - 1))
                        load_expert(2 * j + p, p)
                sp.wait_ge(scattered, 2 * 16 * E)

            @block.gpsimd
            def _(pool):
                for p in range(2):
                    if p:
                        pool.wait_ge(ones_set, 2 * p)
                    nc.gpsimd.memset(x_t[p][C:CA, :], 1.0).then_inc(ones_set, 1)
                    pool.wait_ge(ones_set, 2 * p + 1)
                    nc.gpsimd.memset(x_n[p][:, :, C:CA], 1.0).then_inc(ones_set, 1)

                pool.wait_ge(h_copied, NP)
                pool.wait_ge(wts2_in, WTS2)

                def retention(g, first=False):
                    for u in range(TG):
                        k = TG * g + u
                        pool.wait_ge(sb_copied, k + 1)
                        if not (first and u < 2):
                            pool.wait_ge(pv_ready, k - 1)
                        nc.gpsimd.tensor_tensor(sc[u % 2][:, RH // 2:RH, :], sc_tmp[:], decay[:, RH // 2:RH, :], ALU.mult).then_inc(sb_done, 1)
                    pool.wait_ge(c_ready, g + 1)
                    nc.gpsimd.tensor_tensor(ret_sq[:], ret_c[:], ret_c[:], ALU.mult).then_inc(sq_ready, 1)
                    pool.wait_ge(gn_ready, g + 1)
                    nc.gpsimd.tensor_tensor(ret_n[:], ret_n[:], gn_w[:].unsqueeze(1).to_broadcast([T2, TG, D]), ALU.mult).then_inc(pool_step, 1)
                    pool.wait_ge(pool_step, 2 * g + 1)
                    nc.gpsimd.tensor_tensor(ret_n[:], ret_n[:], gn_b[:].unsqueeze(1).to_broadcast([T2, TG, D]), ALU.add).then_inc(pool_step, 1)
                    pool.wait_ge(pool_step, 2 * g + 2)
                    zg = gate_all[:, ds(TG * g, TG), :]
                    nc.gpsimd.tensor_tensor(zg, ret_n[:], zg, ALU.add).then_inc(z_done, 1)

                retention(0, first=True)
                with pool.Fori(1, NG) as g:
                    retention(g)
                with pool.Fori(0, NG) as g:
                    pool.wait_ge(hn_ready, g + 1)
                    nc.gpsimd.tensor_copy(rows[:, ds(TG * g, TG), 0:D], ln[:]).then_inc(rows_copied, 1)

                def gather(e, p):
                    nc.gpsimd.tensor_copy(idx2[p][:, 0:1], idx_all[:, ds(e, 1)])
                    nc.gpsimd.tensor_copy(idx2[p][:, 1:2], idx_all[:, ds(e + E, 1)]).then_inc(idx_copied, 1)
                    pool.wait_ge(idx_copied, e + 1)
                    pool.sem_inc(pool_waited, 1)
                    for s in range(2):
                        nc.gpsimd.indirect_dma_start(out=tok[p][s][:], out_offset=None, in_=prob_rows,
                                                     in_offset=bass.IndirectOffsetOnAxis(ap=idx2[p][:, s:s + 1], axis=0)).then_inc(tok_in[p], 16)

                pool.wait_ge(table_out, 16)
                pool.wait_ge(lr_done, 1)
                for e in range(RING - 1):
                    gather(e, e)
                for p in range(2):
                    pool.wait_ge(out_sent[p], 16 * NG // 2)

                def scatter(e, p, first=False):
                    pool.wait_ge(y_done, 2 * e + 2)
                    if not first:
                        pool.wait_ge(scattered, 32 * e)
                    pool.sem_inc(pool_waited, 1)
                    for s in range(2):
                        nc.gpsimd.indirect_dma_start(out=out, out_offset=bass.IndirectOffsetOnAxis(ap=idx2[p][:, s:s + 1], axis=0),
                                                     in_=y[p][s][:], in_offset=None, compute_op=ALU.add).then_inc(scattered, 16)

                scatter(0, 0, first=True)
                gather(RING - 1, RING - 1)
                for e in range(1, RING):
                    scatter(e, e)
                    gather(e + RING - 1, e - 1)
                with pool.Fori(1, E // RING - 1) as j:
                    for p in range(RING):
                        scatter(RING * j + p, p)
                        gather(RING * j + p + RING - 1, (p - 1) % RING)
                scatter(E - RING, 0)
                gather(E - 1, RING - 1)
                for p in range(1, RING):
                    scatter(E - RING + p, p)

            @block.scalar
            def _(act):
                for k in range(7):
                    if k >= 2:
                        act.wait_ge(bias_stored[k % 2], 48 * (k // 2))
                    for n in range(4):
                        act.wait_ge(bias_mm, 4 * k + n + 1)
                        last = nc.scalar.mul(bias_out[:, k % 2, n * 343:(n + 1) * 343], s_bank[n % 2][0:96, 0:343], -1.0)
                        last.then_inc(bank_read, 1)
                    act.wait_ge(bank_read, 4 * (k + 1))
                    act.sem_inc(bias_copied, 1)
                    if k == 1:
                        act.wait_ge(set_dve, 2)
                        nc.scalar.activation(s_qk[:, 0, :], s_qk[:, 0, :], ACT.Sqrt).then_inc(set_act, 1)
                        nc.scalar.activation(s_v[:, 0, :], s_v[:, 0, :], ACT.Sqrt).then_inc(set_act, 1)

                def exps(k, kp):
                    for c in range(CH):
                        m = chunk_rows(c)
                        act.wait_ge(ttr_done, CH * k + c + 1)
                        nc.scalar.activation(probs[0:m, kp, c, :], probs[0:m, kp, c, :], ACT.Exp,
                                             bias=neg_max[0:m, kp, c:c + 1], scale=-1.0).then_inc(exp_done, 1)

                def copy_px(k, b, f0):
                    for a in range(2):
                        act.wait_ge(px_ready, 2 * k + a + 1)
                        nc.scalar.copy(px_t[:, a * 6:(a + 1) * 6, b * NQ:(b + 1) * NQ],
                                       m_bank[(f0 + a) % 3][0:CA, 0:6 * NQ].rearrange("p (h q) -> p h q", h=6)).then_inc(px_copied, 1)

                def copy_at(i):
                    for a in range(2):
                        act.wait_ge(at_ready, 2 * i + a + 1)
                        nc.scalar.copy(a_t[:, 3 * a:3 * a + 3, :],
                                       m_bank[1 + a][:, 0:3 * T2].rearrange("p (c t) -> p c t", c=3)).then_inc(at_copied, 1)

                def relu(i):
                    act.wait_ge(o_read, 2 * i + 2)
                    nc.scalar.activation(o_u[:], o_sb[:], ACT.Relu, bias=three[:, 0:1]).then_inc(u_ready, 1)

                def body(i, first=False, last=False):
                    exps(2 * i + 1, 1)
                    if not first:
                        relu(i - 1)
                    copy_px(2 * i, 0, 0)
                    if not last:
                        exps(2 * i + 2, 0)
                    copy_px(2 * i + 1, 1, 2)
                    if not first:
                        copy_at(i - 1)

                exps(0, 0)
                body(0, first=True)
                with act.Fori(1, NP - 1) as i:
                    body(i)
                body(NP - 1, last=True)
                relu(NP - 1)
                copy_at(NP - 1)

                act.wait_ge(h_copied, NP)

                def root_ln(n):
                    act.wait_ge(var_ready, n + 1)
                    nc.scalar.activation(rstd[:], rstd[:], ACT.Sqrt).then_inc(std_ready, 1)

                def retention(g, first=False, last=False):
                    act.wait_ge(lt_ready, g + 1)
                    nc.scalar.copy(ln_t[:], bank[0][:, 0:GT]).then_inc(lt_copied, 1)
                    act.wait_ge(k_ready, g + 1)
                    nc.scalar.copy(k_t[:], bank[2][:, 0:GT]).then_inc(k_copied, 1)
                    for a in range(2):
                        act.wait_ge(vg_ready, 2 * g + a + 1)
                        vg = bank[3 + a][0:T2, :].rearrange("p (u v) -> p u v", u=2)
                        nc.scalar.copy(v_sb[:, 2 * a:2 * a + 2, :], vg[:, :, 0:D])
                        nc.scalar.copy(gate_all[:, ds(TG * g + 2 * a, 2), :], vg[:, :, D:2 * D]).then_inc(vg_copied, 1)
                    for u in range(TG):
                        k = TG * g + u
                        act.wait_ge(sb_ready, k + 1)
                        if not (first and u < 1):
                            act.wait_ge(sb_done, k)
                        nc.scalar.copy(sc_tmp[:], bank[6][0:T2, 0:GT].rearrange("p (h t) -> p h t", h=TG)).then_inc(sb_copied, 1)
                    act.wait_ge(pv_ready, TG * g + TG)
                    if not first:
                        act.wait_ge(c_ready, g)
                    nc.scalar.copy(ret[:], bank[7][0:T2, :].rearrange("p (h r) -> p h r", r=RD)).then_inc(ret_copied, 1)
                    if not last:
                        root_ln(g + 1)
                    act.wait_ge(gvar_ready, g + 1)
                    nc.scalar.activation(gstd[:], gstd[:], ACT.Sqrt).then_inc(gstd_ready, 1)

                root_ln(0)
                retention(0, first=True)
                with act.Fori(1, NG - 1) as g:
                    retention(g)
                retention(NG - 1, last=True)

                def silu(g):
                    nc.scalar.activation(z[:], gate_all[:, ds(TG * g, TG), :], ACT.Silu).then_inc(zs_ready, 1)

                def copy_zt(g):
                    act.wait_ge(zt_ready, g + 1)
                    nc.scalar.copy(z_t[:], bank[0][:, 0:GT]).then_inc(zt_copied, 1)

                act.wait_ge(z_done, NG)
                silu(0)
                with act.Fori(0, NG - 1) as g:
                    act.wait_ge(zt_ready, g + 1)
                    silu(g + 1)
                    copy_zt(g)
                copy_zt(NG - 1)

                with act.Fori(0, NG) as g:
                    act.wait_ge(l_var, g + 1)
                    nc.scalar.activation(rstd[:], rstd[:], ACT.Sqrt).then_inc(l_std, 1)
                    act.wait_ge(hnt_ready, g + 1)
                    nc.scalar.copy(hn_g[:], bank[2][:, 0:GT])
                    nc.scalar.copy(hn_t[:, ds(GT * g, GT)], bank[2][:, 0:GT]).then_inc(hnt_copied, 1)

                act.wait_ge(lx_ready, 1)
                nc.scalar.activation(logit[:], logit[:], ACT.Exp).then_inc(le_ready, 1)

                def gelu_shared(g, p, first=False):
                    for c in range(HC):
                        act.wait_ge(sh_ready, HC * g + c + 1)
                        if c == 0 and not first:
                            act.wait_ge(shy_ready, g - 1)
                        nc.scalar.activation(hid[p][:, c, :], bank[c][:, 0:GT], ACT.Gelu_apprx_tanh, bias=sb1[:, c:c + 1]).then_inc(sh_gelu, 1)

                gelu_shared(0, 0, True)
                gelu_shared(1, 1, True)
                with act.Fori(1, NG // 2) as j:
                    for p in range(2):
                        gelu_shared(2 * j + p, p)

                def copy_tt(e, p):
                    act.wait_ge(tt_ready, e + 1)
                    nc.scalar.copy(tok_t[p][:], bank[0][:, 0:CAP]).then_inc(tt_copied, 1)

                def gelu_expert(e, p):
                    for c in range(HC):
                        act.wait_ge(eh_ready, 2 * e + c // 2 + 1)
                        nc.scalar.activation(ehid[p][:, c, :], bank[1 + c // 2][:, (c % 2) * CAP:(c % 2 + 1) * CAP], ACT.Gelu_apprx_tanh,
                                             bias=b1[p][:, c:c + 1]).then_inc(eh_gelu, 1)

                copy_tt(0, 0)
                with act.Fori(0, E // 2 - 1) as j:
                    for p in range(2):
                        gelu_expert(2 * j + p, p)
                        copy_tt(2 * j + p + 1, 1 - p)
                gelu_expert(E - 2, 0)
                copy_tt(E - 1, 1)
                gelu_expert(E - 1, 1)

            @block.vector
            def _(dve):
                done = [0]

                def setup(ins):
                    done[0] += 1
                    ins.then_inc(set_dve, 1)
                    return done[0]

                def hot(k):
                    dve.wait_ge(idx_in[k % 2], 16 * (k // 2 + 1))
                    if k >= 2:
                        dve.wait_ge(bias_mm, 4 * (k - 1))
                    nc.vector.tensor_scalar(onehot[k % 2][:, 0, :], idx_f[:, k % 2, :], iota_off[:, 0:1], None, ALU.is_equal)
                    nc.vector.tensor_scalar(onehot[k % 2][:, 1, :], idx_f[:, k % 2, :], iota_off[:, 1:2], None, ALU.is_equal).then_inc(hot_made, 1)

                dve.wait_ge(const_in, 32)
                nc.vector.memset(bias_parts[:], 0.0).then_inc(parts_done, 1)
                dve.wait_ge(parts_done, 1)
                nc.vector.tensor_copy(bias_parts[:, :, 0, 0:H], bias_cols[:]).then_inc(parts_done, 1)
                dve.wait_ge(parts_done, 2)
                nc.vector.tensor_tensor(bias_rest[:], bias_cols[:], bias_parts[:, :, 0, 0:H], ALU.subtract).then_inc(parts_done, 1)
                dve.wait_ge(parts_done, 3)
                nc.vector.tensor_copy(bias_parts[:, :, 1, 0:H], bias_rest[:]).then_inc(parts_done, 1)
                dve.wait_ge(parts_done, 4)
                nc.vector.tensor_tensor(bias_rest[:], bias_rest[:], bias_parts[:, :, 1, 0:H], ALU.subtract).then_inc(parts_done, 1)
                dve.wait_ge(parts_done, 5)
                nc.vector.tensor_copy(bias_parts[:, :, 2, 0:H], bias_rest[:]).then_inc(parts_done, 1)
                for k in range(3):
                    hot(k)
                dve.wait_ge(wts_in, 7 * 16)
                setup(nc.vector.tensor_scalar_add(s_qk[:, 0, :], par_qk[:, 3, :], EPS))
                setup(nc.vector.tensor_scalar_add(s_v[:, 0, :], par_v[:, 3, :], EPS))
                for n, (s, par) in enumerate(((s_qk, par_qk), (s_v, par_v))):
                    dve.wait_ge(set_act, n + 1)
                    dve.wait_ge(set_dve, setup(nc.vector.reciprocal(s[:, 0, :], s[:, 0, :])))
                    dve.wait_ge(set_dve, setup(nc.vector.tensor_tensor(s[:, 0, :], s[:, 0, :], par[:, 0, :], ALU.mult)))
                    dve.wait_ge(set_dve, setup(nc.vector.tensor_tensor(s[:, 1, :], s[:, 0, :], par[:, 2, :], ALU.mult)))
                    dve.wait_ge(set_dve, setup(nc.vector.tensor_tensor(s[:, 1, :], par[:, 1, :], s[:, 1, :], ALU.subtract)))
                    hot(3 + n)
                for o, w, n in ((q_aug, q_w, 0), (k_aug, k_w, H)):
                    setup(nc.vector.tensor_tensor(o[:, :, 0:C], w[:], s_qk[:, 0, n:n + H].unsqueeze(2).to_broadcast([KD, H, C]), ALU.mult))
                    setup(nc.vector.tensor_copy(o[:, :, C], s_qk[:, 1, n:n + H]))
                dve.wait_ge(set_dve, done[0])
                setup(nc.vector.tensor_scalar(q_aug[:], q_aug[:], -(KD ** -0.5), None, ALU.mult))
                hot(5)
                setup(nc.vector.tensor_tensor(v_aug[0:C, :, 0:VD], v_w[:].rearrange("c (h e) -> c h e", h=H),
                                              s_v[0:C, 0, 0:DH].rearrange("c (h e) -> c h e", h=H), ALU.mult))
                setup(nc.vector.tensor_copy(v_aug[C:CA, :, 0:VD], s_v[C:CA, 1, 0:DH].rearrange("c (h e) -> c h e", h=H)))
                setup(nc.vector.memset(v_aug[0:C, :, VD:VD + 1], 0.0))
                setup(nc.vector.memset(v_aug[C:CA, :, VD:VD + 1], 1.0))
                setup(nc.vector.tensor_tensor(proj[:], proj[:], s_v[:, 0, DH:DH + D].unsqueeze(1).to_broadcast([128, DH // 128, D]), ALU.mult))
                dve.wait_ge(set_dve, done[0])
                setup(nc.vector.tensor_scalar(proj[:], proj[:], 1.0 / 6.0, None, ALU.mult))
                setup(nc.vector.memset(three[:], 3.0))
                assert done[0] == SETUP_STEPS
                hot(6)
                for n in range(3):
                    dve.wait_ge(mat_ready, n + 1)
                    nc.vector.tensor_copy(qk_mat[:, 4 * n:4 * n + 4, :], m_bank[n][0:CA, 0:4 * CA].rearrange("p (h c) -> p h c", h=4)).then_inc(mat_copied, 1)

                def add_bias(k, kp, first=False, chunks=range(CH)):
                    if not first and 0 in chunks:
                        dve.wait_ge(t_ready, 3 * k - 3)
                    for c in chunks:
                        m = chunk_rows(c)
                        if c % 2 == 0:
                            dve.wait_ge(s_ready, 3 * k + c // 2 + 1)
                            dve.sem_inc(dve_waited, 1)
                        ins = nc.vector.tensor_tensor_reduce(
                            out=probs[0:m, kp, c, :], in0=s_bank[c // 2][0:m, (c % 2) * N:(c % 2 + 1) * N],
                            in1=bias_neg[0:m, c, :], scale=1.0, scalar=3.0e38, op0=ALU.add, op1=ALU.min,
                            accum_out=neg_max[0:m, kp, c:c + 1])
                        ins.then_inc(ttr_done, 1)

                def copy_pt(k, kk, t):
                    if True:
                        w = chunk_cols(t)
                        dve.wait_ge(t_ready, 3 * k + t + 1)
                        nc.vector.tensor_copy(p_t[:, :, 2 * CR * t:2 * CR * t + w],
                                              t_bank[(3 * kk + t) % 2][0:HALF, 0:4 * CR].rearrange("p (s r) -> p s r", s=2)[:, :, 0:w]).then_inc(pt_copied, 1)

                def copy_g(i, g):
                    if True:
                        dve.wait_ge(g_ready, 3 * i + g + 1)
                        nc.vector.tensor_copy(g_t[:, :, 4 * g * NQ:4 * (g + 1) * NQ].rearrange("p b (h q) -> p h b q", h=4),
                                              m_bank[g][0:CA, 0:4 * T2].rearrange("p (h b q) -> p h b q", h=4, b=2)).then_inc(g_copied, 1)

                def take_o(i, first=False):
                    for a in range(2):
                        o = m_bank[a][0:T2, 0:6 * (VD + 1)].rearrange("p (h e) -> p h e", h=6)
                        dve.wait_ge(o_ready, 2 * i + a + 1)
                        nc.vector.reciprocal(o_rec[:, a, :], o[:, :, VD]).then_inc(o_rec_done, 1)
                        dve.wait_ge(o_rec_done, 2 * i + a + 1)
                        if a == 0 and not first:
                            dve.wait_ge(a_ready, i)
                        nc.vector.tensor_tensor(o_sb[:, a * 6 * VD:(a + 1) * 6 * VD].rearrange("p (h e) -> p h e", h=6),
                                                o[:, :, 0:VD], o_rec[:, a, :].unsqueeze(2).to_broadcast([T2, 6, VD]), ALU.mult).then_inc(o_read, 1)

                def take_h(i):
                    dve.wait_ge(h_ready, i + 1)
                    nc.vector.tensor_tensor(row_of_h(i), m_bank[2][0:T2, 0:D], s_v[0:T2, 1, DH:DH + D], ALU.add).then_inc(h_copied, 1)

                def hard_swish(i, first=False):
                    dve.wait_ge(u_ready, i + 1)
                    if not first:
                        dve.wait_ge(at_ready, 2 * i)
                    nc.vector.scalar_tensor_tensor(out=o_a[:], in0=o_u[:], scalar=6.0, in1=o_sb[:], op0=ALU.min, op1=ALU.mult).then_inc(a_ready, 1)

                def body(i, first=False, second=False, last=False):
                    add_bias(2 * i + 1, 1, first=first)
                    copy_pt(2 * i, 0, 0)
                    copy_pt(2 * i, 0, 1)
                    if not last:
                        copy_g(i + 1, 0)
                    copy_pt(2 * i, 0, 2)
                    if not last:
                        copy_g(i + 1, 1)
                        copy_g(i + 1, 2)
                    for t in range(2):
                        copy_pt(2 * i + 1, 1, t)
                    if not last:
                        add_bias(2 * i + 2, 0, chunks=range(0, 2))
                    copy_pt(2 * i + 1, 1, 2)
                    if not last:
                        add_bias(2 * i + 2, 0, chunks=range(2, CH))
                    if not first:
                        hard_swish(i - 1, first=second)
                    take_o(i, first=first)
                    if not first:
                        take_h(i - 1)

                for g in range(3):
                    copy_g(0, g)
                dve.wait_ge(bias_back, 96)
                for part in range(2):
                    nc.vector.tensor_tensor(bias_neg[:, 0:CH - 1], bias_neg[:, 0:CH - 1], bias_low[:, part, 0:CH - 1], ALU.add).then_inc(parts_done, 1)
                    m = chunk_rows(CH - 1)
                    nc.vector.tensor_tensor(bias_neg[0:m, CH - 1], bias_neg[0:m, CH - 1], bias_low[0:m, part, CH - 1], ALU.add).then_inc(parts_done, 1)
                    dve.wait_ge(parts_done, 6 + 2 * (part + 1))
                add_bias(0, 0, first=True)
                body(0, first=True)
                body(1, second=True)
                with dve.Fori(2, NP - 1) as i:
                    body(i)
                body(NP - 1, last=True)
                hard_swish(NP - 1)
                take_h(NP - 1)

                dve.wait_ge(wts2_in, WTS2)

                def moments(g, base):
                    for u in range(TG):
                        nc.vector.bn_stats(stats[:, u, :], h_all[:, ds(TG * g + u, 1), :].rearrange("p a c -> p (a c)")).then_inc(step, 1)
                    dve.wait_ge(step, base + TG)
                    dve.sem_inc(dve_waited, 1)
                    for u in range(TG):
                        nc.vector.bn_aggr(mean_var[:, u, :], stats[:, u, :]).then_inc(step, 1)
                    dve.wait_ge(step, base + 2 * TG)
                    return nc.vector.tensor_scalar_add(rstd[:], mean_var[:, :, 1], EPS)

                def normalise(g, base):
                    nc.vector.reciprocal(rstd[:], rstd[:]).then_inc(step, 1)
                    dve.wait_ge(step, base + 1)
                    for u in range(TG):
                        ins = nc.vector.tensor_scalar(ln[:, u, :], h_all[:, ds(TG * g + u, 1), :].rearrange("p a c -> p (a c)"),
                                                      mean_var[:, u, 0:1], rstd[:, u:u + 1], ALU.subtract, ALU.mult)
                    return ins

                LN1 = 2 * TG + 1
                GN1 = 4

                def group_norm_a(g, base, first=False):
                    dve.wait_ge(ret_copied, g + 1)
                    nc.vector.tensor_reduce(gmean[:], ret[:], AX.X, ALU.add).then_inc(step, 1)
                    dve.wait_ge(step, base + 1)
                    nc.vector.tensor_scalar(gmean[:], gmean[:], 1.0 / RD, None, ALU.mult).then_inc(step, 1)
                    dve.wait_ge(step, base + 2)
                    nc.vector.tensor_tensor(ret_c[:], ret[:], gmean[:].unsqueeze(2).to_broadcast([T2, TG * RH, RD]), ALU.subtract).then_inc(c_ready, 1)

                def group_norm_b(g, base, first=False):
                    dve.wait_ge(sq_ready, g + 1)
                    nc.vector.tensor_reduce(gstd[:], ret_sq[:], AX.X, ALU.add).then_inc(step, 1)
                    dve.wait_ge(step, base + 1)
                    nc.vector.tensor_scalar(gstd[:], gstd[:], 1.0 / RD, EPS, ALU.mult, ALU.add).then_inc(gvar_ready, 1)
                    dve.wait_ge(gstd_ready, g + 1)
                    nc.vector.reciprocal(gstd[:], gstd[:]).then_inc(step, 1)
                    dve.wait_ge(step, base + 2)
                    if not first:
                        dve.wait_ge(z_done, g)
                    nc.vector.tensor_tensor(ret_n[:].rearrange("p u (h r) -> p (u h) r", h=RH), ret_c[:],
                                            gstd[:].unsqueeze(2).to_broadcast([T2, TG * RH, RD]), ALU.mult).then_inc(gn_ready, 1)

                def retention(g, base, first=False, last=False):
                    def spread_q(u):
                        k = TG * g + u
                        if u == 0:
                            dve.wait_ge(q_ready, g + 1)
                        if not (first and u < 2):
                            dve.wait_ge(sb_ready, k - 1)
                        nc.vector.tensor_tensor(q_heads[u % 2][:], bank[1][:, u * T2:(u + 1) * T2].unsqueeze(1).to_broadcast([D, RH, T2]),
                                                head_mask[:].unsqueeze(2).to_broadcast([D, RH, T2]), ALU.mult).then_inc(qm_made, 1)

                    def decay_a(u):
                        k = TG * g + u
                        dve.wait_ge(sa_ready, k + 1)
                        if not (first and u < 2):
                            dve.wait_ge(pv_ready, k - 1)
                        nc.vector.tensor_tensor(sc[u % 2][:, 0:RH // 2, :], bank[5][0:T2, 0:GT].rearrange("p (h t) -> p h t", h=TG),
                                                decay[:, 0:RH // 2, :], ALU.mult).then_inc(sa_done, 1)

                    spread_q(0)
                    for u in range(TG):
                        if u < TG - 1:
                            spread_q(u + 1)
                        decay_a(u)
                    n = base
                    if not last:
                        moments(g + 1, n).then_inc(var_ready, 1)
                        n = n + 2 * TG
                    group_norm_a(g, n)
                    n = n + 2
                    if not last:
                        dve.wait_ge(std_ready, g + 2)
                        dve.wait_ge(lt_ready, g + 1)
                        normalise(g + 1, n).then_inc(ln_ready, 1)
                        n = n + 1
                    group_norm_b(g, n, first)

                moments(0, 0).then_inc(var_ready, 1)
                dve.wait_ge(std_ready, 1)
                normalise(0, 2 * TG).then_inc(ln_ready, 1)
                retention(0, LN1, first=True)
                with dve.Fori(1, NG - 1) as g:
                    retention(g, (LN1 + GN1) * g + LN1)
                retention(NG - 1, (LN1 + GN1) * NG - GN1, last=True)
                n_steps = (LN1 + GN1) * NG

                with dve.Fori(0, NG) as g:
                    dve.wait_ge(wo_ready, g + 1)
                    hg = h_all[:, ds(TG * g, TG), :]
                    nc.vector.tensor_tensor(hg, bank[1][0:T2, :].rearrange("p (u c) -> p u c", u=TG), hg, ALU.add).then_inc(h2_done, 1)

                dve.wait_ge(h2_done, NG)
                def second_norm(g, first=False):
                    moments(g, n_steps + LN1 * g).then_inc(l_var, 1)
                    dve.wait_ge(l_std, g + 1)
                    if not first:
                        dve.wait_ge(rows_copied, g)
                    normalise(g, n_steps + LN1 * g + 2 * TG).then_inc(hn_ready, 1)
                    dve.wait_ge(lg_ready, g + 1)
                    nc.vector.tensor_copy(logit[:, ds(TG * g, TG), :], bank[3][0:T2, 0:TG * E].rearrange("p (u e) -> p u e", u=TG)).then_inc(lg_done, 1)

                second_norm(0, first=True)
                with dve.Fori(1, NG) as g:
                    second_norm(g)
                n_steps += LN1 * NG
                m = [n_steps]

                def then(ins):
                    m[0] += 1
                    ins.then_inc(step, 1)
                    dve.wait_ge(step, m[0])

                dve.wait_ge(lg_done, NG)
                then(nc.vector.tensor_reduce(lmax[:], logit[:], AX.X, ALU.max))
                nc.vector.tensor_tensor(logit[:], logit[:], lmax[:].unsqueeze(2).to_broadcast([T2, NP, E]), ALU.subtract).then_inc(lx_ready, 1)
                dve.wait_ge(le_ready, 1)
                then(nc.vector.tensor_reduce(lsum[:], logit[:], AX.X, ALU.add))
                then(nc.vector.reciprocal(lsum[:], lsum[:]))
                dve.wait_ge(rows_copied, NG)
                nc.vector.tensor_tensor(rows[:, :, D:ROW], logit[:], lsum[:].unsqueeze(2).to_broadcast([T2, NP, E]), ALU.mult).then_inc(pr_ready, 1)
                dve.wait_ge(pr_ready, 1)
                nc.vector.tensor_copy(prob_j[:].rearrange("p j (e c) -> p c j e", e=E),
                                      rows[:, :, D:ROW].rearrange("p (c j) e -> p c j e", j=TG)).then_inc(pr_ready, 1)
                nc.vector.memset(thr[:], 0)
                nc.vector.memset(bit[:], 1 << 30)
                dve.wait_ge(xp_ready, 1)
                then(nc.vector.tensor_copy(xp[:], bank[4][:, 0:GT]))
                then(nc.vector.tensor_tensor(h_all[:], h_all[:], sb2[:].unsqueeze(1).to_broadcast([T2, NP, D]), ALU.add))
                n_steps = m[0]

                SEARCH = 5

                def search(q, base):
                    nc.vector.tensor_tensor(cand[:], thr[:], bit[:], ALU.bitwise_or).then_inc(step, 1)
                    dve.wait_ge(step, base + 1)
                    nc.vector.tensor_scalar(above[:], xp[:], cand[:].bitcast(F32), None, ALU.is_ge, ALU.add, accum_out=cnt[:]).then_inc(cnt_ready, 1)
                    dve.wait_ge(tot_ready, q + 1)
                    nc.vector.tensor_scalar(mask[:], bank[6][:, 0:1], CAP - 0.5, -1.0, ALU.is_ge, ALU.mult).then_inc(step, 1)
                    dve.wait_ge(step, base + 2)
                    nc.vector.tensor_tensor(cand[:], mask[:], bit[:], ALU.bitwise_and).then_inc(step, 1)
                    nc.vector.tensor_scalar(bit[:], bit[:], 1, None, ALU.logical_shift_right).then_inc(step, 1)
                    dve.wait_ge(step, base + 4)
                    nc.vector.tensor_tensor(thr[:], thr[:], cand[:], ALU.bitwise_or).then_inc(step, 1)
                    dve.wait_ge(step, base + 5)

                def shared(g, p, base, first=False):
                    for q in range(4):
                        search(4 * g + q, base + SEARCH * q)
                    dve.wait_ge(shy_ready, g + 1)
                    if not first:
                        dve.wait_ge(out_sent[p], 16 * ((g - p) // 2) if isinstance(g, int) else 8 * (g - p))
                    nc.vector.tensor_tensor(out_g[p][:], bank[5 + 2 * p][0:T2, :].rearrange("p (u c) -> p u c", u=TG),
                                            h_all[:, ds(TG * g, TG), :], ALU.add).then_inc(shy_taken, 1)

                shared(0, 0, n_steps, True)
                shared(1, 1, n_steps + 4 * SEARCH, True)
                with dve.Fori(1, NG // 2) as j:
                    for p in range(2):
                        shared(2 * j + p, p, n_steps + 4 * SEARCH * (2 * j + p))
                m[0] += 4 * SEARCH * NG

                t_f = thr[:].bitcast(F32)
                nc.vector.tensor_scalar(above[:], xp[:], t_f, None, ALU.is_gt, ALU.add, accum_out=col[:, 0:1])
                then(nc.vector.tensor_scalar(equal[:], xp[:], t_f, None, ALU.is_equal))
                then(nc.vector.tensor_tensor_scan(scan_e[:], equal[:], equal[:], 0.0, ALU.add, ALU.bypass))
                nc.vector.tensor_copy(col[:, 1:2], scan_e[:, GT - 1:GT]).then_inc(col_ready, 1)
                dve.wait_ge(off_ready, 1)
                then(nc.vector.tensor_scalar(col[:, 2:3], bank[6][:, 8:9], -1.0, float(CAP), ALU.mult, ALU.add))
                then(nc.vector.tensor_tensor(col[:, 2:3], col[:, 2:3], bank[6][:, 16:17], ALU.subtract))
                then(nc.vector.scalar_tensor_tensor(out=sel[:], in0=scan_e[:], scalar=col[:, 2:3], in1=equal[:], op0=ALU.is_le, op1=ALU.mult))
                then(nc.vector.tensor_tensor(sel[:], sel[:], above[:], ALU.add))
                then(nc.vector.tensor_tensor_scan(scan_s[:], sel[:], sel[:], 0.0, ALU.add, ALU.bypass))
                nc.vector.tensor_copy(col[:, 3:4], scan_s[:, GT - 1:GT]).then_inc(col_ready, 1)
                dve.wait_ge(off_ready, 2)
                then(nc.vector.tensor_scalar(col[:, 2:3], bank[6][:, 24:25], -256.0, None, ALU.add))
                nc.vector.scalar_tensor_tensor(out=scan_e[:], in0=scan_s[:], scalar=col[:, 2:3], in1=sel[:], op0=ALU.add, op1=ALU.mult).then_inc(slot_ready, 1)
                dve.wait_ge(slot_taken, 1)
                then(nc.vector.tensor_scalar(slot[:], bank[4][0:T2, :].rearrange("p (j m) -> p j m", j=TG), 255.0, None, ALU.add))
                nc.vector.tensor_scalar(slot_a[:], slot[:], 4, None, ALU.logical_shift_right)
                then(nc.vector.tensor_scalar(slot_b[:], slot[:], SB_ - 1, None, ALU.bitwise_and))
                for j in range(TG):
                    for o, a, w in ((hot_a, slot_a, SA), (hot_b, slot_b, SB_)):
                        nc.vector.tensor_tensor(o[:, j], a[:, j, :].rearrange("p (e c) -> p c e", e=E).unsqueeze(3).to_broadcast([T2, EC, E, w]),
                                                iota_slot[:, 0:w].unsqueeze(1).unsqueeze(1).to_broadcast([T2, EC, E, w]), ALU.is_equal).then_inc(step, 1)
                m[0] += 2 * TG
                dve.wait_ge(step, m[0])
                for j in range(TG):
                    flat = hot_a[:, j].rearrange("p c e a -> p c (e a)")
                    nc.vector.tensor_scalar(hot_ap[:, j].rearrange("p c e a -> p c (e a)"), flat, tok_col[:, 0:1], None, ALU.mult)
                    nc.vector.tensor_tensor(hot_at[:, j].rearrange("p c e a -> p c (e a)"), flat,
                                            tile_num[:, j, :].unsqueeze(2).to_broadcast([T2, EC, E * SA]), ALU.mult).then_inc(hot_ready, 1)
                dve.wait_ge(list_ready, 1)
                lb = bank[5][0:EG * SA, :].rearrange("p (g k m) -> p g k m", g=2, k=2)
                lt = list_t[:].rearrange("p g e b -> p g (e b)")
                then(nc.vector.tensor_scalar(lt, lb[:, :, 1, :], float(T2), None, ALU.mult))
                then(nc.vector.tensor_tensor(lt, lb[:, :, 0, :], lt, ALU.add))
                then(nc.vector.tensor_tensor(list_t[:], list_t[:], diag[:].unsqueeze(1).to_broadcast([EG * SA, 2, EG, SB_]), ALU.mult))
                nc.vector.tensor_reduce(list_s[:], list_t[:].rearrange("p g e b -> p g b e"), AX.X, ALU.add).then_inc(list_done, 1)
                dve.wait_ge(lr_ready, 1)
                nc.vector.tensor_copy(idx_all[:], bank[6][0:TH, 0:2 * E]).then_inc(lr_done, 1)

                def take_y(e, p, first=False):
                    dve.wait_ge(ey_ready, e + 1)
                    dve.wait_ge(ew_in[p % 2], 64 * (e // 2 + 1) if isinstance(e, int) else 32 * (e - p % 2) + 64)
                    if not first:
                        dve.wait_ge(scattered, 32 * (e - RING + 1))
                    for s in range(2):
                        nc.vector.tensor_tensor(y[p][s][:], bank[3][0:TH, s * D:(s + 1) * D], b2[p % 2][:], ALU.add).then_inc(ey_taken, 1)
                    for s in range(2):
                        dve.wait_ge(ey_taken, 2 * e + s + 1)
                        nc.vector.tensor_scalar(y[p][s][:], y[p][s][:], tok[p][s][:, ds(D + e, 1)], None, ALU.mult).then_inc(y_done, 1)

                for e in range(RING):
                    take_y(e, e, first=True)
                with dve.Fori(1, E // RING) as j:
                    for p in range(RING):
                        take_y(RING * j + p, p)

            @block.tensor
            def _(pe):
                pe.wait_ge(parts_done, 6)
                for k in range(7):
                    pe.wait_ge(hot_made, k + 1)
                    for n in range(4):
                        if 4 * k + n >= 2:
                            pe.wait_ge(bank_read, 4 * k + n - 1)
                        for s in range(2):
                            ins = nc.tensor.matmul(s_bank[n % 2][0:96, 0:343], bias_parts[:, s].rearrange("p a b -> p (a b)"),
                                                   onehot[k % 2][:, s, n * 343:(n + 1) * 343], start=(s == 0), stop=(s == 1))
                        ins.then_inc(bias_mm, 1)
                pe.wait_ge(set_dve, SETUP_STEPS)
                for h in range(H):
                    ins = nc.tensor.matmul(m_bank[h // 4][0:CA, (h % 4) * CA:(h % 4 + 1) * CA], q_aug[:, h, :], k_aug[:, h, :], start=True, stop=True)
                    if h % 4 == 3:
                        ins.then_inc(mat_ready, 1)

                def g_product(i, g, p, first=False):
                    if g == 0:
                        pe.wait_ge(x_in[p], 32 * (i // 2 + 1) if isinstance(i, int) else 16 * (i - p) + 32)
                    if first:
                        pe.wait_ge(mat_copied, 3)
                    elif isinstance(i, int) and i == 1:
                        pe.wait_ge(g_copied, g + 1)
                    elif g < 2:
                        pe.wait_ge(o_read, 2 * i - 3 + g)
                    elif not (isinstance(i, int) and i == 2):
                        pe.wait_ge(h_copied, i - 2)
                    xs = x_t[p][:, :].rearrange("c (b y x) -> c b y x", b=2, y=RES)[:, :, ::STRIDE, ::STRIDE]
                    for h in range(4):
                        ins = nc.tensor.matmul(m_bank[g][0:CA, h * T2:(h + 1) * T2].rearrange("c (b y x) -> c b y x", b=2, y=7),
                                               qk_mat[:, 4 * g + h, :], xs, start=True, stop=True)
                    ins.then_inc(g_ready, 1)

                def s_product(k, b, p, first=False, chunks=range(CH)):
                    for c in chunks:
                        m = chunk_rows(c)
                        if c % 2 == 0 and not first:
                            pe.wait_ge(ttr_done, CH * (k - 1) + min(c + 2, CH))
                        ins = nc.tensor.matmul(s_bank[c // 2][0:m, (c % 2) * N:(c % 2 + 1) * N], g_t[:, b, c * CR:c * CR + m],
                                               x_t[p][:, b * N:(b + 1) * N], start=True, stop=True)
                        if c % 2 == 1 or c == CH - 1:
                            ins.then_inc(s_ready, 1)

                def turn_probs(k, kp, f0, first=False, groups=range(3)):
                    for t in groups:
                        pe.wait_ge(exp_done, CH * k + min(2 * t + 2, CH))
                        if not (first and t < 2):
                            pe.wait_ge(pt_copied, 3 * k + t - 1)
                        for c in range(2 * t, min(2 * t + 2, CH)):
                            m = chunk_rows(c)
                            for s in range(2):
                                o = s * 2 * CR + (c - 2 * t) * CR
                                ins = nc.tensor.transpose(t_bank[(f0 + t) % 2][0:HALF, o:o + m], probs[0:m, kp, c, s * HALF:(s + 1) * HALF], ident[0:m, 0:m])
                        ins.then_inc(t_ready, 1)

                def px_product(k, b, p, f0, waits):
                    for a in range(2):
                        pe.wait_ge(pt_copied, 3 * k + 2 + a)
                        waits(a)
                        for s in range(2):
                            ins = nc.tensor.matmul(m_bank[(f0 + a) % 3][0:CA, 0:6 * NQ], x_n[p][:, 2 * b + s, :], p_t[:, s, a * 6 * NQ:(a + 1) * 6 * NQ],
                                                   start=(s == 0), stop=(s == 1))
                        ins.then_inc(px_ready, 1)

                def turn_a(i):
                    for a in range(2):
                        if a == 0:
                            pe.wait_ge(a_ready, i + 1)
                        for c in range(3):
                            ins = nc.tensor.transpose(m_bank[1 + a][:, c * T2:(c + 1) * T2], o_a[:, (3 * a + c) * 128:(3 * a + c + 1) * 128], ident[0:T2, 0:T2])
                        ins.then_inc(at_ready, 1)

                def project(i):
                    pe.wait_ge(at_copied, 2 * i + 2)
                    for c in range(DH // 128):
                        ins = nc.tensor.matmul(m_bank[2][0:T2, 0:D], a_t[:, c, :], proj[:, c, :], start=(c == 0), stop=(c == DH // 128 - 1))
                    ins.then_inc(h_ready, 1)

                def o_product(i, first):
                    for a in range(2):
                        pe.wait_ge(px_copied, 4 * i + 4)
                        if a == 1 and not first:
                            pe.wait_ge(at_copied, 2 * i - 1)
                        for h in range(6):
                            ins = nc.tensor.matmul(m_bank[a][0:T2, h * (VD + 1):(h + 1) * (VD + 1)], px_t[:, 6 * a + h, :], v_aug[:, 6 * a + h, :],
                                                   start=True, stop=True)
                        ins.then_inc(o_ready, 1)

                def body(i, p, first=False, last=False):
                    s_product(2 * i + 1, 1, p)
                    turn_probs(2 * i, 0, 0, first=first, groups=range(0, 2))
                    if not last:
                        g_product(i + 1, 0, 1 - p)
                    turn_probs(2 * i, 0, 0, groups=range(2, 3))
                    if not last:
                        g_product(i + 1, 1, 1 - p)
                        g_product(i + 1, 2, 1 - p)

                    def before_px0(a):
                        if not last:
                            pe.wait_ge(g_copied, 3 * (i + 1) + 1 + a)
                        else:
                            pe.wait_ge(o_read, 2 * i - 1 + a)
                    px_product(2 * i, 0, p, 0, before_px0)
                    turn_probs(2 * i + 1, 1, 3, groups=range(0, 2))
                    if not last:
                        pe.wait_ge(g_copied, 3 * (i + 1) + 3)
                        s_product(2 * i + 2, 0, 1 - p, chunks=range(0, 2))
                    turn_probs(2 * i + 1, 1, 3, groups=range(2, 3))
                    if not last:
                        s_product(2 * i + 2, 0, 1 - p, chunks=range(2, CH))

                    def before_px1(a):
                        if a == 1:
                            pe.wait_ge(px_copied, 4 * i + 1)
                        elif last:
                            pe.wait_ge(h_copied, i - 1)
                    px_product(2 * i + 1, 1, p, 2, before_px1)
                    if not first:
                        pe.wait_ge(px_copied, 4 * i + 3)
                        turn_a(i - 1)
                    o_product(i, first)
                    if not first:
                        project(i - 1)

                pe.wait_ge(ones_set, 4)
                for g in range(3):
                    g_product(0, g, 0, first=True)
                pe.wait_ge(g_copied, 3)
                pe.wait_ge(bank_read, 28)
                s_product(0, 0, 0, first=True)
                body(0, 0, first=True)
                body(1, 1)
                with pe.Fori(1, NP // 2 - 1) as j:
                    body(2 * j, 0)
                    body(2 * j + 1, 1)
                body(NP - 2, 0)
                body(NP - 1, 1, last=True)
                pe.wait_ge(o_read, 2 * NP)
                pe.wait_ge(h_copied, NP - 1)
                turn_a(NP - 1)
                project(NP - 1)

                pe.wait_ge(wts2_in, WTS2)
                pe.wait_ge(h_copied, NP)

                def retention(g, first=False):
                    pe.wait_ge(ln_ready, g + 1)
                    for u in range(TG):
                        ins = nc.tensor.transpose(bank[0][:, u * T2:(u + 1) * T2], ln[:, u, :], ident[0:T2, 0:T2])
                    ins.then_inc(lt_ready, 1)
                    pe.wait_ge(lt_copied, g + 1)
                    if not first:
                        pe.wait_ge(qm_made, TG * g)
                    nc.tensor.matmul(bank[1][:, 0:GT], w_q[:], ln_t[:], start=True, stop=True).then_inc(q_ready, 1)
                    nc.tensor.matmul(bank[2][:, 0:GT], w_k[:], ln_t[:], start=True, stop=True).then_inc(k_ready, 1)
                    for a in range(2):
                        if not first:
                            pe.wait_ge(vg_copied, 2 * g + a - 1)
                        for u in range(2):
                            ins = nc.tensor.matmul(bank[3 + a][0:T2, u * 2 * D:(u + 1) * 2 * D], ln_t[:, (2 * a + u) * T2:(2 * a + u + 1) * T2], w_vg[:],
                                                   start=True, stop=True)
                        ins.then_inc(vg_ready, 1)
                    pe.wait_ge(k_copied, g + 1)

                    def scores(u):
                        k = TG * g + u
                        pe.wait_ge(qm_made, k + 1)
                        for a, (taken, ready) in enumerate(((sa_done, sa_ready), (sb_copied, sb_ready))):
                            if not (first and u == 0):
                                pe.wait_ge(taken, k)
                            nc.tensor.matmul(bank[5 + a][0:T2, 0:GT], k_t[:, u * T2:(u + 1) * T2], q_heads[u % 2][:, 4 * a:4 * a + 4, :],
                                             start=True, stop=True).then_inc(ready, 1)

                    def values(u):
                        k = TG * g + u
                        pe.wait_ge(sa_done, k + 1)
                        pe.wait_ge(sb_done, k + 1)
                        if u == 0:
                            pe.wait_ge(vg_copied, 2 * g + 2)
                            if not first:
                                pe.wait_ge(ret_copied, g)
                        for h in range(RH):
                            ins = nc.tensor.matmul(bank[7][0:T2, u * D + h * RD:u * D + (h + 1) * RD], sc[u % 2][:, h, :],
                                                   v_sb[:, u, h * RD:(h + 1) * RD], start=True, stop=True)
                        ins.then_inc(pv_ready, 1)

                    scores(0)
                    for u in range(TG):
                        if u < TG - 1:
                            scores(u + 1)
                        values(u)

                retention(0, first=True)
                with pe.Fori(1, NG) as g:
                    retention(g)

                def out_projection(g, first=False):
                    pe.wait_ge(zs_ready, g + 1)
                    if not first:
                        pe.wait_ge(zt_copied, g)
                    for u in range(TG):
                        ins = nc.tensor.transpose(bank[0][:, u * T2:(u + 1) * T2], z[:, u, :], ident[0:T2, 0:T2])
                    ins.then_inc(zt_ready, 1)
                    pe.wait_ge(zt_copied, g + 1)
                    if not first:
                        pe.wait_ge(h2_done, g)
                    for u in range(TG):
                        ins = nc.tensor.matmul(bank[1][0:T2, u * D:(u + 1) * D], z_t[:, u * T2:(u + 1) * T2], w_o[:], start=True, stop=True)
                    ins.then_inc(wo_ready, 1)

                out_projection(0, first=True)
                with pe.Fori(1, NG) as g:
                    out_projection(g)

                def gate(g, first=False):
                    pe.wait_ge(hn_ready, g + 1)
                    for u in range(TG):
                        ins = nc.tensor.transpose(bank[2][:, u * T2:(u + 1) * T2], ln[:, u, :], ident[0:T2, 0:T2])
                    ins.then_inc(hnt_ready, 1)
                    pe.wait_ge(hnt_copied, g + 1)
                    if not first:
                        pe.wait_ge(lg_done, g)
                    for u in range(TG):
                        ins = nc.tensor.matmul(bank[3][0:T2, u * E:(u + 1) * E], hn_g[:, u * T2:(u + 1) * T2], gate_w[:], start=True, stop=True)
                    ins.then_inc(lg_ready, 1)

                gate(0, first=True)
                with pe.Fori(1, NG) as g:
                    gate(g)

                pe.wait_ge(pr_ready, 2)
                for j in range(TG):
                    ins = nc.tensor.transpose(bank[4][:, j * T2:(j + 1) * T2],
                                              prob_j[:, j, :], ident[0:T2, 0:T2])
                ins.then_inc(xp_ready, 1)

                def shared(g, p, first=False):
                    def total(q):
                        pe.wait_ge(cnt_ready, 4 * g + q + 1)
                        nc.tensor.matmul(bank[6][:, 0:1], same_expert[:], cnt[:], start=True, stop=True).then_inc(tot_ready, 1)

                    for c in range(HC):
                        if not first:
                            pe.wait_ge(sh_gelu, HC * (g - 1) + c + 1)
                        nc.tensor.matmul(bank[c][:, 0:GT], sw1[:, c * 128:(c + 1) * 128], hn_t[:, ds(GT * g, GT)], start=True, stop=True).then_inc(sh_ready, 1)
                        if c % 2:
                            total(c // 2)
                    pe.wait_ge(sh_gelu, HC * g + HC)
                    if not first:
                        pe.wait_ge(shy_taken, g)
                    for u in range(TG):
                        for c in range(HC):
                            ins = nc.tensor.matmul(bank[5 + 2 * p][0:T2, u * D:(u + 1) * D], hid[p][:, c, u * T2:(u + 1) * T2], sw2[:, c, :],
                                                   start=(c == 0), stop=(c == HC - 1))
                        if u == 1:
                            total(2)
                    ins.then_inc(shy_ready, 1)
                    total(3)

                pe.wait_ge(xp_ready, 1)
                shared(0, 0, first=True)
                shared(1, 1)
                with pe.Fori(1, NG // 2) as j:
                    for p in range(2):
                        shared(2 * j + p, p)

                pe.wait_ge(col_ready, 1)
                nc.tensor.matmul(bank[6][:, 8:9], same_expert[:], col[:, 0:1], start=True, stop=True)
                nc.tensor.matmul(bank[6][:, 16:17], before[:], col[:, 1:2], start=True, stop=True).then_inc(off_ready, 1)
                pe.wait_ge(col_ready, 2)
                nc.tensor.matmul(bank[6][:, 24:25], before[:], col[:, 3:4], start=True, stop=True).then_inc(off_ready, 1)
                pe.wait_ge(slot_ready, 1)
                for j in range(TG):
                    ins = nc.tensor.transpose(bank[4][0:T2, j * 128:(j + 1) * 128], scan_e[:, j * T2:(j + 1) * T2], ident[:])
                ins.then_inc(slot_taken, 1)
                pe.wait_ge(hot_ready, TG)
                pe.wait_ge(shy_taken, NG)
                for g in range(2):
                    for k, hot in enumerate((hot_ap, hot_at)):
                        for j in range(TG):
                            for c in range(EC):
                                ins = nc.tensor.matmul(bank[5][0:EG * SA, (2 * g + k) * 128:(2 * g + k + 1) * 128],
                                                       hot[:, j, c, g * EG:(g + 1) * EG, :].rearrange("p e a -> p (e a)"),
                                                       hot_b[:, j, c, g * EG:(g + 1) * EG, :].rearrange("p e b -> p (e b)"),
                                                       start=(j == 0 and c == 0), stop=(j == TG - 1 and c == EC - 1))
                ins.then_inc(list_ready, 1)
                pe.wait_ge(list_in, 32)
                nc.tensor.transpose(bank[6][0:TH, 0:2 * E], list_r[:], ident[0:2 * E, 0:2 * E]).then_inc(lr_ready, 1)

                def turn_tok(e, p):
                    pe.wait_ge(tok_in[p], 32 * (e // RING + 1) if isinstance(e, int) else (32 // RING) * (e - p) + 32)
                    for s in range(2):
                        ins = nc.tensor.transpose(bank[0][:, s * TH:(s + 1) * TH], tok[p][s][:, 0:D], ident[0:TH, 0:TH])
                    ins.then_inc(tt_ready, 1)

                def hidden(e, p, first=False):
                    pe.wait_ge(ew_in[p], 64 * ((e - p) // 2 + 1) if isinstance(e, int) else 32 * (e - p) + 64)
                    pe.wait_ge(tt_copied, e + 1)
                    for c in range(HC):
                        if not first and c % 2 == 0:
                            pe.wait_ge(eh_gelu, HC * (e - 1) + c + 2)
                        ins = nc.tensor.matmul(bank[1 + c // 2][:, (c % 2) * CAP:(c % 2 + 1) * CAP], w1[p][:, c * 128:(c + 1) * 128], tok_t[p][:],
                                               start=True, stop=True)
                        if c % 2:
                            ins.then_inc(eh_ready, 1)

                def output(e, p, first=False):
                    pe.wait_ge(eh_gelu, HC * e + HC)
                    if not first:
                        pe.wait_ge(ey_taken, 2 * e)
                    for s in range(2):
                        for c in range(HC):
                            ins = nc.tensor.matmul(bank[3][0:TH, s * D:(s + 1) * D], ehid[p][:, c, s * TH:(s + 1) * TH], w2[p][:, c, :],
                                                   start=(c == 0), stop=(c == HC - 1))
                    ins.then_inc(ey_ready, 1)

                turn_tok(0, 0)
                hidden(0, 0, first=True)
                turn_tok(1, 1)
                hidden(1, 1)
                turn_tok(2, 2)
                output(0, 0, first=True)
                hidden(2, 0)
                turn_tok(3, 3)
                output(1, 1)
                with pe.Fori(1, E // RING) as j:
                    for p in range(RING):
                        e = RING * j + p
                        hidden(e - 1, (p - 1) % 2)
                        turn_tok(e, p)
                        output(e - 2, p % 2)
                hidden(E - 1, 1)
                output(E - 2, 0)
                output(E - 1, 1)


WTS2 = 19 * 16
SETUP_STEPS = 22


def chunk_cols(t):
    return sum(chunk_rows(c) for c in range(2 * t, min(2 * t + 2, CH)))


def constants():
    f = np.float32
    t = np.arange(T2)
    diff = (t[None, :] - t[:, None]).astype(f)
    causal = (diff >= 0) & (t[None, :] // NQ == t[:, None] // NQ)
    gammas = 1.0 - np.exp2(-5.0 - np.arange(RH, dtype=f))
    decay = np.where(causal[:, None], np.exp(diff[:, None] * np.log(gammas)[None, :, None]), 0.0) / np.sqrt(f(RD))
    r = np.arange(128)
    same = r[:, None] // EC == r[None, :] // EC
    return {
        "decay": decay.astype(f),
        "head_mask": (np.arange(D)[:, None] // RD == np.arange(RH)[None, :]).astype(f),
        "same_expert": same.astype(f),
        "before": (same & (r[:, None] < r[None, :])).astype(f),
        "iota_slot": np.tile(np.arange(SB_, dtype=f), (T2, 1)),
        "tok_col": np.arange(T2, dtype=f)[:, None],
        "tile_num": np.tile((TG * np.arange(EC)[None, :] + np.arange(TG)[:, None]).astype(f)[None], (T2, 1, 1)),
        "diag": np.repeat((np.arange(EG * SA)[:, None] // SA == np.arange(EG)[None, :]).astype(f)[:, :, None], SB_, 2),
    }


def kernel(**inputs):
    import concourse.bacc as _bacc
    from concourse import mybir as _mybir
    from concourse.bass_utils import run_bass_kernel_spmd as _run

    a = {k: np.asarray(v) for k, v in inputs.items()}
    kv = a["L0_tok_kv_w"].reshape(H, KD + VD, C)

    def per_head(name, lo, hi):
        return a["L0_tok_kv_" + name].reshape(H, KD + VD)[:, lo:hi]

    arrays = {
        "x": a["x"],
        "x_t": a["x"].reshape(B * N, C).T,
        "idx": a["L0_tok_bias_idxs"],
        "bias_cols": a["L0_tok_attention_biases"].T.reshape(2, HALF, H).transpose(1, 0, 2),
        "iota_off": np.arange(NOFF, dtype=np.float32).reshape(2, HALF).T,
        "ident": np.eye(128, dtype=np.float32),
        "q_w": a["L0_tok_q_w"].reshape(H, KD, C).transpose(1, 0, 2),
        "k_w": kv[:, :KD].transpose(1, 0, 2),
        "v_w": kv[:, KD:].transpose(2, 0, 1).reshape(C, DH),
        "proj": a["L0_tok_proj_w"].T.reshape(DH // 128, 128, D).transpose(1, 0, 2),
        "w_q": a["L0_attn_W_Q"], "w_k": a["L0_attn_W_K"], "w_o": a["L0_attn_W_O"],
        "w_vg": np.concatenate([a["L0_attn_W_V"], a["L0_attn_W_G"]], 1),
        "gn_w": a["L0_attn_gn_weight"], "gn_b": a["L0_attn_gn_bias"],
        "gate_w": a["L0_ffn_gate_w"], "sw1": a["L0_ffn_sw1"],
        "sw2": a["L0_ffn_sw2"].reshape(HC, 128, D).transpose(1, 0, 2),
        "sb1": a["L0_ffn_sb1"].reshape(HC, 128).T, "sb2": a["L0_ffn_sb2"],
        "w1": a["L0_ffn_w1"], "w2": a["L0_ffn_w2"].reshape(E, HC, 128, D).transpose(0, 2, 1, 3),
        "b1": a["L0_ffn_b1"].reshape(E, HC, 128).transpose(0, 2, 1), "b2": a["L0_ffn_b2"],
        **constants(),
        "par_qk": np.stack([np.concatenate([a["L0_tok_q_" + n].reshape(H, KD).T, per_head(n, 0, KD).T], 1) for n in "gbmv"], 1),
        "par_v": np.stack([np.concatenate([per_head(n, KD, KD + VD).reshape(-1), a["L0_tok_proj_" + n]]) for n in "gbmv"]),
    }
    nc = _bacc.Bacc("TRN2", target_bir_lowering=False, num_devices=1)
    feed, d = {}, {}
    for name, v in arrays.items():
        v = np.ascontiguousarray(v)
        feed[f"in_{name}_dram"] = v
        d[name] = nc.dram_tensor(f"in_{name}_dram", v.shape, _mybir.dt.from_np(v.dtype), kind="ExternalInput").ap()
    out = nc.dram_tensor("out_dram", (T, D), F32, kind="ExternalOutput").ap()
    build(nc, d, out)
    r = _run(nc, [feed], core_ids=[0])
    return r.results[0]["out_dram"].reshape(B, NQ, D)
```

```python
import math
from contextlib import ExitStack

import numpy as np

import concourse.bass as bass
from concourse import mybir

F32 = mybir.dt.float32
BF16 = mybir.dt.bfloat16
I32 = mybir.dt.int32
ALU = mybir.AluOpType
ACT = mybir.ActivationFunctionType
AX = mybir.AxisListType
ds = bass.ds

B, RES, STRIDE = 64, 14, 2
N = RES * RES
NQ = (RES // STRIDE) ** 2
C = 96
CA = C + 1
H, KD, VD = 12, 32, 64
DH = H * VD
NOFF = N
HALF = N // 2
ROWS = H * NQ
CH = 5
CR = -(-ROWS // CH)
D = 128
T2 = 2 * NQ
NP = B // 2
T = B * NQ
EPS = 1e-5

RH, RD = 8, 16
TG = 4
NG = NP // TG
GT = TG * T2

E = 16
HID = 512
HC = HID // 128
CAP = T // E
TH = CAP // 2
EC = 8
ROW = D + E
SA, SB_ = -(-CAP // 16), 16
SLOTS = SA * SB_
RING = 4
EG = 8


def chunk_rows(c):
    return min(CR, ROWS - c * CR)


def build(nc, d, out):
    with ExitStack() as ctx:
        tok_scope = ExitStack()
        scope = [ctx]

        def sb(name, shape, dt=F32):
            return scope[0].enter_context(nc.sbuf_tensor(name, shape, dt))

        def sem(name):
            return ctx.enter_context(nc.semaphore(name))

        bank = [ctx.enter_context(nc.psum_tensor(f"bank{k}", [128, 512], F32)) for k in range(8)]
        s_bank, t_bank, m_bank = bank[0:3], bank[3:5], bank[5:8]

        prob_rows = nc.dram_tensor("prob_rows", [T, ROW], F32).ap()
        list_d = nc.dram_tensor("list_scratch", [E, SLOTS], F32).ap()
        bias_d = nc.dram_tensor("bias_scratch", [3, H, NQ * N], F32).ap()

        ident = sb("ident", [128, 128])
        w_q, w_k, w_o = (sb(n, [D, D]) for n in ("w_q", "w_k", "w_o"))
        w_vg = sb("w_vg", [D, 2 * D])
        head_mask = sb("head_mask", [D, RH])
        decay = sb("decay", [T2, RH, T2])
        gn_w, gn_b = sb("gn_w", [T2, D]), sb("gn_b", [T2, D])
        gate_w = sb("gate_w", [D, E])
        sw1, sw2 = sb("sw1", [D, HID]), sb("sw2", [128, HC, D])
        sb1, sb2 = sb("sb1", [128, HC]), sb("sb2", [T2, D])
        same_expert = sb("same_expert", [128, 128])
        before = sb("before", [128, 128])
        iota_slot = sb("iota_slot", [T2, SB_])
        tok_col = sb("tok_col", [T2, 1])
        tile_num = sb("tile_num", [T2, TG, EC])
        diag = sb("diag", [EG * SA, EG, SB_])
        h_all = sb("h_all", [T2, NP, D])
        scope[0] = tok_scope
        iota_off = sb("iota_off", [HALF, 2])
        bias_cols = sb("bias_cols", [HALF, 2, H])
        q_w = sb("q_w", [KD, H, C])
        k_w = sb("k_w", [KD, H, C])
        par_qk = sb("par_qk", [KD, 4, 2 * H])
        s_qk = sb("s_qk", [KD, 2, 2 * H])
        q_aug = sb("q_aug", [KD, H, CA])
        k_aug = sb("k_aug", [KD, H, CA])
        qk_mat = sb("qk_mat", [CA, H, CA])
        par_v = sb("par_v", [128, 4, DH + D])
        s_v = sb("s_v", [128, 2, DH + D])
        v_w = sb("v_w", [C, DH])
        v_aug = sb("v_aug", [CA, H, VD + 1])
        proj = sb("proj", [128, DH // 128, D])
        idx_f = sb("idx_f", [HALF, 2, 7 * N], I32)
        onehot = [sb(f"onehot{p}", [HALF, 2, 7 * N], BF16) for p in range(2)]
        bias_rest = sb("bias_rest", [HALF, 2, H])
        bias_parts = sb("bias_parts", [HALF, 2, 3, 32], BF16)
        bias_out = sb("bias_out", [96, 2, 7 * N])
        bias_neg = sb("bias_neg", [CR, CH, N])
        bias_low = sb("bias_low", [CR, 2, CH, N])

        x_t = [sb(f"x_t{p}", [CA, 2 * N]) for p in range(2)]
        x_n = [sb(f"x_n{p}", [HALF, 4, CA]) for p in range(2)]
        g_t = sb("g_t", [CA, 2, ROWS])
        probs = sb("probs", [CR, 2, CH, N])
        neg_max = sb("neg_max", [CR, 2, CH])
        p_t = sb("p_t", [HALF, 2, ROWS])
        px_t = sb("px_t", [CA, H, T2])
        o_rec = sb("o_rec", [T2, 2, H // 2])
        o_sb = sb("o_sb", [T2, DH])
        o_u = sb("o_u", [T2, DH])
        o_a = sb("o_a", [T2, DH])
        three = sb("three", [T2, 1])
        a_t = sb("a_t", [128, DH // 128, T2])
        tok_scope.close()
        scope[0] = ctx

        hn_t = sb("hn_t", [D, T])
        hn_g = [sb(f"hn_g{p}", [D, GT]) for p in range(2)]
        rows = sb("rows", [T2, NP, ROW])
        logit = sb("logit", [T2, NP, E])
        lmax, lsum = sb("lmax", [T2, NP]), sb("lsum", [T2, NP])
        stats = sb("stats", [T2, TG, 6])
        mean_var = sb("mean_var", [T2, TG, 2])
        rstd = sb("rstd", [T2, TG])
        ln = sb("ln", [T2, TG, D])
        stats2 = sb("stats2", [T2, TG, 6])
        mean_var2 = sb("mean_var2", [T2, TG, 2])
        mean_all, rstd_all = sb("mean_all", [T2, NP]), sb("rstd_all", [T2, NP])
        hn = [sb(f"hn{p}", [T2, TG, D]) for p in range(2)]
        ret_scope = ExitStack()
        scope[0] = ret_scope
        ln_t = sb("ln_t", [D, GT])
        k_t = sb("k_t", [D, GT])
        v_sb = sb("v_sb", [T2, TG, D])
        gate_all = sb("gate_all", [T2, NP, D])
        q_heads = [sb(f"q_heads{p}", [D, RH, T2]) for p in range(2)]
        sc_tmp = sb("sc_tmp", [T2, RH // 2, T2])
        sc = [sb(f"sc{p}", [T2, RH, T2]) for p in range(2)]
        ret = sb("ret", [T2, TG * RH, RD])
        ret_c = sb("ret_c", [T2, TG * RH, RD])
        ret_sq = sb("ret_sq", [T2, TG * RH, RD])
        ret_n = sb("ret_n", [T2, TG, D])
        gmean = sb("gmean", [T2, TG * RH])
        gstd = sb("gstd", [T2, TG * RH])
        z = [sb(f"z{p}", [T2, TG, D]) for p in range(2)]
        z_t = [sb(f"z_t{p}", [D, GT]) for p in range(2)]
        ret_scope.close()
        scope[0] = ctx
        prob_j = sb("prob_j", [T2, TG, E * EC])
        xp = sb("xp", [128, GT])
        thr, cand, bit, mask = (sb(n, [128, 1], I32) for n in ("thr", "cand", "bit", "mask"))
        cnt = sb("cnt", [128, 1])
        above, equal, scan_e, sel, scan_s = (sb(n, [128, GT]) for n in ("above", "equal", "scan_e", "sel", "scan_s"))
        col = sb("col", [128, 4])
        hid = [sb(f"hid{p}", [128, HC, GT]) for p in range(2)]
        out_g = [sb(f"out_g{p}", [T2, TG, D]) for p in range(2)]
        slot = sb("slot", [T2, TG, 128], I32)
        slot_a, slot_b = sb("slot_a", [T2, TG, 128], I32), sb("slot_b", [T2, TG, 128], I32)
        hot_a = sb("hot_a", [T2, TG, EC, E, SA], BF16)
        hot_at = sb("hot_at", [T2, TG, EC, E, SA], BF16)
        hot_ap = sb("hot_ap", [T2, TG, EC, E, SA], BF16)
        hot_b = sb("hot_b", [T2, TG, EC, E, SB_], BF16)
        list_t = sb("list_t", [EG * SA, 2, EG, SB_])
        list_s = sb("list_s", [EG * SA, 2, SB_])
        list_r = sb("list_r", [2 * E, TH])
        idx_all = sb("idx_all", [TH, 2 * E], I32)
        idx2 = [sb(f"idx2{p}", [TH, 2], I32) for p in range(RING)]
        tok = [[sb(f"tok{p}{s}", [TH, ROW]) for s in range(2)] for p in range(RING)]
        tok_t = [sb(f"tok_t{p}", [D, CAP]) for p in range(2)]
        w1 = [sb(f"w1{p}", [D, HID]) for p in range(RING)]
        w2 = [sb(f"w2{p}", [128, HC, D]) for p in range(RING)]
        b1 = [sb(f"b1{p}", [128, HC]) for p in range(RING)]
        b2 = [sb(f"b2{p}", [TH, D]) for p in range(RING)]
        ehid = [sb(f"ehid{p}", [128, HC, CAP]) for p in range(2)]
        y = [[sb(f"y{p}{s}", [TH, D]) for s in range(2)] for p in range(RING)]

        small_in, wts2_in = sem("small_in"), sem("wts2_in")
        names = ("step ln_step gn_step stat_step var_ready std_ready ln_ready lt_ready lt_copied q_ready k_ready k_copied vg_ready vg_copied qm_made "
                 "sa_ready sb_ready sb_copied sa_done sb_done pv_ready ret_copied c_ready sq_ready gvar_ready gstd_ready gn_ready "
                 "pool_step z_done zs_ready zt_ready zt_copied wo_ready h2_done stats_done l_var l_std hn_ready hnt_ready hnt_copied hng_copied "
                 "rows_copied lg_ready lg_done lx_ready le_ready pr_ready xp_ready xp_copied sh_ready sh_gelu shy_ready shy_taken "
                 "cnt_ready tot_ready col_ready off_ready slot_ready slot_taken hot_ready list_ready list_done lr_ready lr_done "
                 "table_out list_out list_in idx_copied tt_ready tt_copied eh_ready eh_gelu ey_ready ey_taken y_done "
                 "scattered").split()
        (step, ln_step, gn_step, stat_step, var_ready, std_ready, ln_ready, lt_ready, lt_copied, q_ready, k_ready, k_copied, vg_ready, vg_copied, qm_made,
         sa_ready, sb_ready, sb_copied, sa_done, sb_done, pv_ready, ret_copied, c_ready, sq_ready, gvar_ready, gstd_ready, gn_ready,
         pool_step, z_done, zs_ready, zt_ready, zt_copied, wo_ready, h2_done, stats_done, l_var, l_std, hn_ready, hnt_ready, hnt_copied, hng_copied,
         rows_copied, lg_ready, lg_done, lx_ready, le_ready, pr_ready, xp_ready, xp_copied, sh_ready, sh_gelu, shy_ready, shy_taken,
         cnt_ready, tot_ready, col_ready, off_ready, slot_ready, slot_taken, hot_ready, list_ready, list_done, lr_ready, lr_done,
         table_out, list_out, list_in, idx_copied, tt_ready, tt_copied, eh_ready, eh_gelu, ey_ready, ey_taken, y_done,
         scattered) = (sem(n) for n in names)
        out_sent = [sem(f"out_sent{p}") for p in range(2)]
        tok_in = [sem(f"tok_in{p}") for p in range(RING)]
        ew_in = [sem(f"ew_in{p}") for p in range(RING)]
        out_rows = out.rearrange("(i p) c -> p i c", p=T2)

        const_in = sem("const_in")
        wts_in = sem("wts_in")
        idx_in = [sem(f"idx_in{p}") for p in range(2)]
        bias_back = sem("bias_back")
        bias_stored = [sem(f"bias_stored{p}") for p in range(2)]
        ones_set = sem("ones_set")
        x_in = [sem(f"x_in{p}") for p in range(2)]
        set_dve = sem("set_dve")
        set_act = sem("set_act")
        bank_read, parts_done = sem("bank_read"), sem("parts_done")
        mat_ready = sem("mat_ready")
        mat_copied = sem("mat_copied")
        hot_made = sem("hot_made")
        bias_mm = sem("bias_mm")
        bias_copied = sem("bias_copied")
        g_ready, g_copied = sem("g_ready"), sem("g_copied")
        s_ready, s_taken = sem("s_ready"), sem("s_taken")
        ttr_done, exp_done = sem("ttr_done"), sem("exp_done")
        t_ready, pt_copied = sem("t_ready"), sem("pt_copied")
        px_ready, px_copied = sem("px_ready"), sem("px_copied")
        o_ready, o_read, o_rec_done = sem("o_ready"), sem("o_read"), sem("o_rec_done")
        u_ready, a_ready = sem("u_ready"), sem("a_ready")
        at_ready, at_copied = sem("at_ready"), sem("at_copied")
        h_ready, h_copied = sem("h_ready"), sem("h_copied")
        dve_waited, pool_waited = sem("dve_waited"), sem("pool_waited")

        idx_flat = d["idx"].rearrange("q k -> (q k)")
        W7 = 7 * N

        def row_of_h(g):
            return h_all[:, g, :]

        with nc.Block() as block:
            @block.sync
            def _(sp):
                sp.dma_start(iota_off[:], d["iota_off"]).then_inc(const_in, 16)
                sp.dma_start(bias_cols[:], d["bias_cols"]).then_inc(const_in, 16)
                for k in range(2):
                    sp.dma_start(idx_f[:, k, :], idx_flat[k * W7:(k + 1) * W7].partition_broadcast(HALF)).then_inc(idx_in[k], 16)
                sp.dma_start(par_qk[:], d["par_qk"]).then_inc(wts_in, 16)
                sp.dma_start(q_w[:], d["q_w"]).then_inc(wts_in, 16)
                sp.dma_start(k_w[:], d["k_w"]).then_inc(wts_in, 16)
                sp.dma_start(v_w[:], d["v_w"]).then_inc(wts_in, 16)
                sp.dma_start(proj[:], d["proj"]).then_inc(wts_in, 16)
                sp.dma_start(par_v[:], d["par_v"].partition_broadcast(128)).then_inc(wts_in, 16)
                sp.dma_start(ident[:], d["ident"]).then_inc(wts_in, 16)

                def load_x(i, p):
                    sp.dma_start(x_t[p][0:C, :], d["x_t"][:, ds(i * 2 * N, 2 * N)]).then_inc(x_in[p], 16)
                    sp.dma_start(x_n[p][:, :, 0:C],
                                 d["x"][ds(i * 2, 2)].rearrange("b (s p) c -> p (b s) c", s=2)).then_inc(x_in[p], 16)

                load_x(0, 0)
                load_x(1, 1)
                for k in range(2, 9):
                    if k < 7:
                        sp.wait_ge(hot_made, k - 1)
                        sp.dma_start(idx_f[:, k % 2, :], idx_flat[k * W7:(k + 1) * W7].partition_broadcast(HALF)).then_inc(idx_in[k % 2], 16)
                    sp.wait_ge(bias_copied, k - 1)
                    for part in range(3):
                        sp.dma_start(bias_d[part, :, (k - 2) * W7:(k - 1) * W7],
                                     bias_out[32 * part:32 * part + H, k % 2, :]).then_inc(bias_stored[k % 2], 16)
                sp.wait_ge(bias_stored[0], 4 * 48)
                sp.wait_ge(bias_stored[1], 3 * 48)
                for part, o in ((0, bias_neg[:]), (1, bias_low[:, 0]), (2, bias_low[:, 1])):
                    flat = bias_d[part].rearrange("h (q k) -> (h q) k", k=N)
                    sp.dma_start(o[:, 0:CH - 1, :], flat[0:(CH - 1) * CR].rearrange("(c p) k -> p c k", p=CR)).then_inc(bias_back, 16)
                    sp.dma_start(o[0:chunk_rows(CH - 1), CH - 1, :], flat[(CH - 1) * CR:ROWS]).then_inc(bias_back, 16)
                for o, n in ((w_q, "w_q"), (w_k, "w_k"), (w_vg, "w_vg"), (w_o, "w_o"), (head_mask, "head_mask"), (decay, "decay"),
                             (gate_w, "gate_w"), (sw1, "sw1"), (sw2, "sw2"), (sb1, "sb1"), (same_expert, "same_expert"),
                             (before, "before"), (iota_slot, "iota_slot"), (tok_col, "tok_col"), (tile_num, "tile_num"), (diag, "diag")):
                    sp.dma_start(o[:], d[n]).then_inc(wts2_in, 16)
                for o, n in ((gn_w, "gn_w"), (gn_b, "gn_b"), (sb2, "sb2")):
                    sp.dma_start(o[:], d[n].partition_broadcast(T2)).then_inc(wts2_in, 16)
                with sp.Fori(1, NP // 2) as j:
                    for p in range(2):
                        sp.wait_ge(o_ready, 2 * (2 * j + p) - 2)
                        load_x(2 * j + p, p)
                sp.wait_ge(h_copied, NP)
                sp.wait_ge(rows_copied, NG)
                sp.wait_ge(pr_ready, 1)
                sp.dma_start(prob_rows.rearrange("(i p) c -> p i c", p=T2), rows[:, :, :]).then_inc(table_out, 16)

                def load_expert(e, p):
                    sp.dma_start(w1[p][:], d["w1"][ds(e, 1)].rearrange("e d h -> (e d) h")).then_inc(ew_in[p], 16)
                    sp.dma_start(w2[p][:], d["w2"][ds(e, 1)].rearrange("e k c n -> (e k) c n")).then_inc(ew_in[p], 16)
                    sp.dma_start(b1[p][:], d["b1"][ds(e, 1)].rearrange("e k c -> (e k) c")).then_inc(ew_in[p], 16)
                    sp.dma_start(b2[p][:], d["b2"][ds(e, 1)].rearrange("e n -> (e n)").partition_broadcast(TH)).then_inc(ew_in[p], 16)

                for e in range(RING):
                    load_expert(e, e)
                with sp.Fori(0, NG // 2) as j:
                    for p in range(2):
                        sp.wait_ge(shy_taken, 2 * j + p + 1)
                        sp.dma_start(out_rows[:, ds((2 * j + p) * TG, TG), :], out_g[p][:]).then_inc(out_sent[p], 16)
                sp.wait_ge(list_done, 1)
                sp.dma_start(list_d.rearrange("(g e) (a b) -> (e a) g b", g=2, a=SA), list_s[:]).then_inc(list_out, 16)
                sp.wait_ge(list_out, 16)
                for s in range(2):
                    sp.dma_start(list_r[s * E:(s + 1) * E, :], list_d[:, s * TH:(s + 1) * TH]).then_inc(list_in, 16)
                with sp.Fori(1, E // RING) as j:
                    for p in range(RING):
                        sp.wait_ge(y_done, 2 * (RING * (j - 1) + p + 1))
                        load_expert(RING * j + p, p)
                sp.wait_ge(scattered, 2 * 16 * E)

            @block.gpsimd
            def _(pool):
                for p in range(2):
                    if p:
                        pool.wait_ge(ones_set, 2 * p)
                    nc.gpsimd.memset(x_t[p][C:CA, :], 1.0).then_inc(ones_set, 1)
                    pool.wait_ge(ones_set, 2 * p + 1)
                    nc.gpsimd.memset(x_n[p][:, :, C:CA], 1.0).then_inc(ones_set, 1)

                pool.wait_ge(h_copied, NP)
                pool.wait_ge(wts2_in, WTS2)

                def decay_b(g, u, first=False):
                    k = TG * g + u
                    pool.wait_ge(sb_copied, k + 1)
                    if not (first and u < 2):
                        pool.wait_ge(pv_ready, k - 1)
                    nc.gpsimd.tensor_tensor(sc[u % 2][:, RH // 2:RH, :], sc_tmp[:], decay[:, RH // 2:RH, :], ALU.mult).then_inc(sb_done, 1)

                def squares(g):
                    pool.wait_ge(c_ready, g + 1)
                    nc.gpsimd.tensor_tensor(ret_sq[:], ret_c[:], ret_c[:], ALU.mult).then_inc(sq_ready, 1)

                def gate_input(g):
                    pool.wait_ge(gn_ready, g + 1)
                    nc.gpsimd.tensor_tensor(ret_n[:], ret_n[:], gn_w[:].unsqueeze(1).to_broadcast([T2, TG, D]), ALU.mult).then_inc(pool_step, 1)
                    pool.wait_ge(pool_step, 2 * g + 1)
                    nc.gpsimd.tensor_tensor(ret_n[:], ret_n[:], gn_b[:].unsqueeze(1).to_broadcast([T2, TG, D]), ALU.add).then_inc(pool_step, 1)
                    pool.wait_ge(pool_step, 2 * g + 2)
                    zg = gate_all[:, ds(TG * g, TG), :]
                    nc.gpsimd.tensor_tensor(zg, ret_n[:], zg, ALU.add).then_inc(z_done, 1)

                for u in range(TG):
                    decay_b(0, u, first=True)
                with pool.Fori(1, NG) as g:
                    decay_b(g, 0)
                    squares(g - 1)
                    for u in range(1, TG):
                        decay_b(g, u)
                    gate_input(g - 1)
                squares(NG - 1)
                gate_input(NG - 1)
                with pool.Fori(0, NG // 2) as j:
                    for p in range(2):
                        pool.wait_ge(hn_ready, 2 * j + p + 1)
                        nc.gpsimd.tensor_copy(rows[:, ds(TG * (2 * j + p), TG), 0:D], hn[p][:]).then_inc(rows_copied, 1)

                def gather(e, p):
                    nc.gpsimd.tensor_copy(idx2[p][:, 0:1], idx_all[:, ds(e, 1)])
                    nc.gpsimd.tensor_copy(idx2[p][:, 1:2], idx_all[:, ds(e + E, 1)]).then_inc(idx_copied, 1)
                    pool.wait_ge(idx_copied, e + 1)
                    pool.sem_inc(pool_waited, 1)
                    for s in range(2):
                        nc.gpsimd.indirect_dma_start(out=tok[p][s][:], out_offset=None, in_=prob_rows,
                                                     in_offset=bass.IndirectOffsetOnAxis(ap=idx2[p][:, s:s + 1], axis=0)).then_inc(tok_in[p], 16)

                pool.wait_ge(table_out, 16)
                pool.wait_ge(lr_done, 1)
                for e in range(RING - 1):
                    gather(e, e)
                for p in range(2):
                    pool.wait_ge(out_sent[p], 16 * NG // 2)

                def before_scattered(e):
                    if not (isinstance(e, int) and e == 0):
                        pool.wait_ge(scattered, 32 * e)

                def scatter(e, p):
                    pool.wait_ge(y_done, 2 * e + 2)
                    pool.sem_inc(pool_waited, 1)
                    for s in range(2):
                        nc.gpsimd.indirect_dma_start(out=out, out_offset=bass.IndirectOffsetOnAxis(ap=idx2[p][:, s:s + 1], axis=0),
                                                     in_=y[p][s][:], in_offset=None, compute_op=ALU.add).then_inc(scattered, 16)

                def step_expert(e, p):
                    before_scattered(e)
                    gather(e + RING - 1, (p - 1) % RING)
                    scatter(e, p)

                for e in range(RING):
                    step_expert(e, e)
                with pool.Fori(1, E // RING - 1) as j:
                    for p in range(RING):
                        step_expert(RING * j + p, p)
                step_expert(E - RING, 0)
                for p in range(1, RING):
                    before_scattered(E - RING + p)
                    scatter(E - RING + p, p)

            @block.scalar
            def _(act):
                for k in range(7):
                    if k >= 2:
                        act.wait_ge(bias_stored[k % 2], 48 * (k // 2))
                    for n in range(4):
                        act.wait_ge(bias_mm, 4 * k + n + 1)
                        last = nc.scalar.mul(bias_out[:, k % 2, n * 343:(n + 1) * 343], s_bank[n % 2][0:96, 0:343], -1.0)
                        last.then_inc(bank_read, 1)
                    act.wait_ge(bank_read, 4 * (k + 1))
                    act.sem_inc(bias_copied, 1)
                    if k == 1:
                        act.wait_ge(set_dve, 2)
                        nc.scalar.activation(s_qk[:, 0, :], s_qk[:, 0, :], ACT.Sqrt).then_inc(set_act, 1)
                        nc.scalar.activation(s_v[:, 0, :], s_v[:, 0, :], ACT.Sqrt).then_inc(set_act, 1)

                def exps(k, kp):
                    for c in range(CH):
                        m = chunk_rows(c)
                        act.wait_ge(ttr_done, CH * k + c + 1)
                        nc.scalar.activation(probs[0:m, kp, c, :], probs[0:m, kp, c, :], ACT.Exp,
                                             bias=neg_max[0:m, kp, c:c + 1], scale=-1.0).then_inc(exp_done, 1)

                def copy_px(k, b, f0):
                    for a in range(2):
                        act.wait_ge(px_ready, 2 * k + a + 1)
                        nc.scalar.copy(px_t[:, a * 6:(a + 1) * 6, b * NQ:(b + 1) * NQ],
                                       m_bank[(f0 + a) % 3][0:CA, 0:6 * NQ].rearrange("p (h q) -> p h q", h=6)).then_inc(px_copied, 1)

                def copy_at(i):
                    for a in range(2):
                        act.wait_ge(at_ready, 2 * i + a + 1)
                        nc.scalar.copy(a_t[:, 3 * a:3 * a + 3, :],
                                       m_bank[1 + a][:, 0:3 * T2].rearrange("p (c t) -> p c t", c=3)).then_inc(at_copied, 1)

                def relu(i):
                    act.wait_ge(o_read, 2 * i + 2)
                    nc.scalar.activation(o_u[:], o_sb[:], ACT.Relu, bias=three[:, 0:1]).then_inc(u_ready, 1)

                def body(i, first=False, last=False):
                    exps(2 * i + 1, 1)
                    if not first:
                        relu(i - 1)
                    copy_px(2 * i, 0, 0)
                    if not last:
                        exps(2 * i + 2, 0)
                    copy_px(2 * i + 1, 1, 2)
                    if not first:
                        copy_at(i - 1)

                exps(0, 0)
                body(0, first=True)
                with act.Fori(1, NP - 1) as i:
                    body(i)
                body(NP - 1, last=True)
                relu(NP - 1)
                copy_at(NP - 1)

                act.wait_ge(h_copied, NP)

                def root_ln(n):
                    act.wait_ge(var_ready, n + 1)
                    nc.scalar.activation(rstd[:], rstd[:], ACT.Sqrt).then_inc(std_ready, 1)

                def scores_b(g, u, first=False):
                    k = TG * g + u
                    act.wait_ge(sb_ready, k + 1)
                    if not (first and u < 1):
                        act.wait_ge(sb_done, k)
                    nc.scalar.copy(sc_tmp[:], bank[6][0:T2, 0:GT].rearrange("p (h t) -> p h t", h=TG)).then_inc(sb_copied, 1)

                def copy_lt(g):
                    act.wait_ge(lt_ready, g + 1)
                    nc.scalar.copy(ln_t[:], bank[0][:, 0:GT]).then_inc(lt_copied, 1)

                def copy_k(g):
                    act.wait_ge(k_ready, g + 1)
                    nc.scalar.copy(k_t[:], bank[2][:, 0:GT]).then_inc(k_copied, 1)

                def copy_vg(g):
                    for a in range(2):
                        act.wait_ge(vg_ready, 2 * g + a + 1)
                        vg = bank[3 + a][0:T2, :].rearrange("p (u v) -> p u v", u=2)
                        nc.scalar.copy(v_sb[:, 2 * a:2 * a + 2, :], vg[:, :, 0:D])
                        nc.scalar.copy(gate_all[:, ds(TG * g + 2 * a, 2), :], vg[:, :, D:2 * D]).then_inc(vg_copied, 1)

                def copy_ret(g, first=False):
                    act.wait_ge(pv_ready, TG * g + TG)
                    if not first:
                        act.wait_ge(c_ready, g)
                    nc.scalar.copy(ret[:], bank[7][0:T2, :].rearrange("p (h r) -> p h r", r=RD)).then_inc(ret_copied, 1)

                def root_gn(g):
                    act.wait_ge(gvar_ready, g + 1)
                    nc.scalar.activation(gstd[:], gstd[:], ACT.Sqrt).then_inc(gstd_ready, 1)

                def retention(g, first=False, last=False):
                    scores_b(g, 0, first)
                    if not last:
                        root_ln(g + 1)
                    scores_b(g, 1)
                    scores_b(g, 2)
                    if not last:
                        copy_lt(g + 1)
                    if not first:
                        root_gn(g - 1)
                    scores_b(g, 3)
                    if not last:
                        copy_k(g + 1)
                    copy_ret(g, first)
                    if not last:
                        copy_vg(g + 1)

                root_ln(0)
                copy_lt(0)
                copy_k(0)
                copy_vg(0)
                retention(0, first=True)
                with act.Fori(1, NG - 1) as g:
                    retention(g)
                retention(NG - 1, last=True)
                root_gn(NG - 1)

                def silu(g, p):
                    act.wait_ge(z_done, g + 1)
                    nc.scalar.activation(z[p][:], gate_all[:, ds(TG * g, TG), :], ACT.Silu).then_inc(zs_ready, 1)

                def copy_zt(g, p, first=False):
                    act.wait_ge(zt_ready, g + 1)
                    if not first:
                        act.wait_ge(wo_ready, g - 1)
                    nc.scalar.copy(z_t[p][:], bank[0][:, 0:GT]).then_inc(zt_copied, 1)

                silu(0, 0)
                silu(1, 1)
                for g in range(2):
                    copy_zt(g, g, first=True)
                    silu(g + 2, g)
                with act.Fori(1, NG // 2 - 1) as j:
                    for p in range(2):
                        copy_zt(2 * j + p, p)
                        silu(2 * j + p + 2, p)
                copy_zt(NG - 2, 0)
                copy_zt(NG - 1, 1)

                act.wait_ge(l_var, 1)
                nc.scalar.activation(rstd_all[:], rstd_all[:], ACT.Sqrt).then_inc(l_std, 1)

                def copy_hnt(g, p, first=False):
                    act.wait_ge(hnt_ready, g + 1)
                    if not first:
                        act.wait_ge(lg_ready, g - 1)
                    nc.scalar.copy(hn_g[p][:], bank[2 * p][:, 0:GT]).then_inc(hng_copied, 1)
                    nc.scalar.copy(hn_t[:, ds(GT * g, GT)], bank[2 * p][:, 0:GT]).then_inc(hnt_copied, 1)

                copy_hnt(0, 0, True)
                copy_hnt(1, 1, True)
                with act.Fori(1, NG // 2) as j:
                    for p in range(2):
                        copy_hnt(2 * j + p, p)

                act.wait_ge(lx_ready, 1)
                nc.scalar.activation(logit[:], logit[:], ACT.Exp).then_inc(le_ready, 1)

                def gelu_shared(g, p, first=False):
                    for c in range(HC):
                        act.wait_ge(sh_ready, HC * g + c + 1)
                        if c == 0 and not first:
                            act.wait_ge(shy_ready, g - 1)
                        nc.scalar.activation(hid[p][:, c, :], bank[c][:, 0:GT], ACT.Gelu_apprx_tanh, bias=sb1[:, c:c + 1]).then_inc(sh_gelu, 1)

                gelu_shared(0, 0, True)
                gelu_shared(1, 1, True)
                with act.Fori(1, NG // 2) as j:
                    for p in range(2):
                        gelu_shared(2 * j + p, p)

                def copy_tt(e, p):
                    act.wait_ge(tt_ready, e + 1)
                    nc.scalar.copy(tok_t[p][:], bank[0][:, 0:CAP]).then_inc(tt_copied, 1)

                def gelu_expert(e, p):
                    for c in range(HC):
                        act.wait_ge(eh_ready, 2 * e + c // 2 + 1)
                        nc.scalar.activation(ehid[p % 2][:, c, :], bank[1 + c // 2][:, (c % 2) * CAP:(c % 2 + 1) * CAP], ACT.Gelu_apprx_tanh,
                                             bias=b1[p][:, c:c + 1]).then_inc(eh_gelu, 1)

                copy_tt(0, 0)
                with act.Fori(0, E // RING - 1) as j:
                    for p in range(RING):
                        gelu_expert(RING * j + p, p)
                        copy_tt(RING * j + p + 1, 1 - p % 2)
                for p in range(RING - 1):
                    gelu_expert(E - RING + p, p)
                    copy_tt(E - RING + p + 1, 1 - p % 2)
                gelu_expert(E - 1, RING - 1)

            @block.vector
            def _(dve):
                done = [0]

                def setup(ins):
                    done[0] += 1
                    ins.then_inc(set_dve, 1)
                    return done[0]

                def hot(k):
                    dve.wait_ge(idx_in[k % 2], 16 * (k // 2 + 1))
                    if k >= 2:
                        dve.wait_ge(bias_mm, 4 * (k - 1))
                    nc.vector.tensor_scalar(onehot[k % 2][:, 0, :], idx_f[:, k % 2, :], iota_off[:, 0:1], None, ALU.is_equal)
                    nc.vector.tensor_scalar(onehot[k % 2][:, 1, :], idx_f[:, k % 2, :], iota_off[:, 1:2], None, ALU.is_equal).then_inc(hot_made, 1)

                dve.wait_ge(const_in, 32)
                nc.vector.memset(bias_parts[:], 0.0).then_inc(parts_done, 1)
                dve.wait_ge(parts_done, 1)
                nc.vector.tensor_copy(bias_parts[:, :, 0, 0:H], bias_cols[:]).then_inc(parts_done, 1)
                dve.wait_ge(parts_done, 2)
                nc.vector.tensor_tensor(bias_rest[:], bias_cols[:], bias_parts[:, :, 0, 0:H], ALU.subtract).then_inc(parts_done, 1)
                dve.wait_ge(parts_done, 3)
                nc.vector.tensor_copy(bias_parts[:, :, 1, 0:H], bias_rest[:]).then_inc(parts_done, 1)
                dve.wait_ge(parts_done, 4)
                nc.vector.tensor_tensor(bias_rest[:], bias_rest[:], bias_parts[:, :, 1, 0:H], ALU.subtract).then_inc(parts_done, 1)
                dve.wait_ge(parts_done, 5)
                nc.vector.tensor_copy(bias_parts[:, :, 2, 0:H], bias_rest[:]).then_inc(parts_done, 1)
                for k in range(3):
                    hot(k)
                dve.wait_ge(wts_in, 7 * 16)
                setup(nc.vector.tensor_scalar_add(s_qk[:, 0, :], par_qk[:, 3, :], EPS))
                setup(nc.vector.tensor_scalar_add(s_v[:, 0, :], par_v[:, 3, :], EPS))
                for n, (s, par) in enumerate(((s_qk, par_qk), (s_v, par_v))):
                    dve.wait_ge(set_act, n + 1)
                    dve.wait_ge(set_dve, setup(nc.vector.reciprocal(s[:, 0, :], s[:, 0, :])))
                    dve.wait_ge(set_dve, setup(nc.vector.tensor_tensor(s[:, 0, :], s[:, 0, :], par[:, 0, :], ALU.mult)))
                    dve.wait_ge(set_dve, setup(nc.vector.tensor_tensor(s[:, 1, :], s[:, 0, :], par[:, 2, :], ALU.mult)))
                    dve.wait_ge(set_dve, setup(nc.vector.tensor_tensor(s[:, 1, :], par[:, 1, :], s[:, 1, :], ALU.subtract)))
                    hot(3 + n)
                for o, w, n in ((q_aug, q_w, 0), (k_aug, k_w, H)):
                    setup(nc.vector.tensor_tensor(o[:, :, 0:C], w[:], s_qk[:, 0, n:n + H].unsqueeze(2).to_broadcast([KD, H, C]), ALU.mult))
                    setup(nc.vector.tensor_copy(o[:, :, C], s_qk[:, 1, n:n + H]))
                dve.wait_ge(set_dve, done[0])
                setup(nc.vector.tensor_scalar(q_aug[:], q_aug[:], -(KD ** -0.5), None, ALU.mult))
                hot(5)
                setup(nc.vector.tensor_tensor(v_aug[0:C, :, 0:VD], v_w[:].rearrange("c (h e) -> c h e", h=H),
                                              s_v[0:C, 0, 0:DH].rearrange("c (h e) -> c h e", h=H), ALU.mult))
                setup(nc.vector.tensor_copy(v_aug[C:CA, :, 0:VD], s_v[C:CA, 1, 0:DH].rearrange("c (h e) -> c h e", h=H)))
                setup(nc.vector.memset(v_aug[0:C, :, VD:VD + 1], 0.0))
                setup(nc.vector.memset(v_aug[C:CA, :, VD:VD + 1], 1.0))
                setup(nc.vector.tensor_tensor(proj[:], proj[:], s_v[:, 0, DH:DH + D].unsqueeze(1).to_broadcast([128, DH // 128, D]), ALU.mult))
                dve.wait_ge(set_dve, done[0])
                setup(nc.vector.tensor_scalar(proj[:], proj[:], 1.0 / 6.0, None, ALU.mult))
                setup(nc.vector.memset(three[:], 3.0))
                assert done[0] == SETUP_STEPS
                hot(6)
                for n in range(3):
                    dve.wait_ge(mat_ready, n + 1)
                    nc.vector.tensor_copy(qk_mat[:, 4 * n:4 * n + 4, :], m_bank[n][0:CA, 0:4 * CA].rearrange("p (h c) -> p h c", h=4)).then_inc(mat_copied, 1)

                def add_bias(k, kp, first=False, chunks=range(CH)):
                    if not first and 0 in chunks:
                        dve.wait_ge(t_ready, 3 * k - 3)
                    for c in chunks:
                        m = chunk_rows(c)
                        if c % 2 == 0:
                            dve.wait_ge(s_ready, 3 * k + c // 2 + 1)
                            dve.sem_inc(dve_waited, 1)
                        ins = nc.vector.tensor_tensor_reduce(
                            out=probs[0:m, kp, c, :], in0=s_bank[c // 2][0:m, (c % 2) * N:(c % 2 + 1) * N],
                            in1=bias_neg[0:m, c, :], scale=1.0, scalar=3.0e38, op0=ALU.add, op1=ALU.min,
                            accum_out=neg_max[0:m, kp, c:c + 1])
                        ins.then_inc(ttr_done, 1)

                def copy_pt(k, kk, t):
                    if True:
                        w = chunk_cols(t)
                        dve.wait_ge(t_ready, 3 * k + t + 1)
                        nc.vector.tensor_copy(p_t[:, :, 2 * CR * t:2 * CR * t + w],
                                              t_bank[(3 * kk + t) % 2][0:HALF, 0:4 * CR].rearrange("p (s r) -> p s r", s=2)[:, :, 0:w]).then_inc(pt_copied, 1)

                def copy_g(i, g):
                    if True:
                        dve.wait_ge(g_ready, 3 * i + g + 1)
                        nc.vector.tensor_copy(g_t[:, :, 4 * g * NQ:4 * (g + 1) * NQ].rearrange("p b (h q) -> p h b q", h=4),
                                              m_bank[g][0:CA, 0:4 * T2].rearrange("p (h b q) -> p h b q", h=4, b=2)).then_inc(g_copied, 1)

                def take_o(i, first=False):
                    for a in range(2):
                        o = m_bank[a][0:T2, 0:6 * (VD + 1)].rearrange("p (h e) -> p h e", h=6)
                        dve.wait_ge(o_ready, 2 * i + a + 1)
                        nc.vector.reciprocal(o_rec[:, a, :], o[:, :, VD]).then_inc(o_rec_done, 1)
                        dve.wait_ge(o_rec_done, 2 * i + a + 1)
                        if a == 0 and not first:
                            dve.wait_ge(a_ready, i)
                        nc.vector.tensor_tensor(o_sb[:, a * 6 * VD:(a + 1) * 6 * VD].rearrange("p (h e) -> p h e", h=6),
                                                o[:, :, 0:VD], o_rec[:, a, :].unsqueeze(2).to_broadcast([T2, 6, VD]), ALU.mult).then_inc(o_read, 1)

                def take_h(i):
                    dve.wait_ge(h_ready, i + 1)
                    nc.vector.tensor_tensor(row_of_h(i), m_bank[2][0:T2, 0:D], s_v[0:T2, 1, DH:DH + D], ALU.add).then_inc(h_copied, 1)

                def hard_swish(i, first=False):
                    dve.wait_ge(u_ready, i + 1)
                    if not first:
                        dve.wait_ge(at_ready, 2 * i)
                    nc.vector.scalar_tensor_tensor(out=o_a[:], in0=o_u[:], scalar=6.0, in1=o_sb[:], op0=ALU.min, op1=ALU.mult).then_inc(a_ready, 1)

                def body(i, first=False, second=False, last=False):
                    add_bias(2 * i + 1, 1, first=first)
                    copy_pt(2 * i, 0, 0)
                    copy_pt(2 * i, 0, 1)
                    if not last:
                        copy_g(i + 1, 0)
                    copy_pt(2 * i, 0, 2)
                    if not last:
                        copy_g(i + 1, 1)
                        copy_g(i + 1, 2)
                    for t in range(2):
                        copy_pt(2 * i + 1, 1, t)
                    if not last:
                        add_bias(2 * i + 2, 0, chunks=range(0, 2))
                    copy_pt(2 * i + 1, 1, 2)
                    if not last:
                        add_bias(2 * i + 2, 0, chunks=range(2, CH))
                    if not first:
                        hard_swish(i - 1, first=second)
                    take_o(i, first=first)
                    if not first:
                        take_h(i - 1)

                for g in range(3):
                    copy_g(0, g)
                dve.wait_ge(bias_back, 96)
                for part in range(2):
                    nc.vector.tensor_tensor(bias_neg[:, 0:CH - 1], bias_neg[:, 0:CH - 1], bias_low[:, part, 0:CH - 1], ALU.add).then_inc(parts_done, 1)
                    m = chunk_rows(CH - 1)
                    nc.vector.tensor_tensor(bias_neg[0:m, CH - 1], bias_neg[0:m, CH - 1], bias_low[0:m, part, CH - 1], ALU.add).then_inc(parts_done, 1)
                    dve.wait_ge(parts_done, 6 + 2 * (part + 1))
                add_bias(0, 0, first=True)
                body(0, first=True)
                body(1, second=True)
                with dve.Fori(2, NP - 1) as i:
                    body(i)
                body(NP - 1, last=True)
                hard_swish(NP - 1)
                take_h(NP - 1)

                dve.wait_ge(wts2_in, WTS2)

                LN1 = 2 * TG + 1
                GN1 = 4

                def moments(g):
                    for u in range(TG):
                        nc.vector.bn_stats(stats[:, u, :], h_all[:, ds(TG * g + u, 1), :].rearrange("p a c -> p (a c)")).then_inc(ln_step, 1)
                    dve.wait_ge(ln_step, LN1 * g + TG)
                    dve.sem_inc(dve_waited, 1)
                    for u in range(TG):
                        nc.vector.bn_aggr(mean_var[:, u, :], stats[:, u, :]).then_inc(ln_step, 1)
                    dve.wait_ge(ln_step, LN1 * g + 2 * TG)
                    nc.vector.tensor_scalar_add(rstd[:], mean_var[:, :, 1], EPS).then_inc(var_ready, 1)

                def normalise(g, first=False):
                    dve.wait_ge(std_ready, g + 1)
                    nc.vector.reciprocal(rstd[:], rstd[:]).then_inc(ln_step, 1)
                    dve.wait_ge(ln_step, LN1 * g + LN1)
                    if not first:
                        dve.wait_ge(lt_ready, g)
                    for u in range(TG):
                        ins = nc.vector.tensor_scalar(ln[:, u, :], h_all[:, ds(TG * g + u, 1), :].rearrange("p a c -> p (a c)"),
                                                      mean_var[:, u, 0:1], rstd[:, u:u + 1], ALU.subtract, ALU.mult)
                    ins.then_inc(ln_ready, 1)

                def group_norm_a(g):
                    dve.wait_ge(ret_copied, g + 1)
                    nc.vector.tensor_reduce(gmean[:], ret[:], AX.X, ALU.add).then_inc(gn_step, 1)
                    dve.wait_ge(gn_step, GN1 * g + 1)
                    nc.vector.tensor_scalar(gmean[:], gmean[:], 1.0 / RD, None, ALU.mult).then_inc(gn_step, 1)
                    dve.wait_ge(gn_step, GN1 * g + 2)
                    nc.vector.tensor_tensor(ret_c[:], ret[:], gmean[:].unsqueeze(2).to_broadcast([T2, TG * RH, RD]), ALU.subtract).then_inc(c_ready, 1)

                def group_norm_b(g):
                    dve.wait_ge(sq_ready, g + 1)
                    nc.vector.tensor_reduce(gstd[:], ret_sq[:], AX.X, ALU.add).then_inc(gn_step, 1)
                    dve.wait_ge(gn_step, GN1 * g + 3)
                    nc.vector.tensor_scalar(gstd[:], gstd[:], 1.0 / RD, EPS, ALU.mult, ALU.add).then_inc(gvar_ready, 1)

                def group_norm_c(g, first=False):
                    dve.wait_ge(gstd_ready, g + 1)
                    nc.vector.reciprocal(gstd[:], gstd[:]).then_inc(gn_step, 1)
                    dve.wait_ge(gn_step, GN1 * g + 4)
                    if not first:
                        dve.wait_ge(z_done, g)
                    nc.vector.tensor_tensor(ret_n[:].rearrange("p u (h r) -> p (u h) r", h=RH), ret_c[:],
                                            gstd[:].unsqueeze(2).to_broadcast([T2, TG * RH, RD]), ALU.mult).then_inc(gn_ready, 1)

                def spread_q(g, u, first=False):
                    k = TG * g + u
                    if u == 0:
                        dve.wait_ge(q_ready, g + 1)
                    if not (first and u < 2):
                        dve.wait_ge(sb_ready, k - 1)
                    nc.vector.tensor_tensor(q_heads[u % 2][:], bank[1][:, u * T2:(u + 1) * T2].unsqueeze(1).to_broadcast([D, RH, T2]),
                                            head_mask[:].unsqueeze(2).to_broadcast([D, RH, T2]), ALU.mult).then_inc(qm_made, 1)

                def decay_a(g, u, first=False):
                    k = TG * g + u
                    dve.wait_ge(sa_ready, k + 1)
                    if not (first and u < 2):
                        dve.wait_ge(pv_ready, k - 1)
                    nc.vector.tensor_tensor(sc[u % 2][:, 0:RH // 2, :], bank[5][0:T2, 0:GT].rearrange("p (h t) -> p h t", h=TG),
                                            decay[:, 0:RH // 2, :], ALU.mult).then_inc(sa_done, 1)

                def retention(g, first=False, second=False, last=False):
                    decay_a(g, 0, first)
                    if not first:
                        group_norm_a(g - 1)
                    spread_q(g, 2)
                    decay_a(g, 1, first)
                    if not last:
                        moments(g + 1)
                    spread_q(g, 3)
                    decay_a(g, 2)
                    if not last:
                        normalise(g + 1)
                    if not first:
                        group_norm_b(g - 1)
                    decay_a(g, 3)
                    if not first:
                        group_norm_c(g - 1, second)
                    if not last:
                        spread_q(g + 1, 0)
                        spread_q(g + 1, 1)

                moments(0)
                normalise(0, first=True)
                spread_q(0, 0, first=True)
                spread_q(0, 1, first=True)
                retention(0, first=True)
                retention(1, second=True)
                with dve.Fori(2, NG - 1) as g:
                    retention(g)
                retention(NG - 1, last=True)
                group_norm_a(NG - 1)
                group_norm_b(NG - 1)
                group_norm_c(NG - 1)

                STAT = 2 * TG

                def residual(g, p):
                    dve.wait_ge(wo_ready, g + 1)
                    hg = h_all[:, ds(TG * g, TG), :]
                    nc.vector.tensor_tensor(hg, bank[1 + 2 * p][0:T2, :].rearrange("p (u c) -> p u c", u=TG), hg, ALU.add).then_inc(h2_done, 1)

                def moments2(g):
                    dve.wait_ge(h2_done, g + 1)
                    dve.sem_inc(dve_waited, 1)
                    for u in range(TG):
                        nc.vector.bn_stats(stats2[:, u, :], h_all[:, ds(TG * g + u, 1), :].rearrange("p a c -> p (a c)")).then_inc(stat_step, 1)
                    dve.wait_ge(stat_step, STAT * g + TG)
                    dve.sem_inc(dve_waited, 1)
                    for u in range(TG):
                        nc.vector.bn_aggr(mean_var2[:, u, :], stats2[:, u, :]).then_inc(stat_step, 1)
                    dve.wait_ge(stat_step, STAT * g + 2 * TG)
                    nc.vector.tensor_copy(mean_all[:, ds(TG * g, TG)], mean_var2[:, :, 0])
                    nc.vector.tensor_scalar_add(rstd_all[:, ds(TG * g, TG)], mean_var2[:, :, 1], EPS).then_inc(stats_done, 1)

                residual(0, 0)
                residual(1, 1)
                moments2(0)
                with dve.Fori(1, NG // 2) as j:
                    for p in range(2):
                        residual(2 * j + p, p)
                        moments2(2 * j + p - 1)
                moments2(NG - 1)
                dve.wait_ge(stats_done, NG)
                dve.sem_inc(l_var, 1)

                dve.wait_ge(l_std, 1)
                nc.vector.reciprocal(rstd_all[:], rstd_all[:]).then_inc(stats_done, 1)
                dve.wait_ge(stats_done, NG + 1)

                def second_norm(g, p, first=False):
                    if not first:
                        dve.wait_ge(rows_copied, g - 1)
                        dve.wait_ge(hnt_ready, g - 1)
                    for u in range(TG):
                        ins = nc.vector.tensor_scalar(hn[p][:, u, :], h_all[:, ds(TG * g + u, 1), :].rearrange("p a c -> p (a c)"),
                                                      mean_all[:, ds(TG * g + u, 1)], rstd_all[:, ds(TG * g + u, 1)], ALU.subtract, ALU.mult)
                    ins.then_inc(hn_ready, 1)

                def take_logits(g, p):
                    dve.wait_ge(lg_ready, g + 1)
                    nc.vector.tensor_copy(logit[:, ds(TG * g, TG), :], bank[1 + 2 * p][0:T2, 0:TG * E].rearrange("p (u e) -> p u e", u=TG)).then_inc(lg_done, 1)

                second_norm(0, 0, True)
                second_norm(1, 1, True)
                take_logits(0, 0)
                with dve.Fori(1, NG // 2) as j:
                    for p in range(2):
                        second_norm(2 * j + p, p)
                        take_logits(2 * j + p - 1, 1 - p)
                take_logits(NG - 1, 1)
                n_steps = 0
                m = [n_steps]

                def then(ins):
                    m[0] += 1
                    ins.then_inc(step, 1)
                    dve.wait_ge(step, m[0])

                dve.wait_ge(lg_done, NG)
                then(nc.vector.tensor_reduce(lmax[:], logit[:], AX.X, ALU.max))
                nc.vector.tensor_tensor(logit[:], logit[:], lmax[:].unsqueeze(2).to_broadcast([T2, NP, E]), ALU.subtract).then_inc(lx_ready, 1)
                dve.wait_ge(le_ready, 1)
                then(nc.vector.tensor_reduce(lsum[:], logit[:], AX.X, ALU.add))
                then(nc.vector.reciprocal(lsum[:], lsum[:]))
                dve.wait_ge(rows_copied, NG)
                nc.vector.tensor_tensor(rows[:, :, D:ROW], logit[:], lsum[:].unsqueeze(2).to_broadcast([T2, NP, E]), ALU.mult).then_inc(pr_ready, 1)
                dve.wait_ge(pr_ready, 1)
                nc.vector.tensor_copy(prob_j[:].rearrange("p j (e c) -> p c j e", e=E),
                                      rows[:, :, D:ROW].rearrange("p (c j) e -> p c j e", j=TG)).then_inc(pr_ready, 1)
                nc.vector.memset(thr[:], 0)
                nc.vector.memset(bit[:], 1 << 30)
                dve.wait_ge(xp_ready, 1)
                then(nc.vector.tensor_copy(xp[:], bank[4][:, 0:GT]))
                then(nc.vector.tensor_tensor(h_all[:], h_all[:], sb2[:].unsqueeze(1).to_broadcast([T2, NP, D]), ALU.add))
                n_steps = m[0]

                SEARCH = 5

                def search(q, base):
                    nc.vector.tensor_tensor(cand[:], thr[:], bit[:], ALU.bitwise_or).then_inc(step, 1)
                    dve.wait_ge(step, base + 1)
                    nc.vector.tensor_scalar(above[:], xp[:], cand[:].bitcast(F32), None, ALU.is_ge, ALU.add, accum_out=cnt[:]).then_inc(cnt_ready, 1)
                    dve.wait_ge(tot_ready, q + 1)
                    nc.vector.tensor_scalar(mask[:], bank[6][:, 0:1], CAP - 0.5, -1.0, ALU.is_ge, ALU.mult).then_inc(step, 1)
                    dve.wait_ge(step, base + 2)
                    nc.vector.tensor_tensor(cand[:], mask[:], bit[:], ALU.bitwise_and).then_inc(step, 1)
                    nc.vector.tensor_scalar(bit[:], bit[:], 1, None, ALU.logical_shift_right).then_inc(step, 1)
                    dve.wait_ge(step, base + 4)
                    nc.vector.tensor_tensor(thr[:], thr[:], cand[:], ALU.bitwise_or).then_inc(step, 1)
                    dve.wait_ge(step, base + 5)

                def shared(g, p, base, first=False):
                    for q in range(4):
                        search(4 * g + q, base + SEARCH * q)
                    dve.wait_ge(shy_ready, g + 1)
                    if not first:
                        dve.wait_ge(out_sent[p], 16 * ((g - p) // 2) if isinstance(g, int) else 8 * (g - p))
                    nc.vector.tensor_tensor(out_g[p][:], bank[5 + 2 * p][0:T2, :].rearrange("p (u c) -> p u c", u=TG),
                                            h_all[:, ds(TG * g, TG), :], ALU.add).then_inc(shy_taken, 1)

                shared(0, 0, n_steps, True)
                shared(1, 1, n_steps + 4 * SEARCH, True)
                with dve.Fori(1, NG // 2) as j:
                    for p in range(2):
                        shared(2 * j + p, p, n_steps + 4 * SEARCH * (2 * j + p))
                m[0] += 4 * SEARCH * NG

                t_f = thr[:].bitcast(F32)
                nc.vector.tensor_scalar(above[:], xp[:], t_f, None, ALU.is_gt, ALU.add, accum_out=col[:, 0:1])
                then(nc.vector.tensor_scalar(equal[:], xp[:], t_f, None, ALU.is_equal))
                then(nc.vector.tensor_tensor_scan(scan_e[:], equal[:], equal[:], 0.0, ALU.add, ALU.bypass))
                nc.vector.tensor_copy(col[:, 1:2], scan_e[:, GT - 1:GT]).then_inc(col_ready, 1)
                dve.wait_ge(off_ready, 1)
                then(nc.vector.tensor_scalar(col[:, 2:3], bank[6][:, 8:9], -1.0, float(CAP), ALU.mult, ALU.add))
                then(nc.vector.tensor_tensor(col[:, 2:3], col[:, 2:3], bank[6][:, 16:17], ALU.subtract))
                then(nc.vector.scalar_tensor_tensor(out=sel[:], in0=scan_e[:], scalar=col[:, 2:3], in1=equal[:], op0=ALU.is_le, op1=ALU.mult))
                then(nc.vector.tensor_tensor(sel[:], sel[:], above[:], ALU.add))
                then(nc.vector.tensor_tensor_scan(scan_s[:], sel[:], sel[:], 0.0, ALU.add, ALU.bypass))
                nc.vector.tensor_copy(col[:, 3:4], scan_s[:, GT - 1:GT]).then_inc(col_ready, 1)
                dve.wait_ge(off_ready, 2)
                then(nc.vector.tensor_scalar(col[:, 2:3], bank[6][:, 24:25], -256.0, None, ALU.add))
                nc.vector.scalar_tensor_tensor(out=scan_e[:], in0=scan_s[:], scalar=col[:, 2:3], in1=sel[:], op0=ALU.add, op1=ALU.mult).then_inc(slot_ready, 1)
                dve.wait_ge(slot_taken, 1)
                then(nc.vector.tensor_scalar(slot[:], bank[4][0:T2, :].rearrange("p (j m) -> p j m", j=TG), 255.0, None, ALU.add))
                nc.vector.tensor_scalar(slot_a[:], slot[:], 4, None, ALU.logical_shift_right)
                then(nc.vector.tensor_scalar(slot_b[:], slot[:], SB_ - 1, None, ALU.bitwise_and))
                for j in range(TG):
                    for o, a, w in ((hot_a, slot_a, SA), (hot_b, slot_b, SB_)):
                        nc.vector.tensor_tensor(o[:, j], a[:, j, :].rearrange("p (e c) -> p c e", e=E).unsqueeze(3).to_broadcast([T2, EC, E, w]),
                                                iota_slot[:, 0:w].unsqueeze(1).unsqueeze(1).to_broadcast([T2, EC, E, w]), ALU.is_equal).then_inc(step, 1)
                m[0] += 2 * TG
                dve.wait_ge(step, m[0])
                for j in range(TG):
                    flat = hot_a[:, j].rearrange("p c e a -> p c (e a)")
                    nc.vector.tensor_scalar(hot_ap[:, j].rearrange("p c e a -> p c (e a)"), flat, tok_col[:, 0:1], None, ALU.mult)
                    nc.vector.tensor_tensor(hot_at[:, j].rearrange("p c e a -> p c (e a)"), flat,
                                            tile_num[:, j, :].unsqueeze(2).to_broadcast([T2, EC, E * SA]), ALU.mult).then_inc(hot_ready, 1)
                dve.wait_ge(list_ready, 1)
                lb = bank[5][0:EG * SA, :].rearrange("p (g k m) -> p g k m", g=2, k=2)
                lt = list_t[:].rearrange("p g e b -> p g (e b)")
                then(nc.vector.tensor_scalar(lt, lb[:, :, 1, :], float(T2), None, ALU.mult))
                then(nc.vector.tensor_tensor(lt, lb[:, :, 0, :], lt, ALU.add))
                then(nc.vector.tensor_tensor(list_t[:], list_t[:], diag[:].unsqueeze(1).to_broadcast([EG * SA, 2, EG, SB_]), ALU.mult))
                nc.vector.tensor_reduce(list_s[:], list_t[:].rearrange("p g e b -> p g b e"), AX.X, ALU.add).then_inc(list_done, 1)
                dve.wait_ge(lr_ready, 1)
                nc.vector.tensor_copy(idx_all[:], bank[6][0:TH, 0:2 * E]).then_inc(lr_done, 1)

                def take_y(e, p, first=False):
                    dve.wait_ge(ey_ready, e + 1)
                    dve.wait_ge(ew_in[p], 64 * (e // RING + 1) if isinstance(e, int) else 16 * (e - p) + 64)
                    if not first:
                        dve.wait_ge(scattered, 32 * (e - RING + 1))
                    for s in range(2):
                        nc.vector.tensor_tensor(y[p][s][:], bank[3][0:TH, s * D:(s + 1) * D], b2[p][:], ALU.add).then_inc(ey_taken, 1)
                    for s in range(2):
                        dve.wait_ge(ey_taken, 2 * e + s + 1)
                        nc.vector.tensor_scalar(y[p][s][:], y[p][s][:], tok[p][s][:, ds(D + e, 1)], None, ALU.mult).then_inc(y_done, 1)

                for e in range(RING):
                    take_y(e, e, first=True)
                with dve.Fori(1, E // RING) as j:
                    for p in range(RING):
                        take_y(RING * j + p, p)

            @block.tensor
            def _(pe):
                pe.wait_ge(parts_done, 6)
                for k in range(7):
                    pe.wait_ge(hot_made, k + 1)
                    for n in range(4):
                        if 4 * k + n >= 2:
                            pe.wait_ge(bank_read, 4 * k + n - 1)
                        for s in range(2):
                            ins = nc.tensor.matmul(s_bank[n % 2][0:96, 0:343], bias_parts[:, s].rearrange("p a b -> p (a b)"),
                                                   onehot[k % 2][:, s, n * 343:(n + 1) * 343], start=(s == 0), stop=(s == 1))
                        ins.then_inc(bias_mm, 1)
                pe.wait_ge(set_dve, SETUP_STEPS)
                for h in range(H):
                    ins = nc.tensor.matmul(m_bank[h // 4][0:CA, (h % 4) * CA:(h % 4 + 1) * CA], q_aug[:, h, :], k_aug[:, h, :], start=True, stop=True)
                    if h % 4 == 3:
                        ins.then_inc(mat_ready, 1)

                def g_product(i, g, p, first=False):
                    if g == 0:
                        pe.wait_ge(x_in[p], 32 * (i // 2 + 1) if isinstance(i, int) else 16 * (i - p) + 32)
                    if first:
                        pe.wait_ge(mat_copied, 3)
                    elif isinstance(i, int) and i == 1:
                        pe.wait_ge(g_copied, g + 1)
                    elif g < 2:
                        pe.wait_ge(o_read, 2 * i - 3 + g)
                    elif not (isinstance(i, int) and i == 2):
                        pe.wait_ge(h_copied, i - 2)
                    xs = x_t[p][:, :].rearrange("c (b y x) -> c b y x", b=2, y=RES)[:, :, ::STRIDE, ::STRIDE]
                    for h in range(4):
                        ins = nc.tensor.matmul(m_bank[g][0:CA, h * T2:(h + 1) * T2].rearrange("c (b y x) -> c b y x", b=2, y=7),
                                               qk_mat[:, 4 * g + h, :], xs, start=True, stop=True)
                    ins.then_inc(g_ready, 1)

                def s_product(k, b, p, first=False, chunks=range(CH)):
                    for c in chunks:
                        m = chunk_rows(c)
                        if c % 2 == 0 and not first:
                            pe.wait_ge(ttr_done, CH * (k - 1) + min(c + 2, CH))
                        ins = nc.tensor.matmul(s_bank[c // 2][0:m, (c % 2) * N:(c % 2 + 1) * N], g_t[:, b, c * CR:c * CR + m],
                                               x_t[p][:, b * N:(b + 1) * N], start=True, stop=True)
                        if c % 2 == 1 or c == CH - 1:
                            ins.then_inc(s_ready, 1)

                def turn_probs(k, kp, f0, first=False, groups=range(3)):
                    for t in groups:
                        pe.wait_ge(exp_done, CH * k + min(2 * t + 2, CH))
                        if not (first and t < 2):
                            pe.wait_ge(pt_copied, 3 * k + t - 1)
                        for c in range(2 * t, min(2 * t + 2, CH)):
                            m = chunk_rows(c)
                            for s in range(2):
                                o = s * 2 * CR + (c - 2 * t) * CR
                                ins = nc.tensor.transpose(t_bank[(f0 + t) % 2][0:HALF, o:o + m], probs[0:m, kp, c, s * HALF:(s + 1) * HALF], ident[0:m, 0:m])
                        ins.then_inc(t_ready, 1)

                def px_product(k, b, p, f0, waits):
                    for a in range(2):
                        pe.wait_ge(pt_copied, 3 * k + 2 + a)
                        waits(a)
                        for s in range(2):
                            ins = nc.tensor.matmul(m_bank[(f0 + a) % 3][0:CA, 0:6 * NQ], x_n[p][:, 2 * b + s, :], p_t[:, s, a * 6 * NQ:(a + 1) * 6 * NQ],
                                                   start=(s == 0), stop=(s == 1))
                        ins.then_inc(px_ready, 1)

                def turn_a(i):
                    for a in range(2):
                        if a == 0:
                            pe.wait_ge(a_ready, i + 1)
                        for c in range(3):
                            ins = nc.tensor.transpose(m_bank[1 + a][:, c * T2:(c + 1) * T2], o_a[:, (3 * a + c) * 128:(3 * a + c + 1) * 128], ident[0:T2, 0:T2])
                        ins.then_inc(at_ready, 1)

                def project(i):
                    pe.wait_ge(at_copied, 2 * i + 2)
                    for c in range(DH // 128):
                        ins = nc.tensor.matmul(m_bank[2][0:T2, 0:D], a_t[:, c, :], proj[:, c, :], start=(c == 0), stop=(c == DH // 128 - 1))
                    ins.then_inc(h_ready, 1)

                def o_product(i, first):
                    for a in range(2):
                        pe.wait_ge(px_copied, 4 * i + 4)
                        if a == 1 and not first:
                            pe.wait_ge(at_copied, 2 * i - 1)
                        for h in range(6):
                            ins = nc.tensor.matmul(m_bank[a][0:T2, h * (VD + 1):(h + 1) * (VD + 1)], px_t[:, 6 * a + h, :], v_aug[:, 6 * a + h, :],
                                                   start=True, stop=True)
                        ins.then_inc(o_ready, 1)

                def body(i, p, first=False, last=False):
                    s_product(2 * i + 1, 1, p)
                    turn_probs(2 * i, 0, 0, first=first, groups=range(0, 2))
                    if not last:
                        g_product(i + 1, 0, 1 - p)
                    turn_probs(2 * i, 0, 0, groups=range(2, 3))
                    if not last:
                        g_product(i + 1, 1, 1 - p)
                        g_product(i + 1, 2, 1 - p)

                    def before_px0(a):
                        if not last:
                            pe.wait_ge(g_copied, 3 * (i + 1) + 1 + a)
                        else:
                            pe.wait_ge(o_read, 2 * i - 1 + a)
                    px_product(2 * i, 0, p, 0, before_px0)
                    turn_probs(2 * i + 1, 1, 3, groups=range(0, 2))
                    if not last:
                        pe.wait_ge(g_copied, 3 * (i + 1) + 3)
                        s_product(2 * i + 2, 0, 1 - p, chunks=range(0, 2))
                    turn_probs(2 * i + 1, 1, 3, groups=range(2, 3))
                    if not last:
                        s_product(2 * i + 2, 0, 1 - p, chunks=range(2, CH))

                    def before_px1(a):
                        if a == 1:
                            pe.wait_ge(px_copied, 4 * i + 1)
                        elif last:
                            pe.wait_ge(h_copied, i - 1)
                    px_product(2 * i + 1, 1, p, 2, before_px1)
                    if not first:
                        pe.wait_ge(px_copied, 4 * i + 3)
                        turn_a(i - 1)
                    o_product(i, first)
                    if not first:
                        project(i - 1)

                pe.wait_ge(ones_set, 4)
                for g in range(3):
                    g_product(0, g, 0, first=True)
                pe.wait_ge(g_copied, 3)
                pe.wait_ge(bank_read, 28)
                s_product(0, 0, 0, first=True)
                body(0, 0, first=True)
                body(1, 1)
                with pe.Fori(1, NP // 2 - 1) as j:
                    body(2 * j, 0)
                    body(2 * j + 1, 1)
                body(NP - 2, 0)
                body(NP - 1, 1, last=True)
                pe.wait_ge(o_read, 2 * NP)
                pe.wait_ge(h_copied, NP - 1)
                turn_a(NP - 1)
                project(NP - 1)

                pe.wait_ge(wts2_in, WTS2)
                pe.wait_ge(h_copied, NP)

                def turn_ln(g):
                    pe.wait_ge(ln_ready, g + 1)
                    for u in range(TG):
                        ins = nc.tensor.transpose(bank[0][:, u * T2:(u + 1) * T2], ln[:, u, :], ident[0:T2, 0:T2])
                    ins.then_inc(lt_ready, 1)

                def queries_keys(g, first=False):
                    pe.wait_ge(lt_copied, g + 1)
                    if not first:
                        pe.wait_ge(qm_made, TG * g)
                    nc.tensor.matmul(bank[1][:, 0:GT], w_q[:], ln_t[:], start=True, stop=True).then_inc(q_ready, 1)
                    nc.tensor.matmul(bank[2][:, 0:GT], w_k[:], ln_t[:], start=True, stop=True).then_inc(k_ready, 1)

                def values_gate(g):
                    for a in range(2):
                        for u in range(2):
                            ins = nc.tensor.matmul(bank[3 + a][0:T2, u * 2 * D:(u + 1) * 2 * D], ln_t[:, (2 * a + u) * T2:(2 * a + u + 1) * T2], w_vg[:],
                                                   start=True, stop=True)
                        ins.then_inc(vg_ready, 1)

                def scores(g, u, first=False):
                    k = TG * g + u
                    if u == 0:
                        pe.wait_ge(k_copied, g + 1)
                    pe.wait_ge(qm_made, k + 1)
                    for a, (taken, ready) in enumerate(((sa_done, sa_ready), (sb_copied, sb_ready))):
                        if not (first and u == 0):
                            pe.wait_ge(taken, k)
                        nc.tensor.matmul(bank[5 + a][0:T2, 0:GT], k_t[:, u * T2:(u + 1) * T2], q_heads[u % 2][:, 4 * a:4 * a + 4, :],
                                         start=True, stop=True).then_inc(ready, 1)

                def values(g, u, first=False):
                    k = TG * g + u
                    pe.wait_ge(sa_done, k + 1)
                    pe.wait_ge(sb_done, k + 1)
                    if u == 0:
                        pe.wait_ge(vg_copied, 2 * g + 2)
                        if not first:
                            pe.wait_ge(ret_copied, g)
                    for h in range(RH):
                        ins = nc.tensor.matmul(bank[7][0:T2, u * D + h * RD:u * D + (h + 1) * RD], sc[u % 2][:, h, :],
                                               v_sb[:, u, h * RD:(h + 1) * RD], start=True, stop=True)
                    ins.then_inc(pv_ready, 1)

                def retention(g, first=False, last=False):
                    scores(g, 0, first)
                    scores(g, 1)
                    values(g, 0, first)
                    scores(g, 2)
                    values(g, 1)
                    scores(g, 3)
                    if not last:
                        turn_ln(g + 1)
                    values(g, 2)
                    if not last:
                        queries_keys(g + 1)
                    values(g, 3)
                    if not last:
                        values_gate(g + 1)

                turn_ln(0)
                queries_keys(0, first=True)
                values_gate(0)
                retention(0, first=True)
                with pe.Fori(1, NG - 1) as g:
                    retention(g)
                retention(NG - 1, last=True)

                def turn_z(g, p, first=False):
                    pe.wait_ge(zs_ready, g + 1)
                    if not first:
                        pe.wait_ge(zt_copied, g)
                    for u in range(TG):
                        ins = nc.tensor.transpose(bank[0][:, u * T2:(u + 1) * T2], z[p][:, u, :], ident[0:T2, 0:T2])
                    ins.then_inc(zt_ready, 1)

                def out_projection(g, p, first=False):
                    pe.wait_ge(zt_copied, g + 1)
                    if not first:
                        pe.wait_ge(h2_done, g - 1)
                    for u in range(TG):
                        ins = nc.tensor.matmul(bank[1 + 2 * p][0:T2, u * D:(u + 1) * D], z_t[p][:, u * T2:(u + 1) * T2], w_o[:], start=True, stop=True)
                    ins.then_inc(wo_ready, 1)

                turn_z(0, 0, first=True)
                turn_z(1, 1)
                out_projection(0, 0, first=True)
                turn_z(2, 0)
                out_projection(1, 1, first=True)
                with pe.Fori(1, NG // 2 - 1) as j:
                    for p in range(2):
                        turn_z(2 * j + p + 1, 1 - p)
                        out_projection(2 * j + p, p)
                turn_z(NG - 1, 1)
                out_projection(NG - 2, 0)
                out_projection(NG - 1, 1)

                def turn_hn(g, p, first=False):
                    pe.wait_ge(hn_ready, g + 1)
                    if not first:
                        pe.wait_ge(hnt_copied, g - 1)
                    for u in range(TG):
                        ins = nc.tensor.transpose(bank[2 * p][:, u * T2:(u + 1) * T2], hn[p][:, u, :], ident[0:T2, 0:T2])
                    ins.then_inc(hnt_ready, 1)

                def gate(g, p, first=False):
                    pe.wait_ge(hng_copied, g + 1)
                    if first:
                        pe.wait_ge(h2_done, NG)
                    else:
                        pe.wait_ge(lg_done, g - 1)
                    for u in range(TG):
                        ins = nc.tensor.matmul(bank[1 + 2 * p][0:T2, u * E:(u + 1) * E], hn_g[p][:, u * T2:(u + 1) * T2], gate_w[:], start=True, stop=True)
                    ins.then_inc(lg_ready, 1)

                turn_hn(0, 0, first=True)
                turn_hn(1, 1, first=True)
                gate(0, 0, first=True)
                turn_hn(2, 0)
                gate(1, 1, first=True)
                with pe.Fori(1, NG // 2 - 1) as j:
                    for p in range(2):
                        turn_hn(2 * j + p + 1, 1 - p)
                        gate(2 * j + p, p)
                turn_hn(NG - 1, 1)
                gate(NG - 2, 0)
                gate(NG - 1, 1)

                pe.wait_ge(pr_ready, 2)
                for j in range(TG):
                    ins = nc.tensor.transpose(bank[4][:, j * T2:(j + 1) * T2],
                                              prob_j[:, j, :], ident[0:T2, 0:T2])
                ins.then_inc(xp_ready, 1)

                def shared(g, p, first=False):
                    def total(q):
                        pe.wait_ge(cnt_ready, 4 * g + q + 1)
                        nc.tensor.matmul(bank[6][:, 0:1], same_expert[:], cnt[:], start=True, stop=True).then_inc(tot_ready, 1)

                    for c in range(HC):
                        if not first:
                            pe.wait_ge(sh_gelu, HC * (g - 1) + c + 1)
                        nc.tensor.matmul(bank[c][:, 0:GT], sw1[:, c * 128:(c + 1) * 128], hn_t[:, ds(GT * g, GT)], start=True, stop=True).then_inc(sh_ready, 1)
                        if c % 2:
                            total(c // 2)
                    pe.wait_ge(sh_gelu, HC * g + HC)
                    if not first:
                        pe.wait_ge(shy_taken, g)
                    for u in range(TG):
                        for c in range(HC):
                            ins = nc.tensor.matmul(bank[5 + 2 * p][0:T2, u * D:(u + 1) * D], hid[p][:, c, u * T2:(u + 1) * T2], sw2[:, c, :],
                                                   start=(c == 0), stop=(c == HC - 1))
                        if u == 1:
                            total(2)
                    ins.then_inc(shy_ready, 1)
                    total(3)

                pe.wait_ge(xp_ready, 1)
                shared(0, 0, first=True)
                shared(1, 1)
                with pe.Fori(1, NG // 2) as j:
                    for p in range(2):
                        shared(2 * j + p, p)

                pe.wait_ge(col_ready, 1)
                nc.tensor.matmul(bank[6][:, 8:9], same_expert[:], col[:, 0:1], start=True, stop=True)
                nc.tensor.matmul(bank[6][:, 16:17], before[:], col[:, 1:2], start=True, stop=True).then_inc(off_ready, 1)
                pe.wait_ge(col_ready, 2)
                nc.tensor.matmul(bank[6][:, 24:25], before[:], col[:, 3:4], start=True, stop=True).then_inc(off_ready, 1)
                pe.wait_ge(slot_ready, 1)
                for j in range(TG):
                    ins = nc.tensor.transpose(bank[4][0:T2, j * 128:(j + 1) * 128], scan_e[:, j * T2:(j + 1) * T2], ident[:])
                ins.then_inc(slot_taken, 1)
                pe.wait_ge(hot_ready, TG)
                pe.wait_ge(shy_taken, NG)
                for g in range(2):
                    for k, hot in enumerate((hot_ap, hot_at)):
                        for j in range(TG):
                            for c in range(EC):
                                ins = nc.tensor.matmul(bank[5][0:EG * SA, (2 * g + k) * 128:(2 * g + k + 1) * 128],
                                                       hot[:, j, c, g * EG:(g + 1) * EG, :].rearrange("p e a -> p (e a)"),
                                                       hot_b[:, j, c, g * EG:(g + 1) * EG, :].rearrange("p e b -> p (e b)"),
                                                       start=(j == 0 and c == 0), stop=(j == TG - 1 and c == EC - 1))
                ins.then_inc(list_ready, 1)
                pe.wait_ge(list_in, 32)
                nc.tensor.transpose(bank[6][0:TH, 0:2 * E], list_r[:], ident[0:2 * E, 0:2 * E]).then_inc(lr_ready, 1)

                def turn_tok(e, p):
                    pe.wait_ge(tok_in[p], 32 * (e // RING + 1) if isinstance(e, int) else (32 // RING) * (e - p) + 32)
                    for s in range(2):
                        ins = nc.tensor.transpose(bank[0][:, s * TH:(s + 1) * TH], tok[p][s][:, 0:D], ident[0:TH, 0:TH])
                    ins.then_inc(tt_ready, 1)

                def hidden(e, p, first=False):
                    pe.wait_ge(ew_in[p], 64 * (e // RING + 1) if isinstance(e, int) else 16 * (e - p) + 64)
                    pe.wait_ge(tt_copied, e + 1)
                    for c in range(HC):
                        if not first and c % 2 == 0:
                            pe.wait_ge(eh_gelu, HC * (e - 1) + c + 2)
                        ins = nc.tensor.matmul(bank[1 + c // 2][:, (c % 2) * CAP:(c % 2 + 1) * CAP], w1[p][:, c * 128:(c + 1) * 128], tok_t[p % 2][:],
                                               start=True, stop=True)
                        if c % 2:
                            ins.then_inc(eh_ready, 1)

                def output(e, p, first=False):
                    pe.wait_ge(eh_gelu, HC * e + HC)
                    if not first:
                        pe.wait_ge(ey_taken, 2 * e)
                    for s in range(2):
                        for c in range(HC):
                            ins = nc.tensor.matmul(bank[3][0:TH, s * D:(s + 1) * D], ehid[p % 2][:, c, s * TH:(s + 1) * TH], w2[p][:, c, :],
                                                   start=(c == 0), stop=(c == HC - 1))
                    ins.then_inc(ey_ready, 1)

                turn_tok(0, 0)
                hidden(0, 0, first=True)
                turn_tok(1, 1)
                hidden(1, 1)
                turn_tok(2, 2)
                output(0, 0, first=True)
                hidden(2, 2)
                turn_tok(3, 3)
                output(1, 1)
                with pe.Fori(1, E // RING) as j:
                    for p in range(RING):
                        e = RING * j + p
                        hidden(e - 1, (p - 1) % RING)
                        output(e - 2, (p - 2) % RING)
                        turn_tok(e, p)
                hidden(E - 1, RING - 1)
                output(E - 2, RING - 2)
                output(E - 1, RING - 1)


WTS2 = 19 * 16
SETUP_STEPS = 22


def chunk_cols(t):
    return sum(chunk_rows(c) for c in range(2 * t, min(2 * t + 2, CH)))


def constants():
    f = np.float32
    t = np.arange(T2)
    diff = (t[None, :] - t[:, None]).astype(f)
    causal = (diff >= 0) & (t[None, :] // NQ == t[:, None] // NQ)
    gammas = 1.0 - np.exp2(-5.0 - np.arange(RH, dtype=f))
    decay = np.where(causal[:, None], np.exp(diff[:, None] * np.log(gammas)[None, :, None]), 0.0) / np.sqrt(f(RD))
    r = np.arange(128)
    same = r[:, None] // EC == r[None, :] // EC
    return {
        "decay": decay.astype(f),
        "head_mask": (np.arange(D)[:, None] // RD == np.arange(RH)[None, :]).astype(f),
        "same_expert": same.astype(f),
        "before": (same & (r[:, None] < r[None, :])).astype(f),
        "iota_slot": np.tile(np.arange(SB_, dtype=f), (T2, 1)),
        "tok_col": np.arange(T2, dtype=f)[:, None],
        "tile_num": np.tile((TG * np.arange(EC)[None, :] + np.arange(TG)[:, None]).astype(f)[None], (T2, 1, 1)),
        "diag": np.repeat((np.arange(EG * SA)[:, None] // SA == np.arange(EG)[None, :]).astype(f)[:, :, None], SB_, 2),
    }


def kernel(**inputs):
    import concourse.bacc as _bacc
    from concourse import mybir as _mybir
    from concourse.bass_utils import run_bass_kernel_spmd as _run

    a = {k: np.asarray(v) for k, v in inputs.items()}
    kv = a["L0_tok_kv_w"].reshape(H, KD + VD, C)

    def per_head(name, lo, hi):
        return a["L0_tok_kv_" + name].reshape(H, KD + VD)[:, lo:hi]

    arrays = {
        "x": a["x"],
        "x_t": a["x"].reshape(B * N, C).T,
        "idx": a["L0_tok_bias_idxs"],
        "bias_cols": a["L0_tok_attention_biases"].T.reshape(2, HALF, H).transpose(1, 0, 2),
        "iota_off": np.arange(NOFF, dtype=np.float32).reshape(2, HALF).T,
        "ident": np.eye(128, dtype=np.float32),
        "q_w": a["L0_tok_q_w"].reshape(H, KD, C).transpose(1, 0, 2),
        "k_w": kv[:, :KD].transpose(1, 0, 2),
        "v_w": kv[:, KD:].transpose(2, 0, 1).reshape(C, DH),
        "proj": a["L0_tok_proj_w"].T.reshape(DH // 128, 128, D).transpose(1, 0, 2),
        "w_q": a["L0_attn_W_Q"], "w_k": a["L0_attn_W_K"], "w_o": a["L0_attn_W_O"],
        "w_vg": np.concatenate([a["L0_attn_W_V"], a["L0_attn_W_G"]], 1),
        "gn_w": a["L0_attn_gn_weight"], "gn_b": a["L0_attn_gn_bias"],
        "gate_w": a["L0_ffn_gate_w"], "sw1": a["L0_ffn_sw1"],
        "sw2": a["L0_ffn_sw2"].reshape(HC, 128, D).transpose(1, 0, 2),
        "sb1": a["L0_ffn_sb1"].reshape(HC, 128).T, "sb2": a["L0_ffn_sb2"],
        "w1": a["L0_ffn_w1"], "w2": a["L0_ffn_w2"].reshape(E, HC, 128, D).transpose(0, 2, 1, 3),
        "b1": a["L0_ffn_b1"].reshape(E, HC, 128).transpose(0, 2, 1), "b2": a["L0_ffn_b2"],
        **constants(),
        "par_qk": np.stack([np.concatenate([a["L0_tok_q_" + n].reshape(H, KD).T, per_head(n, 0, KD).T], 1) for n in "gbmv"], 1),
        "par_v": np.stack([np.concatenate([per_head(n, KD, KD + VD).reshape(-1), a["L0_tok_proj_" + n]]) for n in "gbmv"]),
    }
    nc = _bacc.Bacc("TRN2", target_bir_lowering=False, num_devices=1)
    feed, d = {}, {}
    for name, v in arrays.items():
        v = np.ascontiguousarray(v)
        feed[f"in_{name}_dram"] = v
        d[name] = nc.dram_tensor(f"in_{name}_dram", v.shape, _mybir.dt.from_np(v.dtype), kind="ExternalInput").ap()
    out = nc.dram_tensor("out_dram", (T, D), F32, kind="ExternalOutput").ap()
    build(nc, d, out)
    r = _run(nc, [feed], core_ids=[0])
    return r.results[0]["out_dram"].reshape(B, NQ, D)
```

```python
import math
from contextlib import ExitStack

import numpy as np

import concourse.bass as bass
from concourse import mybir

F32 = mybir.dt.float32
BF16 = mybir.dt.bfloat16
I32 = mybir.dt.int32
ALU = mybir.AluOpType
ACT = mybir.ActivationFunctionType
AX = mybir.AxisListType
ds = bass.ds

B, RES, STRIDE = 64, 14, 2
N = RES * RES
NQ = (RES // STRIDE) ** 2
C = 96
CA = C + 1
H, KD, VD = 12, 32, 64
DH = H * VD
NOFF = N
HALF = N // 2
ROWS = H * NQ
CH = 5
CR = -(-ROWS // CH)
D = 128
T2 = 2 * NQ
NP = B // 2
T = B * NQ
EPS = 1e-5

RH, RD = 8, 16
TG = 4
NG = NP // TG
GT = TG * T2

E = 16
HID = 512
HC = HID // 128
CAP = T // E
TH = CAP // 2
EC = 8
ROW = D + E
SA, SB_ = -(-CAP // 16), 16
SLOTS = SA * SB_
RING = 4
EG = 8


def chunk_rows(c):
    return min(CR, ROWS - c * CR)


def build(nc, d, out):
    with ExitStack() as ctx:
        tok_scope = ExitStack()
        scope = [ctx]

        def sb(name, shape, dt=F32):
            return scope[0].enter_context(nc.sbuf_tensor(name, shape, dt))

        def sem(name):
            return ctx.enter_context(nc.semaphore(name))

        psum = ctx.enter_context(nc.psum_tensor("psum", [128, 8, 512], F32))
        bank = [psum[:, k, :] for k in range(8)]
        s_bank, t_bank, m_bank = bank[0:3], bank[3:5], bank[5:8]

        prob_rows = nc.dram_tensor("prob_rows", [T, ROW], F32).ap()
        list_d = nc.dram_tensor("list_scratch", [E, SLOTS], F32).ap()
        bias_d = nc.dram_tensor("bias_scratch", [3, H, NQ * N], F32).ap()

        ident = sb("ident", [128, 128])
        w_q, w_k, w_o = (sb(n, [D, D]) for n in ("w_q", "w_k", "w_o"))
        w_vg = sb("w_vg", [D, 2 * D])
        head_mask = sb("head_mask", [D, RH])
        decay = sb("decay", [T2, RH, T2])
        gn_w, gn_b = sb("gn_w", [T2, D]), sb("gn_b", [T2, D])
        gate_w = sb("gate_w", [D, E])
        sw1, sw2 = sb("sw1", [D, HID]), sb("sw2", [128, HC, D])
        sb1, sb2 = sb("sb1", [128, HC]), sb("sb2", [T2, D])
        same_expert = sb("same_expert", [128, 128])
        before = sb("before", [128, 128])
        iota_slot = sb("iota_slot", [T2, SB_])
        tok_col = sb("tok_col", [T2, 1])
        tile_num = sb("tile_num", [T2, TG, EC])
        diag = sb("diag", [EG * SA, EG, SB_])
        h_all = sb("h_all", [T2, NP, D])
        stats = sb("stats", [T2, TG, 6])
        mean_var = sb("mean_var", [T2, TG, 2])
        rstd = sb("rstd", [T2, TG])
        ln = sb("ln", [T2, TG, D])
        scope[0] = tok_scope
        iota_off = sb("iota_off", [HALF, 2])
        bias_cols = sb("bias_cols", [HALF, 2, H])
        q_w = sb("q_w", [KD, H, C])
        k_w = sb("k_w", [KD, H, C])
        par_qk = sb("par_qk", [KD, 4, 2 * H])
        s_qk = sb("s_qk", [KD, 2, 2 * H])
        q_aug = sb("q_aug", [KD, H, CA])
        k_aug = sb("k_aug", [KD, H, CA])
        qk_mat = sb("qk_mat", [CA, H, CA])
        NV = (DH + D) // 128
        par_v = sb("par_v", [128, 4, NV])
        s_v = sb("s_v", [128, 2, NV])
        s_diag = sb("s_diag", [128, 2, NV, 128])
        ones = sb("ones", [128, 128])
        proj_shift = sb("proj_shift", [T2, D])
        v_w = sb("v_w", [C, DH])
        v_aug = sb("v_aug", [CA, H, VD + 1])
        proj = sb("proj", [128, DH // 128, D])
        idx_i = sb("idx_i", [7, 7 * N], I32)
        idx_bf = sb("idx_bf", [7, 7 * N], BF16)
        pick_row = sb("pick_row", [7, 7, HALF], BF16)
        onehot = [sb(f"onehot{p}", [HALF, 2, 7 * N], BF16) for p in range(2)]
        bias_rest = sb("bias_rest", [HALF, 2, H])
        bias_parts = sb("bias_parts", [HALF, 2, 3, 32], BF16)
        bias_out = sb("bias_out", [96, 2, 7 * N])
        bias_neg = sb("bias_neg", [CR, CH, N])
        bias_low = sb("bias_low", [CR, 2, CH, N])

        x_t = [sb(f"x_t{p}", [CA, 2 * N]) for p in range(2)]
        x_n = [sb(f"x_n{p}", [HALF, 4, CA]) for p in range(2)]
        g_t = sb("g_t", [CA, 2, ROWS])
        probs = sb("probs", [CR, 2, CH, N])
        neg_max = sb("neg_max", [CR, 2, CH])
        p_t = sb("p_t", [HALF, 2, ROWS])
        px_t = sb("px_t", [CA, H, T2])
        o_rec = sb("o_rec", [T2, 2, H // 2])
        o_sb = sb("o_sb", [T2, DH])
        o_u = sb("o_u", [T2, DH])
        o_a = sb("o_a", [T2, DH])
        three = sb("three", [T2, 1])
        a_t = sb("a_t", [128, DH // 128, T2])
        tok_scope.close()
        scope[0] = ctx

        hn_t = sb("hn_t", [D, T])
        hn_g = [sb(f"hn_g{p}", [D, GT]) for p in range(2)]
        rows = sb("rows", [T2, NP, ROW])
        logit = sb("logit", [T2, NP, E])
        lmax, lsum = sb("lmax", [T2, NP]), sb("lsum", [T2, NP])
        stats2 = [sb(f"stats2{p}", [T2, TG, 6]) for p in range(2)]
        mean_var2 = [sb(f"mean_var2{p}", [T2, TG, 2]) for p in range(2)]
        mean_all, rstd_all = sb("mean_all", [T2, NP]), sb("rstd_all", [T2, NP])
        hn = [sb(f"hn{p}", [T2, TG, D]) for p in range(2)]
        ret_scope = ExitStack()
        scope[0] = ret_scope
        ln_t = sb("ln_t", [D, GT])
        k_t = sb("k_t", [D, GT])
        v_sb = sb("v_sb", [T2, TG, D])
        gate_all = sb("gate_all", [T2, NP, D])
        q_heads = [sb(f"q_heads{p}", [D, RH, T2]) for p in range(2)]
        sc_tmp = sb("sc_tmp", [T2, RH // 2, T2])
        sc = [sb(f"sc{p}", [T2, RH, T2]) for p in range(2)]
        ret = sb("ret", [T2, TG * RH, RD])
        ret_c = sb("ret_c", [T2, TG * RH, RD])
        ret_sq = sb("ret_sq", [T2, TG * RH, RD])
        ret_n = sb("ret_n", [T2, TG, D])
        gmean = sb("gmean", [T2, TG * RH])
        gstd = sb("gstd", [T2, TG * RH])
        z = [sb(f"z{p}", [T2, TG, D]) for p in range(2)]
        z_t = [sb(f"z_t{p}", [D, GT]) for p in range(2)]
        ret_scope.close()
        scope[0] = ctx
        prob_j = sb("prob_j", [T2, TG, E * EC])
        xp = sb("xp", [128, GT])
        thr = sb("thr", [128, 1], I32)
        digit = sb("digit", [128, 2, 3], I32)
        cand, mask, flip = (sb(n, [128, 3], I32) for n in ("cand", "mask", "flip"))
        cnt = sb("cnt", [128, 3])
        above, equal, scan_e, sel, scan_s = (sb(n, [128, GT]) for n in ("above", "equal", "scan_e", "sel", "scan_s"))
        col = sb("col", [128, 4])
        hid = [sb(f"hid{p}", [128, HC, GT]) for p in range(2)]
        out_g = [sb(f"out_g{p}", [T2, TG, D]) for p in range(2)]
        slot = sb("slot", [T2, TG, 128], I32)
        slot_a, slot_b = sb("slot_a", [T2, TG, 128], I32), sb("slot_b", [T2, TG, 128], I32)
        hot_a = sb("hot_a", [T2, TG, EC, E, SA], BF16)
        hot_at = sb("hot_at", [T2, TG, EC, E, SA], BF16)
        hot_ap = sb("hot_ap", [T2, TG, EC, E, SA], BF16)
        hot_b = sb("hot_b", [T2, TG, EC, E, SB_], BF16)
        list_t = sb("list_t", [EG * SA, 2, EG, SB_])
        list_s = sb("list_s", [EG * SA, 2, SB_])
        list_r = sb("list_r", [2 * E, TH])
        idx_all = sb("idx_all", [TH, 2 * E], I32)
        idx_from = [sb(f"idx_from{p}", [TH, 2], I32) for p in range(RING)]
        idx_to = [sb(f"idx_to{p}", [TH, 2], I32) for p in range(RING)]
        tok = [[sb(f"tok{p}{s}", [TH, ROW]) for s in range(2)] for p in range(RING)]
        tok_t = [sb(f"tok_t{p}", [D, CAP]) for p in range(2)]
        w1 = [sb(f"w1{p}", [D, HID]) for p in range(RING)]
        w2 = [sb(f"w2{p}", [128, HC, D]) for p in range(RING)]
        b1 = [sb(f"b1{p}", [128, HC]) for p in range(RING)]
        b2 = [sb(f"b2{p}", [TH, D]) for p in range(RING)]
        ehid = [sb(f"ehid{p}", [128, HC, CAP]) for p in range(2)]
        y = [[sb(f"y{p}{s}", [TH, D]) for s in range(2)] for p in range(RING)]

        small_in, wts2_in = sem("small_in"), sem("wts2_in")
        names = ("step ln_step gn_step stat_step var_ready std_ready ln_ready lt_ready lt_copied q_ready k_ready k_copied vg_ready vg_copied qm_made "
                 "sa_ready sb_ready sb_copied sa_done sb_done pv_ready ret_copied c_ready sq_ready gvar_ready gstd_ready gn_ready "
                 "pool_step z_done zs_ready zt_ready zt_copied wo_ready h2_done stats_done aggr_done sb2_added l_var l_std hn_ready hnt_ready hnt_copied hng_copied "
                 "rows_copied lg_ready lg_done lx_ready le_ready pr_ready xp_ready xp_copied sh_ready sh_gelu shy_ready shy_taken out_ready "
                 "cnt_ready tot_ready col_ready off_ready slot_ready slot_taken hot_ready made_a made_b slots_split place_ready tile_even tile_odd list_ready list_done lr_ready lr_done "
                 "table_out list_out list_in idx_copied tt_ready tt_copied eh_ready eh_gelu ey_ready ey_taken y_done "
                 "scattered").split()
        (step, ln_step, gn_step, stat_step, var_ready, std_ready, ln_ready, lt_ready, lt_copied, q_ready, k_ready, k_copied, vg_ready, vg_copied, qm_made,
         sa_ready, sb_ready, sb_copied, sa_done, sb_done, pv_ready, ret_copied, c_ready, sq_ready, gvar_ready, gstd_ready, gn_ready,
         pool_step, z_done, zs_ready, zt_ready, zt_copied, wo_ready, h2_done, stats_done, aggr_done, sb2_added, l_var, l_std, hn_ready, hnt_ready, hnt_copied, hng_copied,
         rows_copied, lg_ready, lg_done, lx_ready, le_ready, pr_ready, xp_ready, xp_copied, sh_ready, sh_gelu, shy_ready, shy_taken, out_ready,
         cnt_ready, tot_ready, col_ready, off_ready, slot_ready, slot_taken, hot_ready, made_a, made_b, slots_split, place_ready, tile_even, tile_odd, list_ready, list_done, lr_ready, lr_done,
         table_out, list_out, list_in, idx_copied, tt_ready, tt_copied, eh_ready, eh_gelu, ey_ready, ey_taken, y_done,
         scattered) = (sem(n) for n in names)
        out_sent = [sem(f"out_sent{p}") for p in range(2)]
        tok_in = [sem(f"tok_in{p}") for p in range(RING)]
        ew_in = [sem(f"ew_in{p}") for p in range(RING)]
        out_rows = out.rearrange("(i p) c -> p i c", p=T2)

        const_in = sem("const_in")
        par_in, wts_in = sem("par_in"), sem("wts_in")
        bias_back = sem("bias_back")
        bias_stored = [sem(f"bias_stored{p}") for p in range(2)]
        ones_set, ones_made = sem("ones_set"), sem("ones_made")
        idx_spread, scale_ready = sem("idx_spread"), sem("scale_ready")
        x_in = [sem(f"x_in{p}") for p in range(2)]
        set_dve = sem("set_dve")
        set_act = sem("set_act")
        bank_read, parts_done = sem("bank_read"), sem("parts_done")
        mat_ready = sem("mat_ready")
        mat_copied = sem("mat_copied")
        hot_made, idx_cast = sem("hot_made"), sem("idx_cast")
        bias_mm = sem("bias_mm")
        bias_copied = sem("bias_copied")
        g_ready, g_copied = sem("g_ready"), sem("g_copied")
        s_ready, s_taken = sem("s_ready"), sem("s_taken")
        ttr_done, exp_done = sem("ttr_done"), sem("exp_done")
        t_ready, pt_copied = sem("t_ready"), sem("pt_copied")
        px_ready, px_copied = sem("px_ready"), sem("px_copied")
        o_ready, o_read, o_rec_done = sem("o_ready"), sem("o_read"), sem("o_rec_done")
        u_ready, a_ready = sem("u_ready"), sem("a_ready")
        at_ready, at_copied = sem("at_ready"), sem("at_copied")
        h_ready, h_copied = sem("h_ready"), sem("h_copied")
        dve_waited, pool_waited = sem("dve_waited"), sem("pool_waited")

        idx_flat = d["idx"].rearrange("q k -> (q k)")
        W7 = 7 * N

        def row_of_h(g):
            return h_all[:, g, :]

        with nc.Block() as block:
            @block.sync
            def _(sp):
                sp.dma_start(iota_off[:], d["iota_off"]).then_inc(const_in, 16)
                sp.dma_start(bias_cols[:], d["bias_cols"]).then_inc(const_in, 16)
                sp.dma_start(ident[:], d["ident"]).then_inc(const_in, 16)
                sp.dma_start(idx_i[:], idx_flat.rearrange("(k n) -> k n", k=7)).then_inc(const_in, 16)
                sp.dma_start(par_qk[:], d["par_qk"]).then_inc(par_in, 16)
                sp.dma_start(par_v[:], d["par_v"]).then_inc(par_in, 16)
                sp.dma_start(q_w[:], d["q_w"]).then_inc(wts_in, 16)
                sp.dma_start(k_w[:], d["k_w"]).then_inc(wts_in, 16)
                sp.dma_start(v_w[:], d["v_w"]).then_inc(wts_in, 16)
                sp.dma_start(proj[:], d["proj"]).then_inc(wts_in, 16)

                def load_x(i, p):
                    sp.dma_start(x_t[p][0:C, :], d["x_t"][:, ds(i * 2 * N, 2 * N)]).then_inc(x_in[p], 16)
                    sp.dma_start(x_n[p][:, :, 0:C],
                                 d["x"][ds(i * 2, 2)].rearrange("b (s p) c -> p (b s) c", s=2)).then_inc(x_in[p], 16)

                load_x(0, 0)
                load_x(1, 1)
                for k in range(2, 9):
                    sp.wait_ge(bias_copied, k - 1)
                    for part in range(3):
                        sp.dma_start(bias_d[part, :, (k - 2) * W7:(k - 1) * W7],
                                     bias_out[32 * part:32 * part + H, k % 2, :]).then_inc(bias_stored[k % 2], 16)
                sp.wait_ge(bias_stored[0], 4 * 48)
                sp.wait_ge(bias_stored[1], 3 * 48)
                for part, o in ((0, bias_neg[:]), (1, bias_low[:, 0]), (2, bias_low[:, 1])):
                    flat = bias_d[part].rearrange("h (q k) -> (h q) k", k=N)
                    sp.dma_start(o[:, 0:CH - 1, :], flat[0:(CH - 1) * CR].rearrange("(c p) k -> p c k", p=CR)).then_inc(bias_back, 16)
                    sp.dma_start(o[0:chunk_rows(CH - 1), CH - 1, :], flat[(CH - 1) * CR:ROWS]).then_inc(bias_back, 16)
                for o, n in ((w_q, "w_q"), (w_k, "w_k"), (w_vg, "w_vg"), (w_o, "w_o"), (head_mask, "head_mask"), (decay, "decay"),
                             (gate_w, "gate_w"), (sw1, "sw1"), (sw2, "sw2"), (sb1, "sb1"), (same_expert, "same_expert"),
                             (before, "before"), (iota_slot, "iota_slot"), (tok_col, "tok_col"), (tile_num, "tile_num"), (diag, "diag")):
                    sp.dma_start(o[:], d[n]).then_inc(wts2_in, 16)
                for o, n in ((gn_w, "gn_w"), (gn_b, "gn_b"), (sb2, "sb2")):
                    sp.dma_start(o[:], d[n].partition_broadcast(T2)).then_inc(wts2_in, 16)
                with sp.Fori(1, NP // 2) as j:
                    for p in range(2):
                        sp.wait_ge(o_ready, 2 * (2 * j + p) - 2)
                        load_x(2 * j + p, p)
                sp.wait_ge(h_copied, NP)
                sp.wait_ge(rows_copied, NG)
                sp.wait_ge(pr_ready, 1)
                sp.dma_start(prob_rows.rearrange("(i p) c -> p i c", p=T2), rows[:, :, :]).then_inc(table_out, 16)

                def load_expert(e, p):
                    sp.dma_start(w1[p][:], d["w1"][ds(e, 1)].rearrange("e d h -> (e d) h")).then_inc(ew_in[p], 16)
                    sp.dma_start(w2[p][:], d["w2"][ds(e, 1)].rearrange("e k c n -> (e k) c n")).then_inc(ew_in[p], 16)
                    sp.dma_start(b1[p][:], d["b1"][ds(e, 1)].rearrange("e k c -> (e k) c")).then_inc(ew_in[p], 16)
                    sp.dma_start(b2[p][:], d["b2"][ds(e, 1)].rearrange("e n -> (e n)").partition_broadcast(TH)).then_inc(ew_in[p], 16)

                for e in range(RING):
                    load_expert(e, e)
                with sp.Fori(0, NG // 2) as j:
                    for p in range(2):
                        sp.wait_ge(out_ready, 2 * j + p + 1)
                        sp.dma_start(out_rows[:, ds((2 * j + p) * TG, TG), :], out_g[p][:]).then_inc(out_sent[p], 16)
                sp.wait_ge(list_done, 1)
                sp.dma_start(list_d.rearrange("(g e) (a b) -> (e a) g b", g=2, a=SA), list_s[:]).then_inc(list_out, 16)
                sp.wait_ge(list_out, 16)
                for s in range(2):
                    sp.dma_start(list_r[s * E:(s + 1) * E, :], list_d[:, s * TH:(s + 1) * TH]).then_inc(list_in, 16)
                with sp.Fori(1, E // RING) as j:
                    for p in range(RING):
                        sp.wait_ge(y_done, 2 * (RING * (j - 1) + p + 1))
                        load_expert(RING * j + p, p)
                sp.wait_ge(scattered, 2 * 16 * E)

            @block.gpsimd
            def _(pool):
                for p in range(2):
                    if p:
                        pool.wait_ge(ones_set, 2 * p)
                    nc.gpsimd.memset(x_t[p][C:CA, :], 1.0).then_inc(ones_set, 1)
                    pool.wait_ge(ones_set, 2 * p + 1)
                    nc.gpsimd.memset(x_n[p][:, :, C:CA], 1.0).then_inc(ones_set, 1)
                pool.wait_ge(ones_set, 4)
                nc.gpsimd.memset(ones[:], 1.0).then_inc(ones_made, 1)

                pool.wait_ge(h_copied, NP)
                pool.wait_ge(wts2_in, WTS2)

                def decay_b(g, u, first=False):
                    k = TG * g + u
                    pool.wait_ge(sb_copied, k + 1)
                    if not (first and u < 2):
                        pool.wait_ge(pv_ready, k - 1)
                    nc.gpsimd.tensor_tensor(sc[u % 2][:, RH // 2:RH, :], sc_tmp[:], decay[:, RH // 2:RH, :], ALU.mult).then_inc(sb_done, 1)

                def squares(g):
                    pool.wait_ge(c_ready, g + 1)
                    nc.gpsimd.tensor_tensor(ret_sq[:], ret_c[:], ret_c[:], ALU.mult).then_inc(sq_ready, 1)

                def gate_input(g):
                    pool.wait_ge(gn_ready, g + 1)
                    nc.gpsimd.tensor_tensor(ret_n[:], ret_n[:], gn_w[:].unsqueeze(1).to_broadcast([T2, TG, D]), ALU.mult).then_inc(pool_step, 1)
                    pool.wait_ge(pool_step, 2 * g + 1)
                    nc.gpsimd.tensor_tensor(ret_n[:], ret_n[:], gn_b[:].unsqueeze(1).to_broadcast([T2, TG, D]), ALU.add).then_inc(pool_step, 1)
                    pool.wait_ge(pool_step, 2 * g + 2)
                    zg = gate_all[:, ds(TG * g, TG), :]
                    nc.gpsimd.tensor_tensor(zg, ret_n[:], zg, ALU.add).then_inc(z_done, 1)

                for u in range(TG):
                    decay_b(0, u, first=True)
                with pool.Fori(1, NG) as g:
                    decay_b(g, 0)
                    decay_b(g, 1)
                    squares(g - 1)
                    decay_b(g, 2)
                    decay_b(g, 3)
                    gate_input(g - 1)
                squares(NG - 1)
                gate_input(NG - 1)
                with pool.Fori(0, NG // 2) as j:
                    for p in range(2):
                        g = 2 * j + p
                        pool.wait_ge(aggr_done, g + 1)
                        pool.sem_inc(pool_waited, 1)
                        nc.gpsimd.tensor_copy(mean_all[:, ds(TG * g, TG)], mean_var2[p][:, :, 0])
                        nc.gpsimd.tensor_copy(rstd_all[:, ds(TG * g, TG)], mean_var2[p][:, :, 1]).then_inc(stats_done, 1)
                with pool.Fori(0, NG // 2) as j:
                    for p in range(2):
                        pool.wait_ge(hn_ready, 2 * j + p + 1)
                        nc.gpsimd.tensor_copy(rows[:, ds(TG * (2 * j + p), TG), 0:D], hn[p][:]).then_inc(rows_copied, 1)

                nc.gpsimd.tensor_tensor(h_all[:], h_all[:], sb2[:].unsqueeze(1).to_broadcast([T2, NP, D]), ALU.add).then_inc(sb2_added, 1)
                def add_residual(g, p):
                    pool.wait_ge(shy_taken, g + 1)
                    nc.gpsimd.tensor_tensor(out_g[p][:], out_g[p][:], h_all[:, ds(TG * g, TG), :], ALU.add).then_inc(out_ready, 1)

                pool.wait_ge(sb2_added, 1)
                with pool.Fori(0, NG // 2) as j:
                    for p in range(2):
                        add_residual(2 * j + p, p)

                for j in range(1, TG, 2):
                    pool.wait_ge(made_a, j + 1)
                    nc.gpsimd.tensor_tensor(hot_at[:, j].rearrange("p c e a -> p c (e a)"), hot_a[:, j].rearrange("p c e a -> p c (e a)"),
                                            tile_num[:, j, :].unsqueeze(2).to_broadcast([T2, EC, E * SA]), ALU.mult).then_inc(tile_odd, 1)

                def gather(p):
                    for s in range(2):
                        nc.gpsimd.indirect_dma_start(out=tok[p][s][:], out_offset=None, in_=prob_rows,
                                                     in_offset=bass.IndirectOffsetOnAxis(ap=idx_from[p][:, s:s + 1], axis=0)).then_inc(tok_in[p], 16)

                pool.wait_ge(table_out, 16)
                pool.wait_ge(idx_copied, RING)
                for e in range(RING - 1):
                    gather(e)
                for p in range(2):
                    pool.wait_ge(out_sent[p], 16 * NG // 2)

                def before_scattered(e):
                    if not (isinstance(e, int) and e == 0):
                        pool.wait_ge(scattered, 32 * e)

                def scatter(e, p):
                    pool.wait_ge(y_done, 2 * e + 2)
                    pool.sem_inc(pool_waited, 1)
                    for s in range(2):
                        nc.gpsimd.indirect_dma_start(out=out, out_offset=bass.IndirectOffsetOnAxis(ap=idx_to[p][:, s:s + 1], axis=0),
                                                     in_=y[p][s][:], in_offset=None, compute_op=ALU.add).then_inc(scattered, 16)

                def step_expert(e, p):
                    gather((p - 1) % RING)
                    before_scattered(e)
                    scatter(e, p)

                for e in range(RING):
                    step_expert(e, e)
                with pool.Fori(1, E // RING - 1) as j:
                    for p in range(RING):
                        step_expert(RING * j + p, p)
                step_expert(E - RING, 0)
                for p in range(1, RING):
                    before_scattered(E - RING + p)
                    scatter(E - RING + p, p)

            @block.scalar
            def _(act):
                act.wait_ge(set_dve, 2)
                nc.scalar.activation(s_v[:, 0, :], s_v[:, 0, :], ACT.Sqrt).then_inc(set_act, 1)
                nc.scalar.activation(s_qk[:, 0, :], s_qk[:, 0, :], ACT.Sqrt).then_inc(set_act, 1)
                for k in range(7):
                    if k >= 2:
                        act.wait_ge(bias_stored[k % 2], 48 * (k // 2))
                    for n in range(4):
                        act.wait_ge(bias_mm, 4 * k + n + 1)
                        last = nc.scalar.mul(bias_out[:, k % 2, n * 343:(n + 1) * 343], s_bank[n % 2][0:96, 0:343], -1.0)
                        last.then_inc(bank_read, 1)
                    act.wait_ge(bank_read, 4 * (k + 1))
                    act.sem_inc(bias_copied, 1)

                def exps(k, kp):
                    for c in range(CH):
                        m = chunk_rows(c)
                        act.wait_ge(ttr_done, CH * k + c + 1)
                        nc.scalar.activation(probs[0:m, kp, c, :], probs[0:m, kp, c, :], ACT.Exp,
                                             bias=neg_max[0:m, kp, c:c + 1], scale=-1.0).then_inc(exp_done, 1)

                def copy_px(k, b, banks):
                    for a in range(2):
                        act.wait_ge(px_ready, 2 * k + a + 1)
                        nc.scalar.copy(px_t[:, a * 6:(a + 1) * 6, b * NQ:(b + 1) * NQ],
                                       m_bank[banks[a]][0:CA, 0:6 * NQ].rearrange("p (h q) -> p h q", h=6)).then_inc(px_copied, 1)

                def copy_at(i):
                    for a in range(2):
                        act.wait_ge(at_ready, 2 * i + a + 1)
                        nc.scalar.copy(a_t[:, 3 * a:3 * a + 3, :],
                                       m_bank[1 + a][:, 0:3 * T2].rearrange("p (c t) -> p c t", c=3)).then_inc(at_copied, 1)

                def relu(i):
                    act.wait_ge(o_read, 2 * i + 2)
                    nc.scalar.activation(o_u[:], o_sb[:], ACT.Relu, bias=three[:, 0:1]).then_inc(u_ready, 1)

                def body(i, first=False, last=False):
                    exps(2 * i + 1, 1)
                    if not first:
                        relu(i - 1)
                    copy_px(2 * i, 0, (0, 1))
                    if not last:
                        exps(2 * i + 2, 0)
                    copy_px(2 * i + 1, 1, (0, 2))
                    if not first:
                        copy_at(i - 1)

                exps(0, 0)
                body(0, first=True)
                with act.Fori(1, NP - 1) as i:
                    body(i)
                body(NP - 1, last=True)
                relu(NP - 1)

                def root_ln(n):
                    act.wait_ge(var_ready, n + 1)
                    nc.scalar.activation(rstd[:], rstd[:], ACT.Sqrt).then_inc(std_ready, 1)

                root_ln(0)
                copy_at(NP - 1)

                act.wait_ge(h_copied, NP)

                def scores_b(g, u, first=False):
                    k = TG * g + u
                    act.wait_ge(sb_ready, k + 1)
                    if not (first and u < 1):
                        act.wait_ge(sb_done, k)
                    nc.scalar.copy(sc_tmp[:], bank[6][0:T2, 0:GT].rearrange("p (h t) -> p h t", h=TG)).then_inc(sb_copied, 1)

                def copy_lt(g):
                    act.wait_ge(lt_ready, g + 1)
                    nc.scalar.copy(ln_t[:], bank[0][:, 0:GT]).then_inc(lt_copied, 1)

                def copy_k(g):
                    act.wait_ge(k_ready, g + 1)
                    nc.scalar.copy(k_t[:], bank[2][:, 0:GT]).then_inc(k_copied, 1)

                def copy_vg(g):
                    for a in range(2):
                        act.wait_ge(vg_ready, 2 * g + a + 1)
                        vg = bank[3 + a][0:T2, :].rearrange("p (u v) -> p u v", u=2)
                        nc.scalar.copy(v_sb[:, 2 * a:2 * a + 2, :], vg[:, :, 0:D])
                        nc.scalar.copy(gate_all[:, ds(TG * g + 2 * a, 2), :], vg[:, :, D:2 * D]).then_inc(vg_copied, 1)

                def copy_ret(g, first=False):
                    act.wait_ge(pv_ready, TG * g + TG)
                    if not first:
                        act.wait_ge(c_ready, g)
                    nc.scalar.copy(ret[:], bank[7][0:T2, :].rearrange("p (h r) -> p h r", r=RD)).then_inc(ret_copied, 1)

                def root_gn(g):
                    act.wait_ge(gvar_ready, g + 1)
                    nc.scalar.activation(gstd[:], gstd[:], ACT.Sqrt).then_inc(gstd_ready, 1)

                def retention(g, first=False, last=False):
                    scores_b(g, 0, first)
                    scores_b(g, 1)
                    scores_b(g, 2)
                    if not last:
                        root_ln(g + 1)
                    scores_b(g, 3)
                    if not last:
                        copy_lt(g + 1)
                    if not first:
                        root_gn(g - 1)
                    copy_ret(g, first)
                    if not last:
                        copy_k(g + 1)
                        copy_vg(g + 1)

                copy_lt(0)
                copy_k(0)
                copy_vg(0)
                retention(0, first=True)
                with act.Fori(1, NG - 1) as g:
                    retention(g)
                retention(NG - 1, last=True)
                root_gn(NG - 1)

                def silu(g, p):
                    act.wait_ge(z_done, g + 1)
                    nc.scalar.activation(z[p][:], gate_all[:, ds(TG * g, TG), :], ACT.Silu).then_inc(zs_ready, 1)

                def copy_zt(g, p, first=False):
                    act.wait_ge(zt_ready, g + 1)
                    if not first:
                        act.wait_ge(wo_ready, g - 1)
                    nc.scalar.copy(z_t[p][:], bank[0][:, 0:GT]).then_inc(zt_copied, 1)

                silu(0, 0)
                silu(1, 1)
                for g in range(2):
                    copy_zt(g, g, first=True)
                    silu(g + 2, g)
                with act.Fori(1, NG // 2 - 1) as j:
                    for p in range(2):
                        copy_zt(2 * j + p, p)
                        silu(2 * j + p + 2, p)
                copy_zt(NG - 2, 0)
                copy_zt(NG - 1, 1)

                act.wait_ge(l_var, 1)
                nc.scalar.activation(rstd_all[:], rstd_all[:], ACT.Sqrt).then_inc(l_std, 1)

                def copy_hnt(g, p, first=False):
                    act.wait_ge(hnt_ready, g + 1)
                    if not first:
                        act.wait_ge(lg_ready, g - 1)
                    nc.scalar.copy(hn_g[p][:], bank[2 * p][:, 0:GT]).then_inc(hng_copied, 1)
                    nc.scalar.copy(hn_t[:, ds(GT * g, GT)], bank[2 * p][:, 0:GT]).then_inc(hnt_copied, 1)

                def take_logits(g, p):
                    act.wait_ge(lg_ready, g + 1)
                    nc.scalar.copy(logit[:, ds(TG * g, TG), :], bank[1 + 2 * p][0:T2, 0:TG * E].rearrange("p (u e) -> p u e", u=TG)).then_inc(lg_done, 1)

                copy_hnt(0, 0, True)
                copy_hnt(1, 1, True)
                take_logits(0, 0)
                with act.Fori(1, NG // 2) as j:
                    for p in range(2):
                        copy_hnt(2 * j + p, p)
                        take_logits(2 * j + p - 1, 1 - p)
                take_logits(NG - 1, 1)

                act.wait_ge(lx_ready, 1)
                nc.scalar.activation(logit[:], logit[:], ACT.Exp).then_inc(le_ready, 1)

                def gelu_shared(g, p, first=False):
                    for c in range(HC):
                        act.wait_ge(sh_ready, HC * g + c + 1)
                        if c == 0 and not first:
                            act.wait_ge(shy_ready, g - 1)
                        nc.scalar.activation(hid[p][:, c, :], bank[c][:, 0:GT], ACT.Gelu_apprx_tanh, bias=sb1[:, c:c + 1]).then_inc(sh_gelu, 1)

                def take_shared(g, p, first=False):
                    act.wait_ge(shy_ready, g + 1)
                    if not first:
                        act.wait_ge(out_sent[p], 16 * ((g - p) // 2) if isinstance(g, int) else 8 * (g - p))
                    nc.scalar.copy(out_g[p][:], bank[5 + 2 * p][0:T2, :].rearrange("p (u c) -> p u c", u=TG)).then_inc(shy_taken, 1)

                for g in range(2):
                    gelu_shared(g, g, True)
                    take_shared(g, g, True)
                with act.Fori(1, NG // 2) as j:
                    for p in range(2):
                        gelu_shared(2 * j + p, p)
                        take_shared(2 * j + p, p)

                for j in range(TG):
                    act.wait_ge(made_a, j + 1)
                    nc.scalar.mul(hot_ap[:, j].rearrange("p c e a -> p c (e a)"), hot_a[:, j].rearrange("p c e a -> p c (e a)"), tok_col[:, 0:1]).then_inc(place_ready, 1)
                    if j % 2 == 0:
                        for c in range(EC):
                            ins = nc.scalar.mul(hot_at[:, j, c], hot_a[:, j, c], float(TG * c + j))
                        ins.then_inc(tile_even, 1)

                def copy_tt(e, p):
                    act.wait_ge(tt_ready, e + 1)
                    nc.scalar.copy(tok_t[p][:], bank[0][:, 0:CAP]).then_inc(tt_copied, 1)

                def gelu_expert(e, p):
                    for c in range(HC):
                        act.wait_ge(eh_ready, 2 * e + c // 2 + 1)
                        nc.scalar.activation(ehid[p % 2][:, c, :], bank[1 + c // 2][:, (c % 2) * CAP:(c % 2 + 1) * CAP], ACT.Gelu_apprx_tanh,
                                             bias=b1[p][:, c:c + 1]).then_inc(eh_gelu, 1)

                copy_tt(0, 0)
                with act.Fori(0, E // RING - 1) as j:
                    for p in range(RING):
                        gelu_expert(RING * j + p, p)
                        copy_tt(RING * j + p + 1, 1 - p % 2)
                for p in range(RING - 1):
                    gelu_expert(E - RING + p, p)
                    copy_tt(E - RING + p + 1, 1 - p % 2)
                gelu_expert(E - 1, RING - 1)

            @block.vector
            def _(dve):
                done = [0]

                def setup(ins):
                    done[0] += 1
                    ins.then_inc(set_dve, 1)
                    return done[0]

                def hot(k):
                    for u in range(2):
                        dve.wait_ge(idx_spread, 2 * k + u + 1)
                        if k >= 2 and u == 0:
                            dve.wait_ge(bias_mm, 4 * (k - 1))
                        for s in range(2):
                            ins = nc.vector.tensor_scalar(onehot[k % 2][:, s, u * W7 // 2:(u + 1) * W7 // 2].rearrange("p (a b) -> p a b", a=2),
                                                          psum[0:HALF, 4 + 2 * u:6 + 2 * u, 0:343], iota_off[:, s:s + 1], None, ALU.is_equal)
                        ins.then_inc(hot_made, 1)

                dve.wait_ge(const_in, 64)
                nc.vector.tensor_copy(idx_bf[:], idx_i[:]).then_inc(idx_cast, 1)
                nc.vector.tensor_copy(pick_row[:], ident[0:7, 0:7].unsqueeze(2).to_broadcast([7, 7, HALF])).then_inc(idx_cast, 1)
                nc.vector.memset(bias_parts[:], 0.0).then_inc(parts_done, 1)
                dve.wait_ge(parts_done, 1)
                nc.vector.tensor_copy(bias_parts[:, :, 0, 0:H], bias_cols[:]).then_inc(parts_done, 1)
                dve.wait_ge(parts_done, 2)
                nc.vector.tensor_tensor(bias_rest[:], bias_cols[:], bias_parts[:, :, 0, 0:H], ALU.subtract).then_inc(parts_done, 1)
                dve.wait_ge(parts_done, 3)
                nc.vector.tensor_copy(bias_parts[:, :, 1, 0:H], bias_rest[:]).then_inc(parts_done, 1)
                dve.wait_ge(parts_done, 4)
                nc.vector.tensor_tensor(bias_rest[:], bias_rest[:], bias_parts[:, :, 1, 0:H], ALU.subtract).then_inc(parts_done, 1)
                dve.wait_ge(parts_done, 5)
                nc.vector.tensor_copy(bias_parts[:, :, 2, 0:H], bias_rest[:]).then_inc(parts_done, 1)
                hot(0)
                dve.wait_ge(par_in, 2 * 16)
                setup(nc.vector.tensor_scalar_add(s_qk[:, 0, :], par_qk[:, 3, :], EPS))
                setup(nc.vector.tensor_scalar_add(s_v[:, 0, :], par_v[:, 3, :], EPS))
                hot(1)
                for n, (s, par) in enumerate(((s_v, par_v), (s_qk, par_qk))):
                    dve.wait_ge(set_act, n + 1)
                    dve.wait_ge(set_dve, setup(nc.vector.reciprocal(s[:, 0, :], s[:, 0, :])))
                    dve.wait_ge(set_dve, setup(nc.vector.tensor_tensor(s[:, 0, :], s[:, 0, :], par[:, 0, :], ALU.mult)))
                    dve.wait_ge(set_dve, setup(nc.vector.tensor_tensor(s[:, 1, :], s[:, 0, :], par[:, 2, :], ALU.mult)))
                    dve.wait_ge(set_dve, setup(nc.vector.tensor_tensor(s[:, 1, :], par[:, 1, :], s[:, 1, :], ALU.subtract)))
                    hot(2 + n)
                setup(nc.vector.tensor_scalar(s_v[:, 0, NV - 1:NV], s_v[:, 0, NV - 1:NV], 1.0 / 6.0, None, ALU.mult))
                setup(nc.vector.tensor_scalar(s_qk[:, :, 0:H], s_qk[:, :, 0:H], -(KD ** -0.5), None, ALU.mult))
                hot(4)
                hot(5)
                hot(6)
                dve.wait_ge(wts_in, 4 * 16)
                dve.wait_ge(set_dve, done[0])
                for o, w, n in ((q_aug, q_w, 0), (k_aug, k_w, H)):
                    setup(nc.vector.tensor_tensor(o[:, :, 0:C], w[:], s_qk[:, 0, n:n + H].unsqueeze(2).to_broadcast([KD, H, C]), ALU.mult))
                    setup(nc.vector.tensor_copy(o[:, :, C], s_qk[:, 1, n:n + H]))
                assert done[0] == AUG_STEPS
                for k in range(2):
                    setup(nc.vector.tensor_tensor(s_diag[:, k], ident[:].unsqueeze(1).to_broadcast([128, NV, 128]),
                                                  s_v[:, k, :].unsqueeze(2).to_broadcast([128, NV, 128]), ALU.mult))
                assert done[0] == DIAG_STEPS
                for n in range(3):
                    dve.wait_ge(mat_ready, n + 1)
                    nc.vector.tensor_copy(qk_mat[:, 4 * n:4 * n + 4, :], m_bank[n][0:CA, 0:4 * CA].rearrange("p (h c) -> p h c", h=4)).then_inc(mat_copied, 1)
                dve.wait_ge(scale_ready, 1)
                for a in range(2):
                    setup(nc.vector.tensor_tensor(v_aug[0:C, 6 * a:6 * a + 6, 0:VD], v_w[:, a * 6 * VD:(a + 1) * 6 * VD].rearrange("c (h e) -> c h e", h=6),
                                                  bank[2 + a][0:C, 0:6 * VD].rearrange("c (h e) -> c h e", h=6), ALU.mult))
                setup(nc.vector.memset(v_aug[0:C, :, VD:VD + 1], 0.0))
                setup(nc.vector.memset(v_aug[C:CA, :, VD:VD + 1], 1.0))
                setup(nc.vector.tensor_tensor(proj[:], proj[:], bank[2][:, 384:512].unsqueeze(1).to_broadcast([128, DH // 128, D]), ALU.mult))
                dve.wait_ge(scale_ready, 2)
                for a in range(2):
                    setup(nc.vector.tensor_copy(v_aug[C:CA, 6 * a:6 * a + 6, 0:VD], bank[a][C:CA, 0:6 * VD].rearrange("c (h e) -> c h e", h=6)))
                setup(nc.vector.tensor_copy(proj_shift[:], bank[0][0:T2, 384:512]))
                setup(nc.vector.memset(three[:], 3.0))
                assert done[0] == SETUP_STEPS

                def add_bias(k, kp, first=False, chunks=range(CH)):
                    if not first and 0 in chunks:
                        dve.wait_ge(t_ready, 3 * k - 3)
                    for c in chunks:
                        m = chunk_rows(c)
                        if c % 2 == 0:
                            dve.wait_ge(s_ready, 3 * k + c // 2 + 1)
                            dve.sem_inc(dve_waited, 1)
                        ins = nc.vector.tensor_tensor_reduce(
                            out=probs[0:m, kp, c, :], in0=s_bank[c // 2][0:m, (c % 2) * N:(c % 2 + 1) * N],
                            in1=bias_neg[0:m, c, :], scale=1.0, scalar=3.0e38, op0=ALU.add, op1=ALU.min,
                            accum_out=neg_max[0:m, kp, c:c + 1])
                        ins.then_inc(ttr_done, 1)

                def copy_pt(k, kk, t):
                    if True:
                        w = chunk_cols(t)
                        dve.wait_ge(t_ready, 3 * k + t + 1)
                        nc.vector.tensor_copy(p_t[:, :, 2 * CR * t:2 * CR * t + w],
                                              t_bank[(3 * kk + t) % 2][0:HALF, 0:4 * CR].rearrange("p (s r) -> p s r", s=2)[:, :, 0:w]).then_inc(pt_copied, 1)

                def copy_g(i, g):
                    if True:
                        dve.wait_ge(g_ready, 3 * i + g + 1)
                        nc.vector.tensor_copy(g_t[:, :, 4 * g * NQ:4 * (g + 1) * NQ].rearrange("p b (h q) -> p h b q", h=4),
                                              m_bank[g][0:CA, 0:4 * T2].rearrange("p (h b q) -> p h b q", h=4, b=2)).then_inc(g_copied, 1)

                def take_o(i, first=False):
                    for a in range(2):
                        o = m_bank[a][0:T2, 0:6 * (VD + 1)].rearrange("p (h e) -> p h e", h=6)
                        dve.wait_ge(o_ready, 2 * i + a + 1)
                        nc.vector.reciprocal(o_rec[:, a, :], o[:, :, VD]).then_inc(o_rec_done, 1)
                        dve.wait_ge(o_rec_done, 2 * i + a + 1)
                        if a == 0 and not first:
                            dve.wait_ge(a_ready, i)
                        nc.vector.tensor_tensor(o_sb[:, a * 6 * VD:(a + 1) * 6 * VD].rearrange("p (h e) -> p h e", h=6),
                                                o[:, :, 0:VD], o_rec[:, a, :].unsqueeze(2).to_broadcast([T2, 6, VD]), ALU.mult).then_inc(o_read, 1)

                def take_h(i):
                    dve.wait_ge(h_ready, i + 1)
                    nc.vector.tensor_tensor(row_of_h(i), m_bank[2][0:T2, 0:D], proj_shift[:], ALU.add).then_inc(h_copied, 1)

                def hard_swish(i, first=False):
                    dve.wait_ge(u_ready, i + 1)
                    if not first:
                        dve.wait_ge(at_ready, 2 * i)
                    nc.vector.scalar_tensor_tensor(out=o_a[:], in0=o_u[:], scalar=6.0, in1=o_sb[:], op0=ALU.min, op1=ALU.mult).then_inc(a_ready, 1)

                def body(i, first=False, second=False, last=False):
                    add_bias(2 * i + 1, 1, first=first)
                    copy_pt(2 * i, 0, 0)
                    copy_pt(2 * i, 0, 1)
                    if not last:
                        copy_g(i + 1, 0)
                        copy_g(i + 1, 1)
                    copy_pt(2 * i, 0, 2)
                    if not last:
                        copy_g(i + 1, 2)
                    for t in range(2):
                        copy_pt(2 * i + 1, 1, t)
                    if not last:
                        add_bias(2 * i + 2, 0, chunks=range(0, 2))
                    copy_pt(2 * i + 1, 1, 2)
                    if not last:
                        add_bias(2 * i + 2, 0, chunks=range(2, CH))
                    if not first:
                        hard_swish(i - 1, first=second)
                    take_o(i, first=first)
                    if not first:
                        take_h(i - 1)

                LN1 = 2 * TG + 1
                GN1 = 4

                def moments(g):
                    for u in range(TG):
                        nc.vector.bn_stats(stats[:, u, :], h_all[:, ds(TG * g + u, 1), :].rearrange("p a c -> p (a c)")).then_inc(ln_step, 1)
                    dve.wait_ge(ln_step, LN1 * g + TG)
                    dve.sem_inc(dve_waited, 1)
                    for u in range(TG):
                        nc.vector.bn_aggr(mean_var[:, u, :], stats[:, u, :]).then_inc(ln_step, 1)
                    dve.wait_ge(ln_step, LN1 * g + 2 * TG)
                    nc.vector.tensor_scalar_add(rstd[:], mean_var[:, :, 1], EPS).then_inc(var_ready, 1)

                def normalise(g, first=False):
                    dve.wait_ge(std_ready, g + 1)
                    nc.vector.reciprocal(rstd[:], rstd[:]).then_inc(ln_step, 1)
                    dve.wait_ge(ln_step, LN1 * g + LN1)
                    if not first:
                        dve.wait_ge(lt_ready, g)
                    for u in range(TG):
                        ins = nc.vector.tensor_scalar(ln[:, u, :], h_all[:, ds(TG * g + u, 1), :].rearrange("p a c -> p (a c)"),
                                                      mean_var[:, u, 0:1], rstd[:, u:u + 1], ALU.subtract, ALU.mult)
                    ins.then_inc(ln_ready, 1)

                for g in range(3):
                    copy_g(0, g)
                dve.wait_ge(bias_back, 96)
                for part in range(2):
                    nc.vector.tensor_tensor(bias_neg[:, 0:CH - 1], bias_neg[:, 0:CH - 1], bias_low[:, part, 0:CH - 1], ALU.add).then_inc(parts_done, 1)
                    m = chunk_rows(CH - 1)
                    nc.vector.tensor_tensor(bias_neg[0:m, CH - 1], bias_neg[0:m, CH - 1], bias_low[0:m, part, CH - 1], ALU.add).then_inc(parts_done, 1)
                    dve.wait_ge(parts_done, 6 + 2 * (part + 1))
                add_bias(0, 0, first=True)
                body(0, first=True)
                body(1, second=True)
                with dve.Fori(2, NP - 1) as i:
                    body(i)
                dve.wait_ge(h_copied, TG)
                dve.sem_inc(dve_waited, 1)
                moments(0)
                body(NP - 1, last=True)
                hard_swish(NP - 1)
                normalise(0, first=True)
                take_h(NP - 1)

                dve.wait_ge(wts2_in, WTS2)

                def group_norm_a(g):
                    dve.wait_ge(ret_copied, g + 1)
                    nc.vector.tensor_reduce(gmean[:], ret[:], AX.X, ALU.add).then_inc(gn_step, 1)
                    dve.wait_ge(gn_step, GN1 * g + 1)
                    nc.vector.tensor_scalar(gmean[:], gmean[:], 1.0 / RD, None, ALU.mult).then_inc(gn_step, 1)
                    dve.wait_ge(gn_step, GN1 * g + 2)
                    nc.vector.tensor_tensor(ret_c[:], ret[:], gmean[:].unsqueeze(2).to_broadcast([T2, TG * RH, RD]), ALU.subtract).then_inc(c_ready, 1)

                def group_norm_b(g):
                    dve.wait_ge(sq_ready, g + 1)
                    nc.vector.tensor_reduce(gstd[:], ret_sq[:], AX.X, ALU.add).then_inc(gn_step, 1)
                    dve.wait_ge(gn_step, GN1 * g + 3)
                    nc.vector.tensor_scalar(gstd[:], gstd[:], 1.0 / RD, EPS, ALU.mult, ALU.add).then_inc(gvar_ready, 1)

                def group_norm_c(g, first=False):
                    dve.wait_ge(gstd_ready, g + 1)
                    nc.vector.reciprocal(gstd[:], gstd[:]).then_inc(gn_step, 1)
                    dve.wait_ge(gn_step, GN1 * g + 4)
                    if not first:
                        dve.wait_ge(z_done, g)
                    nc.vector.tensor_tensor(ret_n[:].rearrange("p u (h r) -> p (u h) r", h=RH), ret_c[:],
                                            gstd[:].unsqueeze(2).to_broadcast([T2, TG * RH, RD]), ALU.mult).then_inc(gn_ready, 1)

                def spread_q(g, u, first=False):
                    k = TG * g + u
                    if u == 0:
                        dve.wait_ge(q_ready, g + 1)
                    if not (first and u < 2):
                        dve.wait_ge(sb_ready, k - 1)
                    nc.vector.tensor_tensor(q_heads[u % 2][:], bank[1][:, u * T2:(u + 1) * T2].unsqueeze(1).to_broadcast([D, RH, T2]),
                                            head_mask[:].unsqueeze(2).to_broadcast([D, RH, T2]), ALU.mult).then_inc(qm_made, 1)

                def decay_a(g, u, first=False):
                    k = TG * g + u
                    dve.wait_ge(sa_ready, k + 1)
                    if not (first and u < 2):
                        dve.wait_ge(pv_ready, k - 1)
                    nc.vector.tensor_tensor(sc[u % 2][:, 0:RH // 2, :], bank[5][0:T2, 0:GT].rearrange("p (h t) -> p h t", h=TG),
                                            decay[:, 0:RH // 2, :], ALU.mult).then_inc(sa_done, 1)

                def retention(g, first=False, second=False, last=False):
                    decay_a(g, 0, first)
                    spread_q(g, 2)
                    decay_a(g, 1, first)
                    if not first:
                        group_norm_a(g - 1)
                    spread_q(g, 3)
                    decay_a(g, 2)
                    if not last:
                        moments(g + 1)
                    decay_a(g, 3)
                    if not last:
                        normalise(g + 1)
                    if not first:
                        group_norm_b(g - 1)
                        group_norm_c(g - 1, second)
                    if not last:
                        spread_q(g + 1, 0)
                        spread_q(g + 1, 1)

                spread_q(0, 0, first=True)
                spread_q(0, 1, first=True)
                retention(0, first=True)
                retention(1, second=True)
                with dve.Fori(2, NG - 1) as g:
                    retention(g)
                retention(NG - 1, last=True)
                group_norm_a(NG - 1)
                group_norm_b(NG - 1)
                group_norm_c(NG - 1)

                STAT = TG

                def residual(g, p):
                    dve.wait_ge(wo_ready, g + 1)
                    hg = h_all[:, ds(TG * g, TG), :]
                    nc.vector.tensor_tensor(hg, bank[1 + 2 * p][0:T2, :].rearrange("p (u c) -> p u c", u=TG), hg, ALU.add).then_inc(h2_done, 1)

                def moments2(g, p, first=False):
                    dve.wait_ge(h2_done, g + 1)
                    if not (isinstance(g, int) and g < 2):
                        dve.wait_ge(stats_done, g - 1)
                    dve.sem_inc(dve_waited, 1)
                    for u in range(TG):
                        nc.vector.bn_stats(stats2[p][:, u, :], h_all[:, ds(TG * g + u, 1), :].rearrange("p a c -> p (a c)")).then_inc(stat_step, 1)
                    dve.wait_ge(stat_step, STAT * g + TG)
                    dve.sem_inc(dve_waited, 1)
                    for u in range(TG):
                        ins = nc.vector.bn_aggr(mean_var2[p][:, u, :], stats2[p][:, u, :])
                    ins.then_inc(aggr_done, 1)

                residual(0, 0)
                residual(1, 1)
                moments2(0, 0)
                residual(2, 0)
                moments2(1, 1)
                residual(3, 1)
                moments2(2, 0)
                with dve.Fori(2, NG // 2) as j:
                    for p in range(2):
                        residual(2 * j + p, p)
                        moments2(2 * j + p - 1, 1 - p)
                moments2(NG - 1, 1)
                dve.wait_ge(stats_done, NG)
                nc.vector.tensor_scalar_add(rstd_all[:], rstd_all[:], EPS).then_inc(l_var, 1)

                dve.wait_ge(l_std, 1)
                nc.vector.reciprocal(rstd_all[:], rstd_all[:]).then_inc(stats_done, 1)
                dve.wait_ge(stats_done, NG + 1)

                def second_norm(g, p, first=False):
                    if not first:
                        dve.wait_ge(rows_copied, g - 1)
                        dve.wait_ge(hnt_ready, g - 1)
                    for u in range(TG):
                        ins = nc.vector.tensor_scalar(hn[p][:, u, :], h_all[:, ds(TG * g + u, 1), :].rearrange("p a c -> p (a c)"),
                                                      mean_all[:, ds(TG * g + u, 1)], rstd_all[:, ds(TG * g + u, 1)], ALU.subtract, ALU.mult)
                    ins.then_inc(hn_ready, 1)

                second_norm(0, 0, True)
                second_norm(1, 1, True)
                with dve.Fori(1, NG // 2) as j:
                    for p in range(2):
                        second_norm(2 * j + p, p)
                n_steps = 0
                m = [n_steps]

                def then(ins):
                    m[0] += 1
                    ins.then_inc(step, 1)
                    dve.wait_ge(step, m[0])

                dve.wait_ge(lg_done, NG)
                then(nc.vector.tensor_reduce(lmax[:], logit[:], AX.X, ALU.max))
                nc.vector.tensor_tensor(logit[:], logit[:], lmax[:].unsqueeze(2).to_broadcast([T2, NP, E]), ALU.subtract).then_inc(lx_ready, 1)
                dve.wait_ge(le_ready, 1)
                then(nc.vector.tensor_reduce(lsum[:], logit[:], AX.X, ALU.add))
                then(nc.vector.reciprocal(lsum[:], lsum[:]))
                dve.wait_ge(rows_copied, NG)
                nc.vector.tensor_tensor(rows[:, :, D:ROW], logit[:], lsum[:].unsqueeze(2).to_broadcast([T2, NP, E]), ALU.mult).then_inc(pr_ready, 1)
                dve.wait_ge(pr_ready, 1)
                nc.vector.tensor_copy(prob_j[:].rearrange("p j (e c) -> p c j e", e=E),
                                      rows[:, :, D:ROW].rearrange("p (c j) e -> p c j e", j=TG)).then_inc(pr_ready, 1)
                nc.vector.memset(thr[:], 0)
                for k in range(1, 4):
                    nc.vector.memset(digit[:, 0, k - 1:k], k << 28)
                    nc.vector.memset(digit[:, 1, k - 1:k], (k ^ (k - 1)) << 28)
                dve.wait_ge(xp_ready, 1)
                then(nc.vector.tensor_copy(xp[:], bank[4][:, 0:GT]))
                n_steps = m[0]

                SEARCH = 7

                def search(q, base):
                    nc.vector.tensor_tensor(cand[:], thr[:].to_broadcast([128, 3]), digit[:, 0, :], ALU.bitwise_or).then_inc(step, 1)
                    dve.wait_ge(step, base + 1)
                    for k, hits in enumerate((above, equal, sel)):
                        ins = nc.vector.tensor_scalar(hits[:], xp[:], cand[:, k:k + 1].bitcast(F32), None, ALU.is_ge, ALU.add, accum_out=cnt[:, k:k + 1])
                    ins.then_inc(cnt_ready, 1)
                    dve.wait_ge(tot_ready, q + 1)
                    nc.vector.tensor_scalar(mask[:], bank[6][:, 0:3], CAP - 0.5, -1.0, ALU.is_ge, ALU.mult).then_inc(step, 1)
                    dve.wait_ge(step, base + 2)
                    nc.vector.tensor_tensor(flip[:], mask[:], digit[:, 1, :], ALU.bitwise_and).then_inc(step, 1)
                    dve.wait_ge(step, base + 3)
                    nc.vector.tensor_tensor(thr[:], thr[:], flip[:, 0:1], ALU.bitwise_xor).then_inc(step, 1)
                    nc.vector.tensor_tensor(flip[:, 1:2], flip[:, 1:2], flip[:, 2:3], ALU.bitwise_xor).then_inc(step, 1)
                    nc.vector.tensor_scalar(digit[:], digit[:], 2, None, ALU.logical_shift_right).then_inc(step, 1)
                    dve.wait_ge(step, base + 5)
                    nc.vector.tensor_tensor(thr[:], thr[:], flip[:, 1:2], ALU.bitwise_xor).then_inc(step, 1)
                    dve.wait_ge(step, base + 7)

                for q in range(2):
                    search(q, n_steps + SEARCH * q)
                with dve.Fori(1, NG - 1) as g:
                    for q in range(2):
                        search(2 * g + q, n_steps + SEARCH * (2 * g + q))
                search(2 * NG - 2, n_steps + SEARCH * (2 * NG - 2))
                m[0] += SEARCH * (2 * NG - 1)

                t_f = thr[:].bitcast(F32)
                nc.vector.tensor_scalar(above[:], xp[:], t_f, None, ALU.is_gt, ALU.add, accum_out=col[:, 0:1])
                then(nc.vector.tensor_scalar(equal[:], xp[:], t_f, None, ALU.is_equal))
                then(nc.vector.tensor_tensor_scan(scan_e[:], equal[:], equal[:], 0.0, ALU.add, ALU.bypass))
                nc.vector.tensor_copy(col[:, 1:2], scan_e[:, GT - 1:GT]).then_inc(col_ready, 1)
                dve.wait_ge(off_ready, 1)
                then(nc.vector.tensor_scalar(col[:, 2:3], bank[6][:, 8:9], -1.0, float(CAP), ALU.mult, ALU.add))
                then(nc.vector.tensor_tensor(col[:, 2:3], col[:, 2:3], bank[6][:, 16:17], ALU.subtract))
                then(nc.vector.scalar_tensor_tensor(out=sel[:], in0=scan_e[:], scalar=col[:, 2:3], in1=equal[:], op0=ALU.is_le, op1=ALU.mult))
                then(nc.vector.tensor_tensor(sel[:], sel[:], above[:], ALU.add))
                then(nc.vector.tensor_tensor_scan(scan_s[:], sel[:], sel[:], 0.0, ALU.add, ALU.bypass))
                nc.vector.tensor_copy(col[:, 3:4], scan_s[:, GT - 1:GT]).then_inc(col_ready, 1)
                dve.wait_ge(off_ready, 2)
                then(nc.vector.tensor_scalar(col[:, 2:3], bank[6][:, 24:25], -256.0, None, ALU.add))
                nc.vector.scalar_tensor_tensor(out=scan_e[:], in0=scan_s[:], scalar=col[:, 2:3], in1=sel[:], op0=ALU.add, op1=ALU.mult).then_inc(slot_ready, 1)
                dve.wait_ge(slot_taken, 1)
                then(nc.vector.tensor_scalar(slot[:], bank[4][0:T2, :].rearrange("p (j m) -> p j m", j=TG), 255.0, None, ALU.add))
                nc.vector.tensor_scalar(slot_a[:], slot[:], 4, None, ALU.logical_shift_right).then_inc(step, 1)
                m[0] += 1
                nc.vector.tensor_scalar(slot_b[:], slot[:], SB_ - 1, None, ALU.bitwise_and).then_inc(slots_split, 1)
                dve.wait_ge(step, m[0])
                def one_hot(j, o, a, w, made):
                    nc.vector.tensor_tensor(o[:, j], a[:, j, :].rearrange("p (e c) -> p c e", e=E).unsqueeze(3).to_broadcast([T2, EC, E, w]),
                                            iota_slot[:, 0:w].unsqueeze(1).unsqueeze(1).to_broadcast([T2, EC, E, w]), ALU.is_equal).then_inc(made, 1)

                one_hot(0, hot_a, slot_a, SA, made_a)
                dve.wait_ge(slots_split, 1)
                one_hot(0, hot_b, slot_b, SB_, made_b)
                one_hot(1, hot_a, slot_a, SA, made_a)
                one_hot(1, hot_b, slot_b, SB_, made_b)
                one_hot(2, hot_a, slot_a, SA, made_a)
                one_hot(2, hot_b, slot_b, SB_, made_b)
                one_hot(3, hot_a, slot_a, SA, made_a)
                one_hot(3, hot_b, slot_b, SB_, made_b)
                dve.wait_ge(list_ready, 1)
                for g in range(2):
                    then(nc.vector.tensor_scalar(list_t[:, g].rearrange("p e b -> p (e b)"), bank[2 * g + 1][0:EG * SA, 0:128], float(T2), None, ALU.mult))
                for g in range(2):
                    lt = list_t[:, g].rearrange("p e b -> p (e b)")
                    then(nc.vector.tensor_tensor(lt, bank[2 * g][0:EG * SA, 0:128], lt, ALU.add))
                then(nc.vector.tensor_tensor(list_t[:], list_t[:], diag[:].unsqueeze(1).to_broadcast([EG * SA, 2, EG, SB_]), ALU.mult))
                nc.vector.tensor_reduce(list_s[:], list_t[:].rearrange("p g e b -> p g b e"), AX.X, ALU.add).then_inc(list_done, 1)
                dve.wait_ge(lr_ready, 1)
                nc.vector.tensor_copy(idx_all[:], bank[6][0:TH, 0:2 * E]).then_inc(lr_done, 1)
                dve.wait_ge(lr_done, 1)

                def copy_idx(o, e):
                    for s in range(2):
                        ins = nc.vector.tensor_copy(o[:, s:s + 1], idx_all[:, ds(e + E * s, 1)])
                    return ins

                for e in range(RING):
                    copy_idx(idx_from[e], e).then_inc(idx_copied, 1)

                def take_y(e, p, first=False, last=False):
                    dve.wait_ge(ey_ready, e + 1)
                    dve.wait_ge(ew_in[p], 64 * (e // RING + 1) if isinstance(e, int) else 16 * (e - p) + 64)
                    if not first:
                        dve.wait_ge(scattered, 32 * (e - RING + 1))
                    copy_idx(idx_to[p], e)
                    for s in range(2):
                        nc.vector.tensor_tensor(y[p][s][:], bank[3][0:TH, s * D:(s + 1) * D], b2[p][:], ALU.add).then_inc(ey_taken, 1)
                    for s in range(2):
                        dve.wait_ge(ey_taken, 2 * e + s + 1)
                        if s == 0 and not last:
                            copy_idx(idx_from[p], e + RING)
                        nc.vector.tensor_scalar(y[p][s][:], y[p][s][:], tok[p][s][:, ds(D + e, 1)], None, ALU.mult).then_inc(y_done, 1)

                for e in range(RING):
                    take_y(e, e, first=True)
                with dve.Fori(1, E // RING - 1) as j:
                    for p in range(RING):
                        take_y(RING * j + p, p)
                for p in range(RING):
                    take_y(E - RING + p, p, last=True)

            @block.tensor
            def _(pe):
                def spread_index(n):
                    if n >= 2:
                        pe.wait_ge(hot_made, n - 1)
                    k, u = n // 2, n % 2
                    for a in range(2):
                        ins = nc.tensor.matmul(bank[4 + 2 * u + a][0:HALF, 0:343], pick_row[:, k, :],
                                               idx_bf[:, (2 * u + a) * 343:(2 * u + a + 1) * 343], start=True, stop=True)
                    ins.then_inc(idx_spread, 1)

                def spread_scale(k):
                    b0, b1 = (bank[2], bank[3]) if k == 0 else (bank[0], bank[1])
                    for o, lo, hi in ((b0[:, 0:384], 0, 3), (b1[:, 0:384], 3, 6), (b0[:, 384:512], 6, 7)):
                        ins = nc.tensor.matmul(o, ones[:], s_diag[:, k, lo:hi, :].rearrange("p a b -> p (a b)"), start=True, stop=True)
                    ins.then_inc(scale_ready, 1)

                pe.wait_ge(idx_cast, 2)
                spread_index(0)
                spread_index(1)
                pe.wait_ge(parts_done, 6)
                for k in range(7):
                    if k < 6:
                        spread_index(2 * k + 2)
                        spread_index(2 * k + 3)
                    pe.wait_ge(hot_made, 2 * k + 2)
                    for n in range(4):
                        if 4 * k + n >= 2:
                            pe.wait_ge(bank_read, 4 * k + n - 1)
                        for s in range(2):
                            ins = nc.tensor.matmul(s_bank[n % 2][0:96, 0:343], bias_parts[:, s].rearrange("p a b -> p (a b)"),
                                                   onehot[k % 2][:, s, n * 343:(n + 1) * 343], start=(s == 0), stop=(s == 1))
                        ins.then_inc(bias_mm, 1)
                pe.wait_ge(set_dve, AUG_STEPS)
                for h in range(H):
                    ins = nc.tensor.matmul(m_bank[h // 4][0:CA, (h % 4) * CA:(h % 4 + 1) * CA], q_aug[:, h, :], k_aug[:, h, :], start=True, stop=True)
                    if h % 4 == 3:
                        ins.then_inc(mat_ready, 1)

                pe.wait_ge(ones_made, 1)
                pe.wait_ge(set_dve, DIAG_STEPS)
                spread_scale(0)
                pe.wait_ge(bank_read, 28)
                spread_scale(1)

                def g_product(i, g, p, first=False):
                    if g == 0:
                        pe.wait_ge(x_in[p], 32 * (i // 2 + 1) if isinstance(i, int) else 16 * (i - p) + 32)
                    if first:
                        pe.wait_ge(mat_copied, 3)
                    elif isinstance(i, int) and i == 1:
                        pe.wait_ge(g_copied, g + 1)
                    elif g < 2:
                        pe.wait_ge(o_read, 2 * i - 3 + g)
                    elif not (isinstance(i, int) and i == 2):
                        pe.wait_ge(h_copied, i - 2)
                    xs = x_t[p][:, :].rearrange("c (b y x) -> c b y x", b=2, y=RES)[:, :, ::STRIDE, ::STRIDE]
                    for h in range(4):
                        ins = nc.tensor.matmul(m_bank[g][0:CA, h * T2:(h + 1) * T2].rearrange("c (b y x) -> c b y x", b=2, y=7),
                                               qk_mat[:, 4 * g + h, :], xs, start=True, stop=True)
                    ins.then_inc(g_ready, 1)

                def s_product(k, b, p, first=False, chunks=range(CH)):
                    for c in chunks:
                        m = chunk_rows(c)
                        if c % 2 == 0 and not first:
                            pe.wait_ge(ttr_done, CH * (k - 1) + min(c + 2, CH))
                        ins = nc.tensor.matmul(s_bank[c // 2][0:m, (c % 2) * N:(c % 2 + 1) * N], g_t[:, b, c * CR:c * CR + m],
                                               x_t[p][:, b * N:(b + 1) * N], start=True, stop=True)
                        if c % 2 == 1 or c == CH - 1:
                            ins.then_inc(s_ready, 1)

                def turn_probs(k, kp, f0, first=False, groups=range(3)):
                    for t in groups:
                        pe.wait_ge(exp_done, CH * k + min(2 * t + 2, CH))
                        if not (first and t < 2):
                            pe.wait_ge(pt_copied, 3 * k + t - 1)
                        for c in range(2 * t, min(2 * t + 2, CH)):
                            m = chunk_rows(c)
                            for s in range(2):
                                o = s * 2 * CR + (c - 2 * t) * CR
                                ins = nc.tensor.transpose(t_bank[(f0 + t) % 2][0:HALF, o:o + m], probs[0:m, kp, c, s * HALF:(s + 1) * HALF], ident[0:m, 0:m])
                        ins.then_inc(t_ready, 1)

                def px_product(k, b, p, banks, waits):
                    for a in range(2):
                        pe.wait_ge(pt_copied, 3 * k + 2 + a)
                        waits(a)
                        for s in range(2):
                            ins = nc.tensor.matmul(m_bank[banks[a]][0:CA, 0:6 * NQ], x_n[p][:, 2 * b + s, :], p_t[:, s, a * 6 * NQ:(a + 1) * 6 * NQ],
                                                   start=(s == 0), stop=(s == 1))
                        ins.then_inc(px_ready, 1)

                def turn_a(i, a):
                    if a == 0:
                        pe.wait_ge(a_ready, i + 1)
                    for c in range(3):
                        ins = nc.tensor.transpose(m_bank[1 + a][:, c * T2:(c + 1) * T2], o_a[:, (3 * a + c) * 128:(3 * a + c + 1) * 128], ident[0:T2, 0:T2])
                    ins.then_inc(at_ready, 1)

                def project(i):
                    pe.wait_ge(at_copied, 2 * i + 2)
                    for c in range(DH // 128):
                        ins = nc.tensor.matmul(m_bank[2][0:T2, 0:D], a_t[:, c, :], proj[:, c, :], start=(c == 0), stop=(c == DH // 128 - 1))
                    ins.then_inc(h_ready, 1)

                def o_product(i, a, first):
                    pe.wait_ge(px_copied, 4 * i + 3 + a)
                    if a == 1 and not first:
                        pe.wait_ge(at_copied, 2 * i - 1)
                    for h in range(6):
                        ins = nc.tensor.matmul(m_bank[a][0:T2, h * (VD + 1):(h + 1) * (VD + 1)], px_t[:, 6 * a + h, :], v_aug[:, 6 * a + h, :],
                                               start=True, stop=True)
                    ins.then_inc(o_ready, 1)

                def body(i, p, first=False, last=False):
                    s_product(2 * i + 1, 1, p)
                    turn_probs(2 * i, 0, 0, first=first, groups=range(0, 2))
                    if not last:
                        g_product(i + 1, 0, 1 - p)
                        g_product(i + 1, 1, 1 - p)
                    turn_probs(2 * i, 0, 0, groups=range(2, 3))
                    if not last:
                        g_product(i + 1, 2, 1 - p)

                    def before_px0(a):
                        if not last:
                            pe.wait_ge(g_copied, 3 * (i + 1) + 1 + a)
                        else:
                            pe.wait_ge(o_read, 2 * i - 1 + a)
                    px_product(2 * i, 0, p, (0, 1), before_px0)
                    turn_probs(2 * i + 1, 1, 3, groups=range(0, 2))
                    if not last:
                        pe.wait_ge(g_copied, 3 * (i + 1) + 3)
                        s_product(2 * i + 2, 0, 1 - p, chunks=range(0, 2))
                    turn_probs(2 * i + 1, 1, 3, groups=range(2, 3))
                    if not last:
                        s_product(2 * i + 2, 0, 1 - p, chunks=range(2, CH))

                    def before_px1(a):
                        if a == 0:
                            pe.wait_ge(px_copied, 4 * i + 1)
                        elif last:
                            pe.wait_ge(h_copied, i - 1)
                    px_product(2 * i + 1, 1, p, (0, 2), before_px1)
                    if not first:
                        pe.wait_ge(px_copied, 4 * i + 2)
                        turn_a(i - 1, 0)
                    o_product(i, 0, first)
                    if not first:
                        pe.wait_ge(px_copied, 4 * i + 4)
                        turn_a(i - 1, 1)
                    o_product(i, 1, first)
                    if not first:
                        project(i - 1)

                pe.wait_ge(ones_set, 4)
                for g in range(3):
                    g_product(0, g, 0, first=True)
                pe.wait_ge(g_copied, 3)
                pe.wait_ge(set_dve, SETUP_STEPS)
                s_product(0, 0, 0, first=True)
                body(0, 0, first=True)
                body(1, 1)
                with pe.Fori(1, NP // 2 - 1) as j:
                    body(2 * j, 0)
                    body(2 * j + 1, 1)
                body(NP - 2, 0)
                body(NP - 1, 1, last=True)
                pe.wait_ge(o_read, 2 * NP)
                pe.wait_ge(h_copied, NP - 1)
                for a in range(2):
                    turn_a(NP - 1, a)
                project(NP - 1)

                pe.wait_ge(wts2_in, WTS2)
                pe.wait_ge(h_copied, NP)

                def turn_ln(g):
                    pe.wait_ge(ln_ready, g + 1)
                    for u in range(TG):
                        ins = nc.tensor.transpose(bank[0][:, u * T2:(u + 1) * T2], ln[:, u, :], ident[0:T2, 0:T2])
                    ins.then_inc(lt_ready, 1)

                def queries_keys(g, first=False):
                    pe.wait_ge(lt_copied, g + 1)
                    if not first:
                        pe.wait_ge(qm_made, TG * g)
                    nc.tensor.matmul(bank[1][:, 0:GT], w_q[:], ln_t[:], start=True, stop=True).then_inc(q_ready, 1)
                    nc.tensor.matmul(bank[2][:, 0:GT], w_k[:], ln_t[:], start=True, stop=True).then_inc(k_ready, 1)

                def values_gate(g):
                    for a in range(2):
                        for u in range(2):
                            ins = nc.tensor.matmul(bank[3 + a][0:T2, u * 2 * D:(u + 1) * 2 * D], ln_t[:, (2 * a + u) * T2:(2 * a + u + 1) * T2], w_vg[:],
                                                   start=True, stop=True)
                        ins.then_inc(vg_ready, 1)

                def scores(g, u, first=False):
                    k = TG * g + u
                    if u == 0:
                        pe.wait_ge(k_copied, g + 1)
                    pe.wait_ge(qm_made, k + 1)
                    for a, (taken, ready) in enumerate(((sa_done, sa_ready), (sb_copied, sb_ready))):
                        if not (first and u == 0):
                            pe.wait_ge(taken, k)
                        nc.tensor.matmul(bank[5 + a][0:T2, 0:GT], k_t[:, u * T2:(u + 1) * T2], q_heads[u % 2][:, 4 * a:4 * a + 4, :],
                                         start=True, stop=True).then_inc(ready, 1)

                def values(g, u, first=False):
                    k = TG * g + u
                    pe.wait_ge(sa_done, k + 1)
                    pe.wait_ge(sb_done, k + 1)
                    if u == 0:
                        pe.wait_ge(vg_copied, 2 * g + 2)
                        if not first:
                            pe.wait_ge(ret_copied, g)
                    for h in range(RH):
                        ins = nc.tensor.matmul(bank[7][0:T2, u * D + h * RD:u * D + (h + 1) * RD], sc[u % 2][:, h, :],
                                               v_sb[:, u, h * RD:(h + 1) * RD], start=True, stop=True)
                    ins.then_inc(pv_ready, 1)

                def retention(g, first=False, last=False):
                    scores(g, 0, first)
                    scores(g, 1)
                    values(g, 0, first)
                    scores(g, 2)
                    values(g, 1)
                    scores(g, 3)
                    values(g, 2)
                    if not last:
                        turn_ln(g + 1)
                    values(g, 3)
                    if not last:
                        queries_keys(g + 1)
                        values_gate(g + 1)

                turn_ln(0)
                queries_keys(0, first=True)
                values_gate(0)
                retention(0, first=True)
                with pe.Fori(1, NG - 1) as g:
                    retention(g)
                retention(NG - 1, last=True)

                def turn_z(g, p, first=False):
                    pe.wait_ge(zs_ready, g + 1)
                    if not first:
                        pe.wait_ge(zt_copied, g)
                    for u in range(TG):
                        ins = nc.tensor.transpose(bank[0][:, u * T2:(u + 1) * T2], z[p][:, u, :], ident[0:T2, 0:T2])
                    ins.then_inc(zt_ready, 1)

                def out_projection(g, p, first=False):
                    pe.wait_ge(zt_copied, g + 1)
                    if not first:
                        pe.wait_ge(h2_done, g - 1)
                    for u in range(TG):
                        ins = nc.tensor.matmul(bank[1 + 2 * p][0:T2, u * D:(u + 1) * D], z_t[p][:, u * T2:(u + 1) * T2], w_o[:], start=True, stop=True)
                    ins.then_inc(wo_ready, 1)

                turn_z(0, 0, first=True)
                turn_z(1, 1)
                out_projection(0, 0, first=True)
                turn_z(2, 0)
                out_projection(1, 1, first=True)
                with pe.Fori(1, NG // 2 - 1) as j:
                    for p in range(2):
                        turn_z(2 * j + p + 1, 1 - p)
                        out_projection(2 * j + p, p)
                turn_z(NG - 1, 1)
                out_projection(NG - 2, 0)
                out_projection(NG - 1, 1)

                def turn_hn(g, p, first=False):
                    pe.wait_ge(hn_ready, g + 1)
                    if not first:
                        pe.wait_ge(hnt_copied, g - 1)
                    for u in range(TG):
                        ins = nc.tensor.transpose(bank[2 * p][:, u * T2:(u + 1) * T2], hn[p][:, u, :], ident[0:T2, 0:T2])
                    ins.then_inc(hnt_ready, 1)

                def gate(g, p, first=False):
                    pe.wait_ge(hng_copied, g + 1)
                    if first:
                        pe.wait_ge(h2_done, NG)
                    else:
                        pe.wait_ge(lg_done, g - 1)
                    for u in range(TG):
                        ins = nc.tensor.matmul(bank[1 + 2 * p][0:T2, u * E:(u + 1) * E], hn_g[p][:, u * T2:(u + 1) * T2], gate_w[:], start=True, stop=True)
                    ins.then_inc(lg_ready, 1)

                turn_hn(0, 0, first=True)
                turn_hn(1, 1, first=True)
                gate(0, 0, first=True)
                turn_hn(2, 0)
                gate(1, 1, first=True)
                with pe.Fori(1, NG // 2 - 1) as j:
                    for p in range(2):
                        turn_hn(2 * j + p + 1, 1 - p)
                        gate(2 * j + p, p)
                turn_hn(NG - 1, 1)
                gate(NG - 2, 0)
                gate(NG - 1, 1)

                pe.wait_ge(pr_ready, 2)
                for j in range(TG):
                    ins = nc.tensor.transpose(bank[4][:, j * T2:(j + 1) * T2],
                                              prob_j[:, j, :], ident[0:T2, 0:T2])
                ins.then_inc(xp_ready, 1)

                def shared(g, p, first=False, last=False):
                    def total(q):
                        pe.wait_ge(cnt_ready, 2 * g + q + 1)
                        nc.tensor.matmul(bank[6][:, 0:3], same_expert[:], cnt[:], start=True, stop=True).then_inc(tot_ready, 1)

                    for c in range(HC):
                        if not first:
                            pe.wait_ge(sh_gelu, HC * (g - 1) + c + 1)
                        nc.tensor.matmul(bank[c][:, 0:GT], sw1[:, c * 128:(c + 1) * 128], hn_t[:, ds(GT * g, GT)], start=True, stop=True).then_inc(sh_ready, 1)
                    total(0)
                    pe.wait_ge(sh_gelu, HC * g + HC)
                    if not first:
                        pe.wait_ge(shy_taken, g)
                    for u in range(TG):
                        for c in range(HC):
                            ins = nc.tensor.matmul(bank[5 + 2 * p][0:T2, u * D:(u + 1) * D], hid[p][:, c, u * T2:(u + 1) * T2], sw2[:, c, :],
                                                   start=(c == 0), stop=(c == HC - 1))
                        if u == TG - 2 and not last:
                            total(1)
                    ins.then_inc(shy_ready, 1)

                pe.wait_ge(xp_ready, 1)
                shared(0, 0, first=True)
                shared(1, 1)
                with pe.Fori(1, NG // 2 - 1) as j:
                    for p in range(2):
                        shared(2 * j + p, p)
                shared(NG - 2, 0)
                shared(NG - 1, 1, last=True)

                pe.wait_ge(col_ready, 1)
                nc.tensor.matmul(bank[6][:, 8:9], same_expert[:], col[:, 0:1], start=True, stop=True)
                nc.tensor.matmul(bank[6][:, 16:17], before[:], col[:, 1:2], start=True, stop=True).then_inc(off_ready, 1)
                pe.wait_ge(col_ready, 2)
                nc.tensor.matmul(bank[6][:, 24:25], before[:], col[:, 3:4], start=True, stop=True).then_inc(off_ready, 1)
                pe.wait_ge(slot_ready, 1)
                for j in range(TG):
                    ins = nc.tensor.transpose(bank[4][0:T2, j * 128:(j + 1) * 128], scan_e[:, j * T2:(j + 1) * T2], ident[:])
                ins.then_inc(slot_taken, 1)
                pe.wait_ge(sh_gelu, HC * NG)
                for j in range(TG):
                    pe.wait_ge(made_b, j + 1)
                    for k, hot in enumerate((hot_ap, hot_at)):
                        if k == 0:
                            pe.wait_ge(place_ready, j + 1)
                        else:
                            pe.wait_ge((tile_even, tile_odd)[j % 2], j // 2 + 1)
                        for g in range(2):
                            for c in range(EC):
                                ins = nc.tensor.matmul(bank[2 * g + k][0:EG * SA, 0:128],
                                                       hot[:, j, c, g * EG:(g + 1) * EG, :].rearrange("p e a -> p (e a)"),
                                                       hot_b[:, j, c, g * EG:(g + 1) * EG, :].rearrange("p e b -> p (e b)"),
                                                       start=(j == 0 and c == 0), stop=(j == TG - 1 and c == EC - 1))
                ins.then_inc(list_ready, 1)
                pe.wait_ge(list_in, 32)
                nc.tensor.transpose(bank[6][0:TH, 0:2 * E], list_r[:], ident[0:2 * E, 0:2 * E]).then_inc(lr_ready, 1)

                def turn_tok(e, p):
                    pe.wait_ge(tok_in[p], 32 * (e // RING + 1) if isinstance(e, int) else (32 // RING) * (e - p) + 32)
                    for s in range(2):
                        ins = nc.tensor.transpose(bank[0][:, s * TH:(s + 1) * TH], tok[p][s][:, 0:D], ident[0:TH, 0:TH])
                    ins.then_inc(tt_ready, 1)

                def hidden(e, p, first=False):
                    pe.wait_ge(ew_in[p], 64 * (e // RING + 1) if isinstance(e, int) else 16 * (e - p) + 64)
                    pe.wait_ge(tt_copied, e + 1)
                    for c in range(HC):
                        if not first and c % 2 == 0:
                            pe.wait_ge(eh_gelu, HC * (e - 1) + c + 2)
                        ins = nc.tensor.matmul(bank[1 + c // 2][:, (c % 2) * CAP:(c % 2 + 1) * CAP], w1[p][:, c * 128:(c + 1) * 128], tok_t[p % 2][:],
                                               start=True, stop=True)
                        if c % 2:
                            ins.then_inc(eh_ready, 1)

                def output(e, p, first=False):
                    pe.wait_ge(eh_gelu, HC * e + HC)
                    if not first:
                        pe.wait_ge(ey_taken, 2 * e)
                    for s in range(2):
                        for c in range(HC):
                            ins = nc.tensor.matmul(bank[3][0:TH, s * D:(s + 1) * D], ehid[p % 2][:, c, s * TH:(s + 1) * TH], w2[p][:, c, :],
                                                   start=(c == 0), stop=(c == HC - 1))
                    ins.then_inc(ey_ready, 1)

                turn_tok(0, 0)
                hidden(0, 0, first=True)
                turn_tok(1, 1)
                hidden(1, 1)
                turn_tok(2, 2)
                output(0, 0, first=True)
                hidden(2, 2)
                turn_tok(3, 3)
                output(1, 1)
                with pe.Fori(1, E // RING) as j:
                    for p in range(RING):
                        e = RING * j + p
                        hidden(e - 1, (p - 1) % RING)
                        output(e - 2, (p - 2) % RING)
                        turn_tok(e, p)
                hidden(E - 1, RING - 1)
                output(E - 2, RING - 2)
                output(E - 1, RING - 1)


WTS2 = 19 * 16
AUG_STEPS = 16
DIAG_STEPS = 18
SETUP_STEPS = 27


def chunk_cols(t):
    return sum(chunk_rows(c) for c in range(2 * t, min(2 * t + 2, CH)))


def constants():
    f = np.float32
    t = np.arange(T2)
    diff = (t[None, :] - t[:, None]).astype(f)
    causal = (diff >= 0) & (t[None, :] // NQ == t[:, None] // NQ)
    gammas = 1.0 - np.exp2(-5.0 - np.arange(RH, dtype=f))
    decay = np.where(causal[:, None], np.exp(diff[:, None] * np.log(gammas)[None, :, None]), 0.0) / np.sqrt(f(RD))
    r = np.arange(128)
    same = r[:, None] // EC == r[None, :] // EC
    return {
        "decay": decay.astype(f),
        "head_mask": (np.arange(D)[:, None] // RD == np.arange(RH)[None, :]).astype(f),
        "same_expert": same.astype(f),
        "before": (same & (r[:, None] < r[None, :])).astype(f),
        "iota_slot": np.tile(np.arange(SB_, dtype=f), (T2, 1)),
        "tok_col": np.arange(T2, dtype=f)[:, None],
        "tile_num": np.tile((TG * np.arange(EC)[None, :] + np.arange(TG)[:, None]).astype(f)[None], (T2, 1, 1)),
        "diag": np.repeat((np.arange(EG * SA)[:, None] // SA == np.arange(EG)[None, :]).astype(f)[:, :, None], SB_, 2),
    }


def kernel(**inputs):
    import concourse.bacc as _bacc
    from concourse import mybir as _mybir
    from concourse.bass_utils import run_bass_kernel_spmd as _run

    a = {k: np.asarray(v) for k, v in inputs.items()}
    kv = a["L0_tok_kv_w"].reshape(H, KD + VD, C)

    def per_head(name, lo, hi):
        return a["L0_tok_kv_" + name].reshape(H, KD + VD)[:, lo:hi]

    arrays = {
        "x": a["x"],
        "x_t": a["x"].reshape(B * N, C).T,
        "idx": a["L0_tok_bias_idxs"],
        "bias_cols": a["L0_tok_attention_biases"].T.reshape(2, HALF, H).transpose(1, 0, 2),
        "iota_off": np.arange(NOFF, dtype=np.float32).reshape(2, HALF).T,
        "ident": np.eye(128, dtype=np.float32),
        "q_w": a["L0_tok_q_w"].reshape(H, KD, C).transpose(1, 0, 2),
        "k_w": kv[:, :KD].transpose(1, 0, 2),
        "v_w": kv[:, KD:].transpose(2, 0, 1).reshape(C, DH),
        "proj": a["L0_tok_proj_w"].T.reshape(DH // 128, 128, D).transpose(1, 0, 2),
        "w_q": a["L0_attn_W_Q"], "w_k": a["L0_attn_W_K"], "w_o": a["L0_attn_W_O"],
        "w_vg": np.concatenate([a["L0_attn_W_V"], a["L0_attn_W_G"]], 1),
        "gn_w": a["L0_attn_gn_weight"], "gn_b": a["L0_attn_gn_bias"],
        "gate_w": a["L0_ffn_gate_w"], "sw1": a["L0_ffn_sw1"],
        "sw2": a["L0_ffn_sw2"].reshape(HC, 128, D).transpose(1, 0, 2),
        "sb1": a["L0_ffn_sb1"].reshape(HC, 128).T, "sb2": a["L0_ffn_sb2"],
        "w1": a["L0_ffn_w1"], "w2": a["L0_ffn_w2"].reshape(E, HC, 128, D).transpose(0, 2, 1, 3),
        "b1": a["L0_ffn_b1"].reshape(E, HC, 128).transpose(0, 2, 1), "b2": a["L0_ffn_b2"],
        **constants(),
        "par_qk": np.stack([np.concatenate([a["L0_tok_q_" + n].reshape(H, KD).T, per_head(n, 0, KD).T], 1) for n in "gbmv"], 1),
        "par_v": np.stack([np.concatenate([per_head(n, KD, KD + VD).reshape(-1), a["L0_tok_proj_" + n]]).reshape(-1, 128).T for n in "gbmv"], 1),
    }
    nc = _bacc.Bacc("TRN2", target_bir_lowering=False, num_devices=1)
    feed, d = {}, {}
    for name, v in arrays.items():
        v = np.ascontiguousarray(v)
        feed[f"in_{name}_dram"] = v
        d[name] = nc.dram_tensor(f"in_{name}_dram", v.shape, _mybir.dt.from_np(v.dtype), kind="ExternalInput").ap()
    out = nc.dram_tensor("out_dram", (T, D), F32, kind="ExternalOutput").ap()
    build(nc, d, out)
    r = _run(nc, [feed], core_ids=[0])
    return r.results[0]["out_dram"].reshape(B, NQ, D)
```
